# Optimizing a Trainium2 kernel written in Bass

```python
import numpy as np
import jax
import jax.numpy as jnp

def _softmax(x, axis=-1):
    return jax.nn.softmax(x, axis=axis)

def _gelu(x):
    return jax.nn.gelu(x, approximate=True)

def _silu(x):
    return jax.nn.silu(x)

def _sigmoid(x):
    return jax.nn.sigmoid(x)

def _layernorm(x, axis=-1, eps=1e-05):
    m = jnp.mean(x, axis=axis, keepdims=True)
    v = jnp.var(x, axis=axis, keepdims=True)
    return (x - m) / jnp.sqrt(v + eps)

def _scatter_add(tgt, idx, src, axis=0):
    return tgt.at[idx].add(src)

def _segment_sum(src, seg, n):
    return jax.ops.segment_sum(src, seg, n)
kernel_name = 'mk_gnn_resnorm_d2_gnn_r64_b82a0f'

def setup_inputs(seed: int=0):
    np.random.seed(seed)
    _w = jnp.asarray

    def _rec_inputs():
        import jax
        import jax.numpy as jnp
        _gk = jax.random.key(seed)
        x = -0.000202 + 1 * jax.random.normal(jax.random.fold_in(_gk, 1), (100000, 64), jnp.float32)
        src = jax.random.randint(jax.random.fold_in(_gk, 2), (25000,), 0, 100000, jnp.int32)
        dst = jax.random.randint(jax.random.fold_in(_gk, 3), (25000,), 0, 100000, jnp.int32)
        _o = jnp.argsort(dst, stable=True)
        src = src[_o]
        dst = dst[_o]
        edge_type_50 = jax.random.randint(jax.random.fold_in(_gk, 13), (25000,), 0, 50, jnp.int32)
        return (x, src, dst, edge_type_50)
    x, src, dst, edge_type_50 = _rec_inputs()

    def _L0_gnn_setup():
        import jax, jax.numpy as jnp
        import numpy as np
        N_NODES = 100000
        N_EDGES = 25000
        D = 64
        BN_EPS = 1e-05
        key = jax.random.key(seed)
        ks = jax.random.split(key, 6)
        h = jax.random.normal(ks[0], (N_NODES, D), dtype=jnp.float32)
        src = jax.random.randint(ks[1], (N_EDGES,), 0, N_NODES)
        dst = jax.random.randint(ks[2], (N_EDGES,), 0, N_NODES)
        W1 = jax.random.normal(ks[3], (D, D), dtype=jnp.float32) * (1.0 / np.sqrt(D))
        b1 = jnp.zeros((D,), dtype=jnp.float32)
        W2 = jax.random.normal(ks[4], (D, D), dtype=jnp.float32) * (1.0 / np.sqrt(D))
        b2 = jnp.zeros((D,), dtype=jnp.float32)
        gamma = jnp.ones((D,), dtype=jnp.float32)
        beta = jnp.zeros((D,), dtype=jnp.float32)
        eps = jnp.zeros((1,), dtype=jnp.float32)
        return {'h': h, 'src': src, 'dst': dst, 'W1': W1, 'b1': b1, 'W2': W2, 'b2': b2, 'gamma': gamma, 'beta': beta, 'eps': eps}
    _L0_gnn_all = _L0_gnn_setup()
    _L0_gnn_in = {k: v for k, v in _L0_gnn_all.items() if k in ('W1', 'b1', 'W2', 'b2', 'gamma', 'beta', 'eps')}
    del _L0_gnn_all

    def _L1_gnn_setup():
        import jax, jax.numpy as jnp
        import numpy as np
        N, H, OUT, R, E, B = (50000, 64, 64, 50, 12500, 4)

        def _glorot(k, shape):
            fan_in, fan_out = (shape[-2], shape[-1])
            s = (6.0 / (fan_in + fan_out)) ** 0.5
            return jax.random.uniform(k, shape, jnp.float32, -s, s)

        def _rgcn_layer(x, src, dst, etype, w_rel, w_root, bias):
            n, d = x.shape
            seg = dst * R + etype
            msgs = x[src]
            s = jax.ops.segment_sum(msgs, seg, num_segments=n * R).reshape(n, R, d)
            cnt = jax.ops.segment_sum(jnp.ones((msgs.shape[0],), x.dtype), seg, num_segments=n * R).reshape(n, R, 1)
            s = s / jnp.maximum(cnt, 1.0)
            if w_rel.ndim == 4:
                nb, db, do = (w_rel.shape[1], w_rel.shape[2], w_rel.shape[3])
                agg = jnp.einsum('nrbd,rbde->nbe', s.reshape(n, R, nb, db), w_rel)
                agg = agg.reshape(n, nb * do)
            else:
                agg = jnp.einsum('nrd,rde->ne', s, w_rel)
            return agg + x @ w_root + bias
        key = jax.random.key(seed)
        ks = jax.random.split(key, 12)
        db = H // B
        inp = {'x': jax.random.normal(ks[0], (N, H), jnp.float32), 'edge_index': jax.random.randint(ks[1], (2, E), 0, N), 'edge_type': jax.random.randint(ks[2], (E,), 0, R), 'w0_rel': _glorot(ks[3], (R, B, db, db)), 'w0_root': _glorot(ks[4], (H, H)), 'b0': jnp.zeros((H,), jnp.float32), 'w1_rel': _glorot(ks[5], (R, B, db, db)), 'w1_root': _glorot(ks[6], (H, H)), 'b1': jnp.zeros((H,), jnp.float32), 'w2_rel': _glorot(ks[7], (R, H, OUT)), 'w2_root': _glorot(ks[8], (H, OUT)), 'b2': jnp.zeros((OUT,), jnp.float32)}
        return inp
    _L1_gnn_all = _L1_gnn_setup()
    _L1_gnn_in = {k: v for k, v in _L1_gnn_all.items() if k in ('w0_rel', 'w0_root', 'b0', 'w1_rel', 'w1_root', 'b1', 'w2_rel', 'w2_root', 'b2')}
    del _L1_gnn_all
    return {'x': x, 'src': src, 'dst': dst, 'edge_type_50': edge_type_50, 'L0_gnn_W1': _L0_gnn_in['W1'], 'L0_gnn_b1': _L0_gnn_in['b1'], 'L0_gnn_W2': _L0_gnn_in['W2'], 'L0_gnn_b2': _L0_gnn_in['b2'], 'L0_gnn_gamma': _L0_gnn_in['gamma'], 'L0_gnn_beta': _L0_gnn_in['beta'], 'L0_gnn_eps': _L0_gnn_in['eps'], 'L1_gnn_w0_rel': _L1_gnn_in['w0_rel'], 'L1_gnn_w0_root': _L1_gnn_in['w0_root'], 'L1_gnn_b0': _L1_gnn_in['b0'], 'L1_gnn_w1_rel': _L1_gnn_in['w1_rel'], 'L1_gnn_w1_root': _L1_gnn_in['w1_root'], 'L1_gnn_b1': _L1_gnn_in['b1'], 'L1_gnn_w2_rel': _L1_gnn_in['w2_rel'], 'L1_gnn_w2_root': _L1_gnn_in['w2_root'], 'L1_gnn_b2': _L1_gnn_in['b2']}

def reference(x, src, dst, edge_type_50, L0_gnn_W1, L0_gnn_b1, L0_gnn_W2, L0_gnn_b2, L0_gnn_gamma, L0_gnn_beta, L0_gnn_eps, L1_gnn_w0_rel, L1_gnn_w0_root, L1_gnn_b0, L1_gnn_w1_rel, L1_gnn_w1_root, L1_gnn_b1, L1_gnn_w2_rel, L1_gnn_w2_root, L1_gnn_b2):
    import jax
    import jax.numpy as jnp

    def _L0_gnn_ref(h, src, dst, W1, b1, W2, b2, gamma, beta, eps):
        import jax, jax.numpy as jnp
        import numpy as np
        N_NODES = 100000
        N_EDGES = 25000
        D = 64
        BN_EPS = 1e-05
        h_in = h
        neigh = jax.ops.segment_sum(h[src], dst, num_segments=N_NODES)
        x = (1.0 + eps[0]) * h + neigh
        x = jax.nn.relu(x @ W1 + b1) @ W2 + b2
        mu = jnp.mean(x, axis=0)
        var = jnp.mean((x - mu) ** 2, axis=0)
        x = (x - mu) * jax.lax.rsqrt(var + BN_EPS) * gamma + beta
        x = jax.nn.relu(x)
        return h_in + x

    def _L1_gnn_ref(x, edge_index, edge_type, w0_rel, w0_root, b0, w1_rel, w1_root, b1, w2_rel, w2_root, b2):
        import jax, jax.numpy as jnp
        import numpy as np
        N, H, OUT, R, E, B = (50000, 64, 64, 50, 12500, 4)

        def _glorot(k, shape):
            fan_in, fan_out = (shape[-2], shape[-1])
            s = (6.0 / (fan_in + fan_out)) ** 0.5
            return jax.random.uniform(k, shape, jnp.float32, -s, s)

        def _rgcn_layer(x, src, dst, etype, w_rel, w_root, bias):
            n, d = x.shape
            seg = dst * R + etype
            msgs = x[src]
            s = jax.ops.segment_sum(msgs, seg, num_segments=n * R).reshape(n, R, d)
            cnt = jax.ops.segment_sum(jnp.ones((msgs.shape[0],), x.dtype), seg, num_segments=n * R).reshape(n, R, 1)
            s = s / jnp.maximum(cnt, 1.0)
            if w_rel.ndim == 4:
                nb, db, do = (w_rel.shape[1], w_rel.shape[2], w_rel.shape[3])
                agg = jnp.einsum('nrbd,rbde->nbe', s.reshape(n, R, nb, db), w_rel)
                agg = agg.reshape(n, nb * do)
            else:
                agg = jnp.einsum('nrd,rde->ne', s, w_rel)
            return agg + x @ w_root + bias
        src, dst = (edge_index[0], edge_index[1])
        h = jax.nn.relu(_rgcn_layer(x, src, dst, edge_type, w0_rel, w0_root, b0))
        h = jax.nn.relu(_rgcn_layer(h, src, dst, edge_type, w1_rel, w1_root, b1))
        return _rgcn_layer(h, src, dst, edge_type, w2_rel, w2_root, b2)
    edge_index = jnp.stack([src, dst])
    x = _layernorm(x + _L0_gnn_ref(x, src, dst, L0_gnn_W1, L0_gnn_b1, L0_gnn_W2, L0_gnn_b2, L0_gnn_gamma, L0_gnn_beta, L0_gnn_eps), axis=-1)
    x = _layernorm(x + _L1_gnn_ref(x, edge_index, edge_type_50, L1_gnn_w0_rel, L1_gnn_w0_root, L1_gnn_b0, L1_gnn_w1_rel, L1_gnn_w1_root, L1_gnn_b1, L1_gnn_w2_rel, L1_gnn_w2_root, L1_gnn_b2), axis=-1)
    return x

_drawn_inputs = setup_inputs


def setup_inputs(seed=0):
    import zlib

    import numpy as np

    out = dict(_drawn_inputs(seed))
    spreads = {'L0_gnn_b1': (0.0, 0.304),
     'L0_gnn_b2': (0.0, 0.8),
     'L0_gnn_gamma': (1.0, 0.2),
     'L0_gnn_beta': (0.0, 0.1),
     'L1_gnn_b0': (0.0, 0.1),
     'L1_gnn_b1': (0.0, 0.1),
     'L1_gnn_b2': (0.0, 0.1)}
    factors = {}
    for name, (base, spread) in spreads.items():
        noise = np.random.default_rng([zlib.crc32(name.encode()), seed]).standard_normal(out[name].shape)
        drawn = base * np.exp(spread * noise) if base else spread * noise
        out[name] = jnp.asarray(drawn.astype(out[name].dtype))
    for name, factor in factors.items():
        out[name] = (out[name] * factor).astype(out[name].dtype)
    return out
```

```python
import numpy as np
import concourse.bass as bass
from concourse import mybir
from contextlib import ExitStack

F32 = mybir.dt.float32
BF16 = mybir.dt.bfloat16
I32 = mybir.dt.int32
ALU = mybir.AluOpType
ACT = mybir.ActivationFunctionType
AX = mybir.AxisListType

N, E, D, R = 100000, 25000, 64, 50
L = 3
P = 128
T = 8
TE = -(-E // (P * T)) * T
EP = P * TE
PE_FULL = E // TE
GE = TE // T
TS = -(-(E // P + R) // T) * T
NS = P * TS
GS = TS // T
ROWS = P * T
GD_FULL = N // ROWS
REST = (N - GD_FULL * ROWS) // T
GD = GD_FULL + 1
U = 4
W = T * D
REC = 4
WD = D + REC
BIG = 1 << 23
BINS = 10
HALF = TS // 2
EPS = 1e-5

assert PE_FULL * TE == E and REST * T + GD_FULL * ROWS == N and HALF <= P


def iters(n, u):
    return -(-n // u)


def per_buffer(n, u, k):
    return (n - k + u - 1) // u


class Signals:

    def __init__(self, make, plan):
        self.sem, self.base = {}, {}
        for name, uses in plan.items():
            self.sem[name] = make(name)
            done = 0
            for stage, count in uses:
                self.base[name, stage] = done
                done += count

    def at(self, name, stage, count):
        return self.base[name, stage] + count


def rounds(eng, n, u, body, last=P):
    full, rest = divmod(n, u)
    with eng.Fori(0, full) as i:
        body(i, [(k, P) for k in range(u)])
    if rest:
        body(full, [(k, P if k < rest - 1 else last) for k in range(rest)])


def build(nc, x, src, dst, etype, W1, b1, W2, b2, gamma, beta, eps, w0_rel, w0_root, b0, w1_rel,
          w1_root, c1, w2_rel, w2_root, c2, out):
    ctx = ExitStack()
    with ctx:
        def sb(name, shape, dt=F32):
            return ctx.enter_context(nc.sbuf_tensor(name, shape, dt))

        def dram(name, shape, dt=F32):
            return nc.dram_tensor(name, shape, dt, kind="Internal").ap()

        def sem(name):
            return ctx.enter_context(nc.semaphore(name))

        src_x = dram("src_x", (EP, D))
        dst_x = dram("dst_x", (EP, D))
        dst_rows = [dram(f"dst_rows{l}", (EP, D)) for l in range(L)]
        src_x1 = dram("src_x1", (EP, D))
        slot_rows = [dram("slot_rows0", (NS, WD))] + [dram(f"slot_rows{l}", (NS, D)) for l in (1, 2)]
        msg_rows = dram("msg_rows", (EP, D))
        node_table = dram("node_table", (N, 1))
        key_line = dram("key_line", (NS + 1,))

        agg = sb("agg", [P, TE * D])
        aggv = agg[:, :].rearrange("p (t d) -> p t d", d=D)
        rel_w = sb("rel_w", [D, L * R * D])
        ident = sb("ident", [P, P])
        before = sb("before", [P, P])
        ones = sb("ones", [P, P])
        pick3 = sb("pick3", [P, P], BF16)
        fold = sb("fold", [P, D])
        bins = sb("bins", [P, R])
        tile_no = sb("tile_no", [HALF, 2])
        slot_no = sb("slot_no", [HALF, 2 * P])
        edge1 = sb("edge1", [P, TE])
        zeros = sb("zeros", [P, N // PE_FULL])
        const = sb("const", [P, 2])
        eps1 = sb("eps1", [P, 1])

        w1 = sb("w1", [P, P])
        w2 = sb("w2", [P, P])
        w2n = sb("w2n", [P, P])
        root = [sb(f"root{l}", [P, P]) for l in range(L)]
        b1c = sb("b1c", [P, 1])
        rootb = [sb(f"rootb{l}", [P, 1]) for l in range(L)]
        row_v = sb("row_v", [P, 6, D])
        bias3 = [sb(f"bias3_{k}", [P, W], BF16) for k in range(L + 1)]
        split = sb("split", [P, 3, D])
        split_b = sb("split_b", [P, 3, D], BF16)

        srci = sb("srci", [P, TE], I32)
        dsti = sb("dsti", [P, TE], I32)
        reli = sb("reli", [P, TE], I32)
        dprev = sb("dprev", [P, TE], I32)
        dnext = sb("dnext", [P, TE], I32)
        dclamp = sb("dclamp", [P, TE], I32)
        last_i = sb("last_i", [P, TE], I32)
        addr_i = sb("addr_i", [P, TE], I32)
        relf = sb("relf", [P, TE])
        keep = sb("keep", [P, TE])
        last = sb("last", [P, TE])
        openk = sb("openk", [P, TE])
        slotf = sb("slotf", [P, TE])
        tmpf = sb("tmpf", [P, TE])
        lo_i = sb("lo_i", [P, TE], I32)
        hi_i = sb("hi_i", [P, TE], I32)
        rec = sb("rec", [P, TE, REC])
        endv = sb("endv", [P, R])
        tot = sb("tot", [P, R])
        excl = sb("excl", [P, R])
        cross = sb("cross", [P, R])
        cnt_i = sb("cnt_i", [P, R], I32)
        tiles = sb("tiles", [P, R])
        tend = sb("tend", [P, R])
        off = sb("off", [P, R])
        relge = sb("relge", [HALF, R])
        relt = sb("relt", [HALF, 2])
        rel_tab = sb("rel_tab", [1, TS], I32)
        ak = sb("ak", [P, D])
        akT = sb("akT", [D, P])
        endT = sb("endT", [D, P])
        carT = sb("carT", [D, P + 1])
        carry = sb("carry", [P, D])

        xr = [sb(f"xr{u}", [P, W]) for u in range(U)]
        xT = [sb(f"xT{u}", [P, W]) for u in range(U)]
        aT = [sb(f"aT{u}", [P, W]) for u in range(U)]
        vr = [sb(f"vr{u}", [P, W]) for u in range(U)]
        orow = [sb(f"orow{u}", [P, W]) for u in range(U)]
        ybn = sb("ybn", [P, GD * 6])
        mom = sb("mom", [P, 2, D])
        sums = sb("sums", [P, 12])
        st = sb("st", [P, U * T, 6])
        lns = sb("lns", [P, 6, U * T])
        lnb = sb("lnb", [P, U * T])
        st2 = sb("st2", [P, U * T, 6])
        lns2 = sb("lns2", [P, 6, U * T])
        lnb2 = sb("lnb2", [P, U * T])
        moment_rhs = sb("moment_rhs", [P, 4, D])
        st_rhs = [moment_rhs[:, k, :] for k in range(2)]
        corr_rhs = [moment_rhs[:, 2 + k, :] for k in range(2)]
        primer = sb("primer", [1, 32])
        runc = sb("runc", [HALF, 4])
        ring_s = [sb(f"ring_s{h}", [P, W]) for h in range(2)]
        ring_d = [sb(f"ring_d{h}", [P, W]) for h in range(2)]
        wide = [sb(f"wide{h}", [P, T, WD]) for h in range(2)]
        idx_a = [sb(f"idx_a{h}", [P, T], I32) for h in range(U)]
        idx_b = [sb(f"idx_b{h}", [P, T], I32) for h in range(2)]
        val = [sb(f"val{h}", [P, T]) for h in range(U)]
        inv = sb("inv", [P, TS])
        slot_rec = sb("slot_rec", [P, TS, 3])
        qidx = sb("qidx", [P, TS], I32)
        lidx = sb("lidx", [P, TS], I32)

        bank = [ctx.enter_context(nc.psum_tensor(f"bank{k}", [P, 512], F32)) for k in range(8)]

        cum = agg[:, 0:R * TE]
        hot = agg[:, R * TE:R * TE + BINS * TE]
        keyT = agg[0:HALF, 0:2 * P]
        keyP = agg[0:HALF, 2 * P:4 * P]
        runS = agg[0:HALF, 4 * P:6 * P]
        runF = agg[0:HALF, 6 * P:8 * P]
        runE = agg[0:HALF, 8 * P:10 * P]
        runX = agg[0:HALF, 10 * P:12 * P]
        line = agg[0:1, 12 * P:12 * P + 4 * (TS + 1)].rearrange("p (k t) -> p k t", k=4)
        rec_in = agg[:, 0:HALF * WD]
        acc = [vr[2], vr[3]]
        srow = [wide[h][:, :, :] for h in range(2)]
        sT = [aT[0], aT[1], aT[2], aT[3]]

        def edge_rows(a, g, n=1):
            return a.rearrange("(p t) d -> p (t d)", p=P)[:, bass.ds(g * W, W)]

        def node_rows(a, g, p):
            if p != P:
                return a[GD_FULL * ROWS:N, :].rearrange("(p j) d -> p (j d)", j=T)
            return a[0:GD_FULL * ROWS, :].rearrange("(g p j) d -> g p (j d)", p=P, j=T)[bass.ds(g, 1)] \
                .rearrange("o p w -> (o p) w")

        def slot_view(l, g):
            w = WD if l == 0 else D
            return slot_rows[l].rearrange("(p t) w -> p t w", p=P)[:, bass.ds(g * T, T), :]

        per_group = {
            "x_turned": ["stats", "x1d", "x1s", "dense", "d0", "d1", "d2"],
            "x_copied": ["stats", "x1d", "x1s", "dense", "d0", "d1", "d2"],
            "hid_ready": ["stats", "x1d", "x1s", "dense"],
            "hid_relu": ["stats", "x1d", "x1s", "dense"],
            "y_ready": ["stats", "x1d", "x1s", "dense", "d0", "d1", "d2"],
            "y_counted": ["stats"],
            "x0_ready": ["x1d"],
            "v_ready": ["x1d", "x1s", "dense", "d0", "d1", "d2"],
            "v_final": ["d2"],
            "v_stats": ["x1d", "x1s", "dense", "d2"],
            "x1_ready": ["x1d", "x1s", "dense", "d0", "d1", "d2"],
            "x1_turned": ["dense"], "x1_copied": ["dense"], "r0_ready": ["dense"], "r0_relu": ["dense"],
            "r1_ready": ["dense"], "r1_relu": ["dense"], "r2_ready": ["dense"],
            "v2_ready": ["dense"], "v2_stats": ["dense"], "out_ready": ["dense"],
        }
        size = dict(stats=GD, x1d=GE, x1s=GE, dense=GD, d0=GE, d1=GE, d2=GE)
        plan = {k: [(s, size[s]) for s in v] for k, v in per_group.items()}
        ln_stages = ["x1d", "x1s", "dense", "d2"]
        plan["ln_step"] = [(s, 4 * iters(size[s], U)) for s in ln_stages]
        plan["var_ready"] = [(s, iters(size[s], U)) for s in ln_stages]
        plan["std_ready"] = [(s, iters(size[s], U)) for s in ln_stages]
        plan["ln2_step"] = [("dense", 4 * iters(GD, U))]
        plan["var2_ready"] = [("dense", iters(GD, U))]
        plan["std2_ready"] = [("dense", iters(GD, U))]
        for u in range(U):
            plan[f"loaded{u}"] = [(s, 16 * per_buffer(size[s], U, u)) for s in per_group["x_turned"]]
            plan[f"stored{u}"] = [(s, 16 * per_buffer(size[s], U, u)) for s in ("x1d", "x1s", "dense", "d0", "d1")]
            plan[f"x1_loaded{u}"] = [("d2", 16 * per_buffer(GE, U, u))]
            plan[f"scattered{u}"] = [("d2", 16 * T * per_buffer(GE, U, u))]
        SL = [f"s{l}" for l in range(L)]
        for k in ("s_turned", "s_copied_a", "s_copied_b", "msg_sums", "msg_ready"):
            plan[k] = [(s, GS) for s in SL]
        for k in ("base_ready", "base_relu"):
            plan[k] = [(s, GS) for s in SL[:2]]
        for h in range(2):
            plan[f"slot_loaded{h}"] = [(s, 16 * per_buffer(GS, 2, h)) for s in SL]
            plan[f"fetched{h}"] = [(s, 16 * T * per_buffer(GS, 2, h)) for s in SL]
            plan[f"msg_out{h}"] = [(s, 16 * T * per_buffer(GS, 2, h)) for s in SL]
            plan[f"slot_stored{h}"] = [(s, 16 * per_buffer(GS, 2, h)) for s in SL[:2]]
        plan["slot_idx"] = [(s, GS) for s in SL]
        seg_uses = ["neigh"] + [f"m{l}" for l in range(L)]
        plan["agg_loaded"] = [(s, 16) for s in seg_uses]
        plan["scanned"] = [(s, D) for s in seg_uses]
        plan["carried"] = [(s, D) for s in seg_uses]
        plan["end_turned"] = [(s, 1) for s in seg_uses]
        plan["carry_step"] = [(s, 3) for s in seg_uses]
        plan["carry_turned"] = [(s, 1) for s in seg_uses]
        SG = Signals(sem, plan)
        S, at = SG.sem, SG.at

        s_fill = sem("filled")
        s_idx = sem("indices_loaded")
        s_wts = sem("weights_loaded")
        s_zero = sem("scratch_zeroed")
        s_dve = sem("vector_step")
        s_pe = sem("tensor_step")
        s_rows = [sem(f"rows_gathered{h}") for h in range(2)]
        s_rst = [sem(f"gathered_stored{h}") for h in range(2)]
        s_cp = sem("index_copied")
        s_pad = sem("pool_pad")
        s_pad_pe = sem("tensor_pad")
        s_tab = [sem(f"table_written{h}") for h in range(2)]
        s_look = [sem(f"table_read{h}") for h in range(U)]
        s_lc = sem("looked_up")
        s_wl = [sem(f"wide_loaded{h}") for h in range(2)]
        s_ws = [sem(f"wide_scattered{h}") for h in range(2)]
        s_e = {k: sem("edge_" + k) for k in ("loaded", "x0", "turned", "copied", "hid", "relu", "y", "base",
                                             "diff", "acc")}
        s_rin = sem("records_loaded")
        s_key = sem("keys_moved")
        s_std = sem("y_std")
        DV = {}
        WTS = 16 * 34

        GA = 2 * 16 * T

        block = ctx.enter_context(nc.Block())

        @block.vector
        def _(dve):
            steps = [0]

            def step(ins, name=None):
                steps[0] += 1
                ins.then_inc(s_dve, 1)
                dve.wait_ge(s_dve, steps[0])
                if name:
                    DV[name] = steps[0]

            tt, ts, stt, scan = dve.tensor_tensor, dve.tensor_scalar, dve.scalar_tensor_tensor, dve.tensor_tensor_scan
            dve.sem_inc(S["v_ready"], U)
            dve.sem_inc(S["v2_ready"], U)
            dve.sem_inc(S["v_final"], U)
            dve.sem_inc(S["y_counted"], U)
            dve.memset(const[:, 0:1], EPS / 4)
            dve.memset(const[:, 1:2], EPS)
            dve.memset(pick3[:, :], 0.0)
            for k in range(L + 1):
                ins = dve.memset(bias3[k][:, :], 0.0)
            step(ins, "consts")
            for k in range(3):
                ins = dve.memset(pick3[32 * k:32 * k + 1, :], 1.0)
            step(ins)

            dve.wait_ge(s_fill, 5)
            dve.wait_ge(s_idx, 16 * 7)
            ts(dclamp[:, :], dsti[:, :], float(N - 1), None, ALU.min)
            tt(keep[:, :], dsti[:, :], dprev[:, :], ALU.is_equal)
            tt(last[:, :], dsti[:, :], dnext[:, :], ALU.not_equal)
            dve.tensor_copy(relf[:, :], reli[:, :])
            step(dve.memset(rec[:, :, :], 0.0), "dst_clamped")
            scan(openk[:, :], keep[:, :], keep[:, :], 1.0, ALU.min, ALU.min)
            step(stt(tmpf[:, :], last[:, :], -float(BIG), dsti[:, :], ALU.mult, ALU.add))
            step(ts(last_i[:, :], tmpf[:, :], float(BIG), None, ALU.add))
            step(ts(tmpf[:, :], dsti[:, :], 1.0, float(R), ALU.add, ALU.mult))
            tt(rec[:, :, 2], tmpf[:, :], relf[:, :], ALU.add)
            dve.tensor_copy(rec[:, :, 0], edge1[:, :])
            step(dve.tensor_copy(ak[:, :], openk[:, TE - 1:TE].to_broadcast([P, D])))

            hotv = hot.rearrange("p (r t) -> p r t", t=TE)
            cumv = cum.rearrange("p (r t) -> p r t", t=TE)

            def mark(c):
                step(tt(hotv, relf[:, :].unsqueeze(1).to_broadcast([P, BINS, TE]),
                        bins[:, c * BINS:(c + 1) * BINS].unsqueeze(2).to_broadcast([P, BINS, TE]), ALU.is_equal))
            for c in range(R // BINS):
                mark(c)
                lo = c * BINS * TE
                step(scan(cum[:, lo:lo + BINS * TE], ones[:, 0:1].to_broadcast([P, BINS * TE]), hot,
                          0.0 if c == 0 else cum[:, lo - 1:lo], ALU.mult, ALU.add))
            dve.memset(excl[:, 0:1], 0.0)
            step(dve.tensor_copy(endv[:, :], cumv[:, :, TE - 1]))
            step(dve.tensor_copy(excl[:, 1:R], endv[:, 0:R - 1]))
            step(tt(tot[:, :], endv[:, :], excl[:, :], ALU.subtract), "counted")
            dve.wait_ge(s_pe, 1)
            ts(cnt_i[:, :], bank[0][:, R:2 * R], float(P - 1), None, ALU.add)
            step(dve.tensor_copy(cross[:, :], bank[0][:, 0:R]))
            step(ts(cnt_i[:, :], cnt_i[:, :], 7, None, ALU.logical_shift_right))
            step(dve.tensor_copy(tiles[:, :], cnt_i[:, :]))
            step(scan(tend[:, :], ones[:, 0:R], tiles[:, :], 0.0, ALU.mult, ALU.add))
            step(tt(off[:, :], tend[:, :], tiles[:, :], ALU.subtract))
            step(stt(off[:, :], off[:, :], float(P), cross[:, :], ALU.mult, ALU.add))
            step(stt(off[:, :], off[:, :], -1.0, excl[:, :], ALU.add, ALU.subtract))
            for h in range(2):
                step(ts(relge[:, :], tend[0:HALF, :], tile_no[:, h:h + 1], None, ALU.is_le))
                step(dve.tensor_reduce(relt[:, h:h + 1], relge[:, :], AX.X, ALU.add))
            step(ts(relt[:, :], relt[:, :], float(R - 1), None, ALU.min), "tile_rel")
            for c in range(R // BINS):
                mark(c)
                part = cumv[:, c * BINS:(c + 1) * BINS, :]
                step(tt(part, part, off[:, c * BINS:(c + 1) * BINS].unsqueeze(2).to_broadcast([P, BINS, TE]), ALU.add))
                step(tt(part, part, hotv, ALU.mult))
                step(dve.tensor_reduce((slotf if c == 0 else tmpf)[:, :], part.rearrange("p r t -> p t r"), AX.X, ALU.add))
                if c:
                    step(tt(slotf[:, :], slotf[:, :], tmpf[:, :], ALU.add))
            step(ts(tmpf[:, :], relf[:, :], float(R), float(BIG), ALU.is_ge, ALU.mult))
            step(tt(hi_i[:, :], slotf[:, :], tmpf[:, :], ALU.add))
            step(ts(lo_i[:, :], hi_i[:, :], P - 1, None, ALU.bitwise_and))
            step(ts(hi_i[:, :], hi_i[:, :], 7, None, ALU.logical_shift_right))
            step(stt(addr_i[:, :], lo_i[:, :], float(TS), hi_i[:, :], ALU.mult, ALU.add))
            dve.wait_ge(s_pe, 3)
            dve.tensor_copy(akT[:, :], bank[2][0:D, 0:P])
            dve.memset(carT[:, 0:1], 0.0)
            step(dve.tensor_copy(rel_tab[:, :], bank[1][0:1, 0:TS]), "sorted")

            def norm_bias(k, row):
                step(dve.tensor_copy(split_b[:, 0, :], row))
                step(tt(split[:, 0, :], row, split_b[:, 0, :], ALU.subtract))
                step(dve.tensor_copy(split_b[:, 1, :], split[:, 0, :]))
                step(tt(split[:, 1, :], split[:, 0, :], split_b[:, 1, :], ALU.subtract))
                step(dve.tensor_copy(split_b[:, 2, :], split[:, 1, :]))
                for r in range(3):
                    q = slice(32 * r, 32 * r + 1)
                    ins = dve.tensor_copy(bias3[k][q, :].rearrange("p (t d) -> p t d", d=D),
                                          split_b[q, r, :].unsqueeze(1).to_broadcast([1, T, D]))
                step(ins)
            dve.wait_ge(s_wts, WTS)
            for k in range(L):
                norm_bias(1 + k, row_v[:, 3 + k, :])
            step(ts(eps1[:, :], eps1[:, :], 1.0, None, ALU.add), "eps")

            def stats(i, us):
                for u, p in us:
                    dve.wait_ge(S["x_turned"], at("x_turned", "stats", U + i * U + u + 1))
                    dve.tensor_copy(xT[u][:, 0:4 * p], bank[2 * u][:, 0:4 * p]).then_inc(S["x_copied"], 1)
                for u, p in us:
                    dve.wait_ge(S["y_ready"], at("y_ready", "stats", i * U + u + 1))
                    dve.bn_stats(ybn[:, bass.ds((i * U + u) * 6, 6)], bank[2 * u][:, 0:4 * p]).then_inc(S["y_counted"], 1)
            rounds(dve, GD, U, stats, last=REST)
            dve.wait_ge(S["y_counted"], at("y_counted", "stats", GD + U))

            def segment_sum(use):
                dve.wait_ge(S["agg_loaded"], at("agg_loaded", use, 16))
                with dve.Fori(0, D // 4) as i:
                    for k in range(4):
                        col = aggv[:, :, bass.ds(i * 4 + k, 1)].rearrange("p t o -> p (t o)")
                        scan(col, keep[:, :], col, 0.0, ALU.mult, ALU.add).then_inc(S["scanned"], 1)
                dve.wait_ge(S["end_turned"], at("end_turned", use, 1))
                dve.tensor_copy(endT[:, :], bank[4][0:D, 0:P]).then_inc(S["carry_step"], 1)
                dve.wait_ge(S["carry_step"], at("carry_step", use, 1))
                scan(carT[:, 1:P + 1], akT[:, :], endT[:, :], 0.0, ALU.mult, ALU.add).then_inc(S["carry_step"], 1)
                dve.wait_ge(S["carry_turned"], at("carry_turned", use, 1))
                dve.tensor_copy(carry[:, :], bank[5][:, 0:D]).then_inc(S["carry_step"], 1)
                dve.wait_ge(S["carry_step"], at("carry_step", use, 3))
                dve.wait_ge(S["scanned"], at("scanned", use, D))
                with dve.Fori(0, D // 4) as i:
                    for k in range(4):
                        col = aggv[:, :, bass.ds(i * 4 + k, 1)].rearrange("p t o -> p (t o)")
                        stt(col, openk[:, :], carry[:, bass.ds(i * 4 + k, 1)], col, ALU.mult, ALU.add).then_inc(S["carried"], 1)
                dve.wait_ge(S["carried"], at("carried", use, D))
            segment_sum("neigh")

            def agg_group(g):
                return agg[:, bass.ds(g * W, W)]

            dve.memset(acc[0][:, :], 0.0)
            step(dve.memset(acc[1][:, :], 0.0))
            dve.sem_inc(s_e["acc"], 1)
            with dve.Fori(0, GE) as g:
                dve.wait_ge(s_e["loaded"], 16 * (g + 1))
                dve.wait_ge(s_e["turned"], g + 1)
                stt(xr[1][:, :], xr[0][:, :], eps1[:, 0:1], agg_group(g), ALU.mult, ALU.add).then_inc(s_e["x0"], 1)
                dve.wait_ge(s_e["turned"], g + 2)
                dve.tensor_copy(xT[0][:, :], bank[0][:, :])
                dve.tensor_copy(xT[1][:, :], bank[2][:, :]).then_inc(s_e["copied"], 1)
                dve.wait_ge(s_e["base"], g + 1)
                dve.wait_ge(s_e["acc"], 2 * g + 1)
                tt(orow[1][:, :], bank[2][:, :], orow[0][:, :], ALU.subtract)
                tt(orow[2][:, :], bank[2][:, :], orow[0][:, :], ALU.add).then_inc(s_e["diff"], 1)
                dve.wait_ge(s_e["diff"], 2 * g + 1)
                tt(orow[1][:, :].rearrange("p (t d) -> p t d", d=D), orow[1][:, :].rearrange("p (t d) -> p t d", d=D),
                   last[:, bass.ds(g * T, T)].unsqueeze(2).to_broadcast([P, T, D]), ALU.mult).then_inc(s_e["diff"], 1)
                dve.wait_ge(s_e["diff"], 2 * g + 2)
                tt(acc[0][:, :], acc[0][:, :], orow[1][:, :], ALU.add)
                tt(orow[2][:, :], orow[2][:, :], orow[1][:, :], ALU.mult).then_inc(s_e["acc"], 1)
                dve.wait_ge(s_e["acc"], 2 * g + 2)
                tt(acc[1][:, :], acc[1][:, :], orow[2][:, :], ALU.add).then_inc(s_e["acc"], 1)
            dve.wait_ge(s_e["acc"], 2 * GE + 1)

            for k in range(2):
                ins = dve.tensor_reduce(corr_rhs[k], acc[k][:, :].rearrange("p (t d) -> p d t", d=D), AX.X, ALU.add)
            step(dve.bn_aggr(sums[:, 0:2], ybn[:, :]))
            step(tt(sums[:, 2:3], sums[:, 0:1], sums[:, 0:1], ALU.mult))
            step(tt(sums[:, 3:4], sums[:, 1:2], sums[:, 2:3], ALU.add))
            for k in range(2):
                ins = ts(st_rhs[k], fold[:, :], sums[:, (0, 3)[k]:(0, 3)[k] + 1], float(N // 2), ALU.mult, ALU.mult)
            step(ins, "moments")
            dve.wait_ge(s_pe, 4)
            ts(mom[:, 0, :], bank[4][:, 0:D], 1.0 / N, None, ALU.mult)
            step(ts(mom[:, 1, :], bank[4][:, D:2 * D], 1.0 / N, None, ALU.mult))
            step(tt(split[:, 0, :], mom[:, 0, :], mom[:, 0, :], ALU.mult))
            step(tt(mom[:, 1, :], mom[:, 1, :], split[:, 0, :], ALU.subtract), "y_var")
            dve.wait_ge(s_std, 1)
            step(dve.reciprocal(mom[:, 1, :], mom[:, 1, :]))
            step(tt(mom[:, 1, :], mom[:, 1, :], row_v[:, 1, :], ALU.mult))
            step(tt(mom[:, 0, :], mom[:, 0, :], row_v[:, 0, :], ALU.add))
            step(tt(mom[:, 0, :], row_v[:, 0, :], mom[:, 0, :], ALU.subtract))
            step(tt(mom[:, 0, :], mom[:, 0, :], mom[:, 1, :], ALU.mult))
            step(tt(mom[:, 0, :], mom[:, 0, :], row_v[:, 2, :], ALU.add))
            step(ts(mom[:, 0, :], mom[:, 0, :], 0.5, None, ALU.mult))
            norm_bias(0, mom[:, 0, :])
            for h in range(2):
                q = slice(h * D, (h + 1) * D)
                ins = stt(w2n[:, q], w2[:, q], 0.5, mom[:, 1, :], ALU.mult, ALU.mult)
            step(ins, "w2n")

            def layer_norm(stage, i, us, buf, stats_, small, nb, names):
                seen, inner, var, std, final = names
                n = T * len(us)
                for u, p in us:
                    for j in range(T):
                        ins = dve.bn_stats(stats_[0:p, u * T + j, :], buf[u][0:p, j * D:(j + 1) * D])
                    ins.then_inc(S[seen], 1)
                c = lambda k: at(inner, stage, i * 4 + k)
                dve.wait_ge(S[seen], at(seen, stage, i * U + len(us)))
                me, m2e, mo, m2o = (stats_[:, 0:n, k] for k in (1, 2, 4, 5))
                tt(small[:, 0, 0:n], me, mo, ALU.add)
                tt(small[:, 1, 0:n], me, mo, ALU.subtract)
                tt(small[:, 2, 0:n], m2e, m2o, ALU.add).then_inc(S[inner], 1)
                dve.wait_ge(S[inner], c(1))
                stt(small[:, 1, 0:n], small[:, 1, 0:n], D / 4.0, small[:, 1, 0:n], ALU.mult, ALU.mult).then_inc(S[inner], 1)
                dve.wait_ge(S[inner], c(2))
                tt(small[:, 3, 0:n], small[:, 1, 0:n], small[:, 2, 0:n], ALU.add).then_inc(S[var], 1)
                dve.wait_ge(S[std], at(std, stage, i + 1))
                dve.reciprocal(small[:, 5, 0:n], small[:, 4, 0:n]).then_inc(S[inner], 1)
                dve.wait_ge(S[inner], c(3))
                stt(nb[:, 0:n], small[:, 0, 0:n], -0.5, small[:, 5, 0:n], ALU.mult, ALU.mult).then_inc(S[inner], 1)
                dve.wait_ge(S[inner], c(4))
                for u, p in us:
                    for j in range(T):
                        k = u * T + j
                        ins = ts(buf[u][0:p, j * D:(j + 1) * D], buf[u][0:p, j * D:(j + 1) * D], small[0:p, 5, k:k + 1],
                                 nb[0:p, k:k + 1], ALU.mult, ALU.add)
                    ins.then_inc(S[final], 1)
            LN1 = ("v_stats", "ln_step", "var_ready", "std_ready", "x1_ready")
            LN2 = ("v2_stats", "ln2_step", "var2_ready", "std2_ready", "out_ready")

            def sum_x(stage, i, us):
                for u, p in us:
                    if stage == "dense":
                        dve.wait_ge(S["v2_ready"], at("v2_ready", stage, i * U + u + 1))
                    else:
                        dve.wait_ge(S[f"stored{u}"], at(f"stored{u}", stage, 16 * (i + 1)))
                    dve.wait_ge(S["y_ready"], at("y_ready", stage, i * U + u + 1))
                    stt(vr[u][0:p, :], bank[2 * u][0:p, :], 0.0, xr[u][0:p, :], ALU.max, ALU.add).then_inc(S["v_ready"], 1)
                dve.wait_ge(S["v_ready"], at("v_ready", stage, U + i * U + len(us)))

            def x1d(i, us):
                for u, p in us:
                    g = i * U + u
                    dve.wait_ge(S["x_turned"], at("x_turned", "x1d", g + 1))
                    dve.wait_ge(S[f"loaded{u}"], at(f"loaded{u}", "x1d", 16 * (i + 1)))
                    stt(orow[u][:, :], xr[u][:, :], eps1[:, 0:1], agg_group(g), ALU.mult, ALU.add).then_inc(S["x0_ready"], 1)
                sum_x("x1d", i, us)
                layer_norm("x1d", i, us, vr, st, lns, lnb, LN1)
            rounds(dve, GE, U, x1d)

            def x1s(i, us):
                sum_x("x1s", i, us)
                layer_norm("x1s", i, us, vr, st, lns, lnb, LN1)
            rounds(dve, GE, U, x1s)
            for u in range(U):
                dve.wait_ge(S[f"stored{u}"], at(f"stored{u}", "x1s", 16 + 16 * per_buffer(GE, U, u)))

            def dense(i, us):
                sum_x("dense", i, us)
                layer_norm("dense", i, us, vr, st, lns, lnb, LN1)
                for u, p in us:
                    dve.wait_ge(S["r2_ready"], at("r2_ready", "dense", i * U + u + 1))
                    dve.wait_ge(S[f"stored{u}"], at(f"stored{u}", "dense", 16 * (i + 1)))
                    dve.wait_ge(S["x1_ready"], at("x1_ready", "dense", i * U + u + 1))
                    tt(orow[u][0:p, :], bank[2 * u][0:p, :], vr[u][0:p, :], ALU.add).then_inc(S["v2_ready"], 1)
                dve.wait_ge(S["v2_ready"], at("v2_ready", "dense", U + i * U + len(us)))
                layer_norm("dense", i, us, orow, st2, lns2, lnb2, LN2)
            rounds(dve, GD, U, dense, last=REST)

            riv = rec_in.rearrange("p (t w) -> p t w", w=WD)
            for h in range(2):
                dve.wait_ge(s_rin, 16 * (h + 1))
                step(dve.tensor_copy(slot_rec[:, h * HALF:(h + 1) * HALF, :], riv[:, :, D:D + 3]),
                     ("half_read", "rec_ready")[h])
            for out_i, k in ((qidx, 0), (lidx, 1)):
                step(ts(inv[:, :], slot_rec[:, :, k], 0.0, float(BIG), ALU.is_equal, ALU.mult))
                step(stt(out_i[:, :], slot_rec[:, :, k], -1.0, inv[:, :], ALU.add, ALU.add))
            dve.wait_ge(s_pe, 5)
            step(dve.tensor_copy(keyT, bank[0][0:HALF, 0:2 * P]), "key_turned")
            dve.wait_ge(s_key, 32)
            step(tt(runF, keyT, keyP, ALU.not_equal))
            tt(runS, runF, slot_no[:, :], ALU.mult)
            step(ts(runX, slot_no[:, :], -float(BIG), None, ALU.add))
            step(tt(runX, runX, runF, ALU.mult))
            step(ts(runE, runX, float(BIG), None, ALU.add))
            for h in range(2):
                q = slice(h * P, (h + 1) * P)
                scan(runS[:, q], runS[:, q], runS[:, q], 0.0, ALU.max, ALU.max)
                e = runE[:, q][:, ::-1]
                ins = scan(e, e, e, float(BIG), ALU.min, ALU.min)
            step(ins, "run_ends")
            dve.wait_ge(s_pe, 6)
            dve.tensor_copy(line[:, 0, 0:TS], bank[1][0:1, 0:TS])
            dve.tensor_copy(line[:, 1, 0:TS], bank[2][0:1, 0:TS])
            dve.memset(line[:, 2, 0:1], 0.0)
            step(dve.memset(line[:, 3, TS:TS + 1], float(BIG)))
            scan(line[:, 2, 1:TS + 1], line[:, 0, 0:TS], line[:, 0, 0:TS], 0.0, ALU.max, ALU.max)
            step(scan(line[:, 3, 0:TS][:, ::-1], line[:, 1, 0:TS][:, ::-1], line[:, 1, 0:TS][:, ::-1], float(BIG),
                      ALU.min, ALU.min), "run_carry")
            dve.wait_ge(s_pe, 7)
            step(dve.tensor_copy(runc[:, :], bank[3][0:HALF, 0:4]))
            for h in range(2):
                q = slice(h * P, (h + 1) * P)
                ts(runS[:, q], runS[:, q], runc[:, h:h + 1], None, ALU.max)
                ts(runX[:, h * P:(h + 1) * P - 1], runE[:, h * P + 1:(h + 1) * P], runc[:, 2 + h:3 + h], None, ALU.min)
                ins = dve.tensor_copy(runX[:, (h + 1) * P - 1:(h + 1) * P], runc[:, 2 + h:3 + h])
            step(ins)
            step(tt(runX, runX, runS, ALU.subtract))
            step(dve.reciprocal(runX, runX), "run_inv")
            dve.wait_ge(s_pe, 8)
            step(dve.tensor_copy(inv[:, :], bank[4][:, 0:TS]), "slots_ready")

            for l in range(L):
                stage = SL[l]

                def slots(i, us, stage=stage):
                    for h, _ in us:
                        dve.wait_ge(S["s_turned"], at("s_turned", stage, 2 + i * 2 + h + 1))
                        dve.tensor_copy(aT[2 * h + 1][0:D, :], bank[4 * h + 1][0:D, :]).then_inc(S["s_copied_b"], 1)
                    for h, _ in us:
                        g = i * 2 + h
                        dve.wait_ge(S["msg_sums"], at("msg_sums", stage, g + 1))
                        dve.wait_ge(S[f"msg_out{h}"], at(f"msg_out{h}", stage, 16 + 16 * T * i))
                        tt(ring_d[h][:, :].rearrange("p (t d) -> p t d", d=D),
                           bank[4 * h + 2][:, :].rearrange("p (t d) -> p t d", d=D),
                           inv[:, bass.ds(g * T, T)].unsqueeze(2).to_broadcast([P, T, D]), ALU.mult).then_inc(S["msg_ready"], 1)
                rounds(dve, GS, 2, slots)
                segment_sum(f"m{l}")
                stage = f"d{l}"

                def dst_stage(i, us, l=l, stage=stage):
                    free = "scattered" if l == L - 1 else "stored"
                    for u, p in us:
                        dve.wait_ge(S[f"{free}{u}"], at(f"{free}{u}", stage, 16 + (16 * T if l == L - 1 else 16) * i))
                        dve.wait_ge(S["y_ready"], at("y_ready", stage, i * U + u + 1))
                        tt(vr[u][:, :], bank[2 * u + 1][:, :], agg_group(i * U + u), ALU.add).then_inc(S["v_ready"], 1)
                    if l == L - 1:
                        for u, p in us:
                            dve.wait_ge(S["v_ready"], at("v_ready", stage, U + i * U + u + 1))
                            dve.wait_ge(S[f"x1_loaded{u}"], at(f"x1_loaded{u}", stage, 16 * (i + 1)))
                            tt(vr[u][:, :], vr[u][:, :], aT[u][:, :], ALU.add).then_inc(S["v_final"], 1)
                        dve.wait_ge(S["v_final"], at("v_final", stage, U + i * U + len(us)))
                        layer_norm(stage, i, us, vr, st, lns, lnb, LN1)
                rounds(dve, GE, U, dst_stage)

        @block.sync
        def _(sp):
            for k, sm in enumerate(s_rst + [S[f"slot_stored{h}"] for h in range(2)]):
                sp.dma_start(primer[:, 24 + k:25 + k], eps.rearrange("(p o) -> p o", p=1)).then_inc(sm, 16)
            sp.wait_ge(s_fill, 1)
            v2 = lambda a, n: a[0:n * TE].rearrange("(p t) -> p t", t=TE)
            sp.dma_start(srci[0:PE_FULL, :], v2(src, PE_FULL)).then_inc(s_idx, 16)
            sp.dma_start(dsti[0:PE_FULL, :], v2(dst, PE_FULL)).then_inc(s_idx, 16)
            sp.dma_start(reli[0:PE_FULL, :], v2(etype, PE_FULL)).then_inc(s_idx, 16)
            sp.dma_start(dprev[1:PE_FULL, :], dst[TE - 1:E - 1].rearrange("(p t) -> p t", t=TE)).then_inc(s_idx, 16)
            sp.dma_start(dprev[0:1, 1:TE], dst[0:TE - 1].rearrange("(p t) -> p t", p=1)).then_inc(s_idx, 16)
            sp.dma_start(dnext[0:PE_FULL - 1, :], dst[1:E - TE + 1].rearrange("(p t) -> p t", t=TE)).then_inc(s_idx, 16)
            sp.dma_start(dnext[PE_FULL - 1:PE_FULL, 0:TE - 1],
                         dst[E - TE + 1:E].rearrange("(p t) -> p t", p=1)).then_inc(s_idx, 16)
            for h in range(2):
                q = slice(h * D, (h + 1) * D)
                for tile, w in ((w1, W1), (w2, W2), (root[0], w0_root), (root[1], w1_root), (root[2], w2_root)):
                    sp.dma_start(tile[q, q], w[:, :]).then_inc(s_wts, 16)
                for tile, b in ((b1c, b1), (rootb[0], b0), (rootb[1], c1), (rootb[2], c2)):
                    sp.dma_start(tile[q, :], b.rearrange("(d o) -> d o", o=1)).then_inc(s_wts, 16)
            for k, b in enumerate((b2, gamma, beta, b0, c1, c2)):
                sp.dma_start(row_v[:, k, :], b.partition_broadcast(P)).then_inc(s_wts, 16)
            sp.dma_start(eps1[:, :], eps.partition_broadcast(P)).then_inc(s_wts, 16)
            wv = rel_w[:, :].rearrange("d (l r o) -> d l r o", l=L, r=R)
            nb = w0_rel.shape[1]
            db = D // nb
            for l, w in ((0, w0_rel), (1, w1_rel)):
                for b in range(nb):
                    q = slice(b * db, (b + 1) * db)
                    sp.dma_start(wv[q, l, :, q], w[:, b].rearrange("r d o -> d r o")).then_inc(s_wts, 16)
            sp.dma_start(wv[:, 2], w2_rel.rearrange("r d o -> d r o")).then_inc(s_wts, 16)

            def load_nodes(stage, i, us):
                for u, p in us:
                    name = "x_turned" if stage == "stats" else "v_ready"
                    sp.wait_ge(S[name], at(name, stage, i * U + u + 1))
                    sp.dma_start(xr[u][0:p, :], node_rows(x, i * U + u, p)).then_inc(S[f"loaded{u}"], 16)

            def store_gathered(i, h):
                sp.wait_ge(s_rows[h], GA * (i + 1))
                g = i * 2 + h
                sp.dma_start(edge_rows(src_x, g), ring_s[h][:, :]).then_inc(s_rst[h], 16)
                sp.dma_start(edge_rows(dst_x, g), ring_d[h][:, :]).then_inc(s_rst[h], 16)

            with sp.Fori(0, GE // 2) as i:
                for h in range(2):
                    load_nodes("stats", i * 2 + h, [(u, P) for u in range(U)])
                    store_gathered(i, h)
            load_nodes("stats", GD // U, [(0, P), (1, REST)])
            store_gathered(GE // 2, 0)

            sp.wait_ge(s_fill, 2)
            sp.dma_start(node_table.rearrange("(p t) o -> p (t o)", p=PE_FULL), zeros[0:PE_FULL, :]).then_inc(s_zero, 16)
            sp.dma_start(msg_rows[E:EP, :].rearrange("(p t) d -> p (t d)", p=120),
                         zeros[0:120, 0:(EP - E) * D // 120]).then_inc(s_zero, 16)
            sp.dma_start(key_line[0:1].rearrange("(p o) -> p o", p=1), zeros[0:1, 0:1]).then_inc(s_zero, 16)
            with sp.Fori(0, GS) as g:
                sp.dma_start(slot_view(0, g), zeros[:, 0:T * WD].rearrange("p (t w) -> p t w", t=T)).then_inc(s_zero, 16)

            sp.wait_ge(s_rst[0], 16 + 32 * per_buffer(GE, 2, 0))
            sp.wait_ge(s_rst[1], 16 + 32 * per_buffer(GE, 2, 1))
            sp.wait_ge(s_dve, DV["sorted"])
            sp.dma_start(agg[:, :], src_x.rearrange("(p t) d -> p (t d)", p=P)).then_inc(S["agg_loaded"], 16)
            with sp.Fori(0, GE) as g:
                sp.wait_ge(s_e["turned"], g + 1)
                sp.dma_start(xr[0][:, :], edge_rows(dst_x, g)).then_inc(s_e["loaded"], 16)

            def load_edges(stage, rows, extra=None):
                def body(i, us):
                    for u, p in us:
                        sp.wait_ge(S["v_ready"], at("v_ready", stage, i * U + u + 1))
                        sp.dma_start(xr[u][:, :], edge_rows(rows, i * U + u)).then_inc(S[f"loaded{u}"], 16)
                        if extra is not None:
                            sp.wait_ge(S["v_final"], at("v_final", stage, i * U + u + 1))
                            sp.dma_start(aT[u][:, :], edge_rows(extra, i * U + u)).then_inc(S[f"x1_loaded{u}"], 16)
                rounds(sp, GE, U, body)

            sp.wait_ge(s_e["acc"], 2 * GE + 1)
            load_edges("x1d", dst_x)
            sp.wait_ge(S["v_ready"], at("v_ready", "x1d", GE + U))
            load_edges("x1s", src_x)
            sp.wait_ge(S["v_ready"], at("v_ready", "x1s", GE + U))
            rounds(sp, GD, U, lambda i, us: load_nodes("dense", i, us), last=REST)

            for h in range(2):
                sp.wait_ge(s_ws[h], 16 + 16 * T * per_buffer(GE, 2, h))
            sv = slot_rows[0].rearrange("(p t) w -> p t w", p=P)
            sp.wait_ge(S["x0_ready"], at("x0_ready", "x1d", GE))
            for h in range(2):
                if h:
                    sp.wait_ge(s_dve, DV["half_read"])
                sp.dma_start(rec_in.rearrange("p (t w) -> p t w", w=WD), sv[:, h * HALF:(h + 1) * HALF, :]).then_inc(s_rin, 16)
            sp.wait_ge(s_dve, DV["key_turned"])
            kl = key_line[1:NS + 1].rearrange("(h t c) -> t h c", h=2, c=P)
            sp.dma_start(kl, keyT.rearrange("t (h c) -> t h c", h=2)).then_inc(s_key, 16)
            sp.wait_ge(s_key, 16)
            sp.dma_start(keyP.rearrange("t (h c) -> t h c", h=2),
                         key_line[0:NS].rearrange("(h t c) -> t h c", h=2, c=P)).then_inc(s_key, 16)

            for l in range(L):
                stage = SL[l]

                def slots(i, us, l=l, stage=stage):
                    for h, _ in us:
                        sp.wait_ge(S["s_turned"], at("s_turned", stage, i * 2 + h + 1))
                        dest = srow[h] if l == 0 else srow[h][:, :, 0:D]
                        sp.dma_start(dest, slot_view(l, i * 2 + h)).then_inc(S[f"slot_loaded{h}"], 16)
                    for h, _ in us:
                        if l < L - 1:
                            sp.wait_ge(S["base_relu"], at("base_relu", stage, i * 2 + h + 1))
                            sp.dma_start(slot_view(l + 1, i * 2 + h),
                                         ring_s[h][:, :].rearrange("p (t d) -> p t d", d=D)).then_inc(S[f"slot_stored{h}"], 16)
                if l:
                    for h in range(2):
                        sp.wait_ge(S[f"slot_stored{h}"], at(f"slot_stored{h}", SL[l - 1], 16 + 16 * per_buffer(GS, 2, h)))
                rounds(sp, GS, 2, slots)
                for h in range(2):
                    sp.wait_ge(S[f"msg_out{h}"], at(f"msg_out{h}", stage, 16 + 16 * T * per_buffer(GS, 2, h)))
                sp.wait_ge(S["v_ready"], at("v_ready", f"d{l - 1}" if l else "dense", (GE if l else GD) + U))
                if l == 0:
                    sp.wait_ge(s_dve, DV["slots_ready"])
                sp.dma_start(agg[:, :], msg_rows.rearrange("(p t) d -> p (t d)", p=P)).then_inc(S["agg_loaded"], 16)
                load_edges(f"d{l}", dst_rows[l], dst_rows[0] if l == L - 1 else None)

        @block.gpsimd
        def _(pool):
            def pad():
                pool.sem_inc(s_pad, 1)

            for w_ in (w1, w2, root[0], root[1], root[2], rel_w):
                pool.memset(w_[:, :], 0.0)
            for t_, v_ in ((srci, 0), (dsti, N), (reli, R), (dprev, -1)):
                pool.memset(t_[:, :], v_)
            pool.memset(dnext[:, :], N).then_inc(s_fill, 1)
            pool.memset(zeros[:, :], 0.0).then_inc(s_fill, 1)
            for k, sm in enumerate(s_tab + s_ws + [S[f"msg_out{h}"] for h in range(2)] + [S[f"scattered{u}"] for u in range(U)]):
                pool.dma_start(primer[:, k:k + 1], eps.rearrange("(p o) -> p o", p=1)).then_inc(sm, 16)
            pool.iota(bins[:, :], [[1, R]], base=0, channel_multiplier=0, allow_small_or_imprecise_dtypes=True)
            pool.iota(tile_no[:, :], [[HALF, 2]], base=0, channel_multiplier=1, allow_small_or_imprecise_dtypes=True)
            pool.iota(slot_no[:, :], [[HALF * P, 2], [1, P]], base=0, channel_multiplier=P,
                      allow_small_or_imprecise_dtypes=True)
            pool.iota(edge1[:, :], [[1, TE]], base=1, channel_multiplier=TE, allow_small_or_imprecise_dtypes=True)
            pool.memset(ident[:, :], 0.0)
            pool.memset(fold[:, :], 0.0)
            pool.memset(before[:, :], 1.0)
            pool.memset(ones[:, :], 1.0).then_inc(s_fill, 1)
            pool.wait_ge(s_fill, 3)
            pool.affine_select(out=ident[:, :], in_=ident[:, :], compare_op=ALU.not_equal, fill=1.0, base=0,
                               pattern=[[-1, P]], channel_multiplier=1)
            pool.affine_select(out=before[:, :], in_=before[:, :], compare_op=ALU.is_gt, fill=0.0, base=0,
                               pattern=[[1, P]], channel_multiplier=-1)
            pool.affine_select(out=fold[:, :], in_=fold[:, :], compare_op=ALU.not_equal, fill=1.0, base=0,
                               pattern=[[-1, D]], channel_multiplier=1).then_inc(s_fill, 1)
            pool.wait_ge(s_fill, 4)
            pool.affine_select(out=fold[:, :], in_=fold[:, :], compare_op=ALU.not_equal, fill=1.0, base=-D,
                               pattern=[[-1, D]], channel_multiplier=1).then_inc(s_fill, 1)

            pool.wait_ge(s_idx, 16 * 7)
            pool.wait_ge(s_dve, DV["dst_clamped"])

            def gather_x(i, us):
                for h, _ in us:
                    g = i * 2 + h
                    pool.wait_ge(s_rst[h], 16 + 32 * i)
                    pad()
                    pool.tensor_copy(idx_a[h][:, :], srci[:, bass.ds(g * T, T)])
                    pool.tensor_copy(idx_b[h][:, :], dclamp[:, bass.ds(g * T, T)]).then_inc(s_cp, 1)
                    pool.wait_ge(s_cp, g + 1)
                    pad()
                    for k in range(T):
                        for ring, idx in ((ring_s, idx_a), (ring_d, idx_b)):
                            pool.indirect_dma_start(
                                out=ring[h][:, k * D:(k + 1) * D], out_offset=None, in_=x[:, :],
                                in_offset=bass.IndirectOffsetOnAxis(ap=idx[h][:, k:k + 1], axis=0)
                            ).then_inc(s_rows[h], 16)
            rounds(pool, GE, 2, gather_x)

            pool.wait_ge(s_zero, 16 * (3 + GS))
            pool.wait_ge(s_dve, DV["sorted"])
            for h in range(2):
                pool.wait_ge(s_rows[h], GA * per_buffer(GE, 2, h))

            def write_table(i, us):
                for h, _ in us:
                    g = i * 2 + h
                    pool.wait_ge(s_tab[h], 16 + 16 * T * i)
                    pad()
                    pool.tensor_copy(idx_a[h][:, :], last_i[:, bass.ds(g * T, T)])
                    pool.tensor_copy(val[h][:, :], edge1[:, bass.ds(g * T, T)]).then_inc(s_cp, 1)
                    pool.wait_ge(s_cp, GE + g + 1)
                    pad()
                    for k in range(T):
                        pool.indirect_dma_start(
                            out=node_table[:, :], out_offset=bass.IndirectOffsetOnAxis(ap=idx_a[h][:, k:k + 1], axis=0),
                            in_=val[h][:, k:k + 1], in_offset=None, bounds_check=N - 1, oob_is_err=False
                        ).then_inc(s_tab[h], 16)
            rounds(pool, GE, 2, write_table)
            for h in range(2):
                pool.wait_ge(s_tab[h], 16 + 16 * T * per_buffer(GE, 2, h))

            def read_table(i, us):
                def fetch(u):
                    g = i * U + u
                    pool.wait_ge(s_lc, g + 1)
                    pad()
                    pool.tensor_copy(idx_a[u][:, :], srci[:, bass.ds(g * T, T)]).then_inc(s_cp, 1)
                    pool.wait_ge(s_cp, 2 * GE + g + 1)
                    pad()
                    for k in range(T):
                        pool.indirect_dma_start(
                            out=val[u][:, k:k + 1], out_offset=None, in_=node_table[:, :],
                            in_offset=bass.IndirectOffsetOnAxis(ap=idx_a[u][:, k:k + 1], axis=0)
                        ).then_inc(s_look[u], 16)

                def keep_value(u):
                    pool.wait_ge(s_look[u], 16 * T * (i + 1))
                    pad()
                    pool.tensor_copy(rec[:, bass.ds((i * U + u) * T, T), 1], val[u][:, :]).then_inc(s_lc, 1)
                ks = [u for u, _ in us]
                for u in ks:
                    fetch(u)
                    if u:
                        keep_value(u - 1)
                keep_value(ks[-1])
            pool.sem_inc(s_lc, U)
            rounds(pool, GE, U, read_table)
            pool.wait_ge(s_lc, GE + U)

            for u in range(U):
                pool.wait_ge(S[f"stored{u}"], at(f"stored{u}", "x1s", 16 + 16 * per_buffer(GE, U, u)))

            def to_slots(i, us):
                for h, _ in us:
                    g = i * 2 + h
                    pool.wait_ge(s_ws[h], 16 + 16 * T * i)
                    pad()
                    pool.dma_start(wide[h][:, :, 0:D], edge_rows(src_x1, g).rearrange("p (t d) -> p t d", d=D)).then_inc(s_wl[h], 16)
                    pool.tensor_copy(wide[h][:, :, D:WD], rec[:, bass.ds(g * T, T), :])
                    pool.tensor_copy(idx_a[h][:, :], addr_i[:, bass.ds(g * T, T)]).then_inc(s_cp, 1)
                for h, _ in us:
                    g = i * 2 + h
                    pool.wait_ge(s_cp, 3 * GE + g + 1)
                    pool.wait_ge(s_wl[h], 16 * (i + 1))
                    pad()
                    for k in range(T):
                        pool.indirect_dma_start(
                            out=slot_rows[0][:, :], out_offset=bass.IndirectOffsetOnAxis(ap=idx_a[h][:, k:k + 1], axis=0),
                            in_=wide[h][:, k, :], in_offset=None, bounds_check=NS - 1, oob_is_err=False
                        ).then_inc(s_ws[h], 16)
            rounds(pool, GE, 2, to_slots)

            for h in range(2):
                pool.wait_ge(s_ws[h], 16 + 16 * T * per_buffer(GE, 2, h))
            pool.wait_ge(s_dve, DV["slots_ready"])
            for l in range(L):
                stage = SL[l]
                if l == 0:
                    for u in range(U):
                        pool.wait_ge(S[f"stored{u}"], at(f"stored{u}", "x1d", 16 + 16 * per_buffer(GE, U, u)))
                else:
                    for u in range(U):
                        pool.wait_ge(S[f"stored{u}"], at(f"stored{u}", f"d{l - 1}", 16 + 16 * per_buffer(GE, U, u)))
                    pool.wait_ge(S["agg_loaded"], at("agg_loaded", f"m{l - 1}", 16))

                def exchange(i, us, l=l, stage=stage):
                    for h, _ in us:
                        g = i * 2 + h
                        pool.wait_ge(S[f"msg_out{h}"], at(f"msg_out{h}", stage, 16 + 16 * T * i))
                        pool.wait_ge(S[f"slot_loaded{h}"], at(f"slot_loaded{h}", stage, 16 * (i + 1)))
                        pad()
                        pool.tensor_copy(idx_a[h][:, :], lidx[:, bass.ds(g * T, T)])
                        pool.tensor_copy(idx_b[h][:, :], qidx[:, bass.ds(g * T, T)]).then_inc(S["slot_idx"], 1)
                        pool.wait_ge(S["slot_idx"], at("slot_idx", stage, g + 1))
                        pad()
                        for k in range(T):
                            pool.indirect_dma_start(
                                out=wide[h][:, k, 0:D], out_offset=None, in_=dst_rows[l][:, :],
                                in_offset=bass.IndirectOffsetOnAxis(ap=idx_a[h][:, k:k + 1], axis=0),
                                bounds_check=EP - 1, oob_is_err=False).then_inc(S[f"fetched{h}"], 16)
                    for h, _ in us:
                        g = i * 2 + h
                        pool.wait_ge(S["msg_ready"], at("msg_ready", stage, g + 1))
                        pad()
                        for k in range(T):
                            pool.indirect_dma_start(
                                out=msg_rows[:, :],
                                out_offset=bass.IndirectOffsetOnAxis(ap=idx_b[h][:, k:k + 1], axis=0),
                                in_=ring_d[h][:, k * D:(k + 1) * D], in_offset=None, bounds_check=EP - 1,
                                oob_is_err=False).then_inc(S[f"msg_out{h}"], 16)
                rounds(pool, GS, 2, exchange)

            for u in range(U):
                pool.wait_ge(S[f"stored{u}"], at(f"stored{u}", "dense", 16 + 16 * per_buffer(GD, U, u)))
            for h in range(2):
                pool.wait_ge(S[f"msg_out{h}"], at(f"msg_out{h}", SL[-1], 16 + 16 * T * per_buffer(GS, 2, h)))

            def write_out(i, us):
                for u, _ in us:
                    g = i * U + u
                    pool.wait_ge(S[f"scattered{u}"], at(f"scattered{u}", "d2", 16 + 16 * T * i))
                    pad()
                    pool.tensor_copy(idx_a[u][:, :], last_i[:, bass.ds(g * T, T)]).then_inc(s_cp, 1)
                    pool.wait_ge(s_cp, 4 * GE + g + 1)
                    pool.wait_ge(S["x1_ready"], at("x1_ready", "d2", g + 1))
                    pad()
                    for k in range(T):
                        pool.indirect_dma_start(
                            out=out[:, :], out_offset=bass.IndirectOffsetOnAxis(ap=idx_a[u][:, k:k + 1], axis=0),
                            in_=vr[u][:, k * D:(k + 1) * D], in_offset=None, bounds_check=N - 1,
                            oob_is_err=False).then_inc(S[f"scattered{u}"], 16)
            rounds(pool, GE, U, write_out)
            for u in range(U):
                pool.wait_ge(S[f"scattered{u}"], at(f"scattered{u}", "d2", 16 + 16 * T * per_buffer(GE, U, u)))

        @block.scalar
        def _(act):
            for u in range(U):
                act.dma_start(primer[:, 16 + u:17 + u], eps.rearrange("(p o) -> p o", p=1)).then_inc(S[f"stored{u}"], 16)
            act.wait_ge(s_wts, WTS)
            act.wait_ge(s_dve, DV["eps"])

            def relu_hidden(stage, i, us, scale):
                for u, p in us:
                    act.wait_ge(S["hid_ready"], at("hid_ready", stage, i * U + u + 1))
                    act.activation(aT[u][:, 0:4 * p], bank[2 * u + 1][:, 0:4 * p], ACT.Relu, bias=b1c[:, 0:1],
                                   scale=scale).then_inc(S["hid_relu"], 1)

            def root_std(stage, var, std, i, us, k):
                act.wait_ge(S[var], at(var, stage, i + 1))
                n = T * len(us)
                small = lns2 if var == "var2_ready" else lns
                act.activation(small[:, 4, 0:n], small[:, 3, 0:n], ACT.Sqrt, bias=const[:, k:k + 1],
                               scale=1.0 / D).then_inc(S[std], 1)

            def copy_x(stage, i, us):
                for u, p in us:
                    act.wait_ge(S["x_turned"], at("x_turned", stage, U + i * U + u + 1))
                    act.activation(xT[u][:, 0:4 * p], bank[2 * u][:, 0:4 * p], ACT.Copy).then_inc(S["x_copied"], 1)

            rounds(act, GD, U, lambda i, us: relu_hidden("stats", i, us, eps1[:, 0:1]), last=REST)

            with act.Fori(0, GE) as g:
                act.wait_ge(s_e["hid"], g + 1)
                act.activation(aT[0][:, :], bank[1][:, :], ACT.Relu, bias=b1c[:, 0:1], scale=eps1[:, 0:1])
                act.activation(aT[1][:, :], bank[3][:, :], ACT.Relu, bias=b1c[:, 0:1]).then_inc(s_e["relu"], 1)
                act.wait_ge(s_e["y"], g + 1)
                act.wait_ge(s_e["acc"], 2 * g + 1)
                act.activation(orow[0][:, :], bank[0][:, :], ACT.Copy).then_inc(s_e["base"], 1)

            act.wait_ge(s_dve, DV["y_var"])
            act.activation(mom[:, 1, :], mom[:, 1, :], ACT.Sqrt, bias=const[:, 1:2]).then_inc(s_std, 1)

            def x1_stage(stage, scale, dest):
                def body(i, us):
                    copy_x(stage, i, us)
                    relu_hidden(stage, i, us, scale)
                    root_std(stage, "var_ready", "std_ready", i, us, 0)
                    for u, p in us:
                        act.wait_ge(S["x1_ready"], at("x1_ready", stage, i * U + u + 1))
                        act.dma_start(edge_rows(dest, i * U + u), vr[u][:, :]).then_inc(S[f"stored{u}"], 16)
                rounds(act, GE, U, body)
            x1_stage("x1d", 1.0, dst_rows[0])
            x1_stage("x1s", eps1[:, 0:1], src_x1)

            def dense(i, us):
                copy_x("dense", i, us)
                relu_hidden("dense", i, us, eps1[:, 0:1])
                root_std("dense", "var_ready", "std_ready", i, us, 0)
                for u, p in us:
                    act.wait_ge(S["x1_turned"], at("x1_turned", "dense", i * U + u + 1))
                    act.activation(xT[u][:, 0:4 * p], bank[2 * u + 1][:, 0:4 * p], ACT.Copy).then_inc(S["x1_copied"], 1)
                for u, p in us:
                    act.wait_ge(S["r0_ready"], at("r0_ready", "dense", i * U + u + 1))
                    act.activation(aT[u][:, 0:4 * p], bank[2 * u][:, 0:4 * p], ACT.Relu, bias=rootb[0][:, 0:1]).then_inc(S["r0_relu"], 1)
                for u, p in us:
                    act.wait_ge(S["r1_ready"], at("r1_ready", "dense", i * U + u + 1))
                    act.activation(xT[u][:, 0:4 * p], bank[2 * u + 1][:, 0:4 * p], ACT.Relu, bias=rootb[1][:, 0:1]).then_inc(S["r1_relu"], 1)
                root_std("dense", "var2_ready", "std2_ready", i, us, 1)
                for u, p in us:
                    act.wait_ge(S["out_ready"], at("out_ready", "dense", i * U + u + 1))
                    act.dma_start(node_rows(out, i * U + u, p), orow[u][0:p, :]).then_inc(S[f"stored{u}"], 16)
            rounds(act, GD, U, dense, last=REST)

            for l in range(L):
                stage = SL[l]

                def slots(i, us, l=l, stage=stage):
                    for h, _ in us:
                        act.wait_ge(S["s_turned"], at("s_turned", stage, 2 + i * 2 + h + 1))
                        act.activation(aT[2 * h][0:D, :], bank[4 * h][0:D, :], ACT.Copy).then_inc(S["s_copied_a"], 1)
                    if l < L - 1:
                        for h, _ in us:
                            act.wait_ge(S["base_ready"], at("base_ready", stage, i * 2 + h + 1))
                            act.wait_ge(S[f"slot_stored{h}"], at(f"slot_stored{h}", stage, 16 * (i + 1)))
                            act.activation(ring_s[h][:, :], bank[4 * h + 3][:, :], ACT.Relu).then_inc(S["base_relu"], 1)
                rounds(act, GS, 2, slots)
                stage = f"d{l}"

                def dst_stage(i, us, l=l, stage=stage):
                    copy_x(stage, i, us)
                    if l == L - 1:
                        root_std(stage, "var_ready", "std_ready", i, us, 1)
                        return
                    for u, _ in us:
                        act.wait_ge(S["v_ready"], at("v_ready", stage, U + i * U + u + 1))
                        act.activation(vr[u][:, :], vr[u][:, :], ACT.Relu).then_inc(S["x1_ready"], 1)
                    for u, _ in us:
                        act.wait_ge(S["x1_ready"], at("x1_ready", stage, i * U + u + 1))
                        act.dma_start(edge_rows(dst_rows[l + 1], i * U + u), vr[u][:, :]).then_inc(S[f"stored{u}"], 16)
                rounds(act, GE, U, dst_stage)

        @block.tensor
        def _(pe):
            mm = pe.matmul
            pe.sem_inc(S["x_turned"], U)
            step = [0]

            def done(ins):
                step[0] += 1
                ins.then_inc(s_pe, 1)

            pe.wait_ge(s_fill, 5)
            pe.wait_ge(s_dve, DV["counted"])
            mm(bank[0][:, 0:R], before[:, :], tot[:, :], start=True, stop=True)
            done(mm(bank[0][:, R:2 * R], ones[:, :], tot[:, :], start=True, stop=True))
            pe.wait_ge(s_dve, DV["tile_rel"])
            mm(bank[1][0:1, 0:HALF], relt[:, 0:1], ident[0:HALF, 0:HALF], start=True, stop=True)
            done(mm(bank[1][0:1, HALF:TS], relt[:, 1:2], ident[0:HALF, 0:HALF], start=True, stop=True))
            done(mm(bank[2][0:D, 0:P], ak[:, :], ident[:, :], start=True, stop=True))
            pe.wait_ge(s_dve, DV["sorted"])
            pe.wait_ge(s_wts, WTS)

            def turn(dest, rows, p):
                for j in range(4):
                    ins = pe.transpose(dest[:, j * p:(j + 1) * p], rows[0:p, j * P:(j + 1) * P], ident[0:p, 0:p])
                return ins

            def turn_x(stage, i, us, rows=None):
                for u, p in us:
                    if rows is None:
                        pe.wait_ge(S[f"loaded{u}"], at(f"loaded{u}", stage, 16 * (i + 1)))
                        if stage == "stats":
                            pe.wait_ge(S["y_counted"], at("y_counted", stage, i * U + u + 1))
                        elif stage == "dense":
                            pe.wait_ge(S["v2_ready"], at("v2_ready", stage, i * U + u + 1))
                        else:
                            pe.wait_ge(S["v_ready"], at("v_ready", stage, i * U + u + 1))
                        turn(bank[2 * u], xr[u], p).then_inc(S["x_turned"], 1)
                    else:
                        pe.wait_ge(S["x0_ready"], at("x0_ready", stage, i * U + u + 1))
                        turn(bank[2 * u], rows[u], p).then_inc(S["x_turned"], 1)

            def hidden(stage, i, us):
                for u, p in us:
                    pe.wait_ge(S["x_copied"], at("x_copied", stage, i * U + u + 1))
                    mm(bank[2 * u + 1][:, 0:4 * p], w1[:, :], xT[u][:, 0:4 * p], start=True, stop=True).then_inc(S["hid_ready"], 1)

            def rows_out(dest, lhs, w, bias, p):
                if bias is not None:
                    mm(dest[0:p, :], pick3[:, 0:p], bias[:, :], start=True, stop=False, skip_group_check=True)
                for j in range(4):
                    ins = mm(dest[0:p, j * P:(j + 1) * P], lhs[:, j * p:(j + 1) * p], w[:, :], start=bias is None,
                             stop=True, skip_group_check=True)
                return ins

            def stats(i, us):
                turn_x("stats", i, us)
                hidden("stats", i, us)
                for u, p in us:
                    pe.wait_ge(S["hid_relu"], at("hid_relu", "stats", i * U + u + 1))
                    mm(bank[2 * u][:, 0:4 * p], w2[:, :], aT[u][:, 0:4 * p], start=True, stop=True).then_inc(S["y_ready"], 1)
            rounds(pe, GD, U, stats, last=REST)
            pe.wait_ge(S["y_counted"], at("y_counted", "stats", GD + U))

            def carry_turns(use):
                pe.wait_ge(S["scanned"], at("scanned", use, D))
                pe.transpose(bank[4][0:D, 0:P], agg[:, (TE - 1) * D:TE * D], ident[:, :]).then_inc(S["end_turned"], 1)
                pe.wait_ge(S["carry_step"], at("carry_step", use, 2))
                pe.transpose(bank[5][:, 0:D], carT[:, 0:P], ident[0:D, 0:D]).then_inc(S["carry_turned"], 1)
                pe.wait_ge(S["carry_step"], at("carry_step", use, 3))
            carry_turns("neigh")

            pe.sem_inc(s_e["turned"], 1)
            with pe.Fori(0, GE) as g:
                pe.wait_ge(s_e["x0"], g + 1)
                pe.wait_ge(s_e["acc"], 2 * g + 1)
                turn(bank[0], xr[0], P)
                turn(bank[2], xr[1], P).then_inc(s_e["turned"], 1)
                pe.wait_ge(s_e["copied"], g + 1)
                mm(bank[1][:, :], w1[:, :], xT[0][:, :], start=True, stop=True)
                mm(bank[3][:, :], w1[:, :], xT[1][:, :], start=True, stop=True).then_inc(s_e["hid"], 1)
                pe.wait_ge(s_e["relu"], g + 1)
                rows_out(bank[0], aT[0], w2, None, P)
                rows_out(bank[2], aT[1], w2, None, P).then_inc(s_e["y"], 1)

            pe.wait_ge(s_dve, DV["moments"])
            for k in range(2):
                mm(bank[4][:, k * D:(k + 1) * D], ones[:, :], st_rhs[k], start=True, stop=False, skip_group_check=True)
                ins = mm(bank[4][:, k * D:(k + 1) * D], ones[:, :], corr_rhs[k], start=False, stop=True, skip_group_check=True)
            done(ins)
            pe.wait_ge(s_dve, DV["w2n"])

            def x1_stage(stage, rows):
                def body(i, us):
                    turn_x(stage, i, us, rows)
                    hidden(stage, i, us)
                    for u, p in us:
                        pe.wait_ge(S["hid_relu"], at("hid_relu", stage, i * U + u + 1))
                        rows_out(bank[2 * u], aT[u], w2n, bias3[0], p).then_inc(S["y_ready"], 1)
                rounds(pe, GE, U, body)
            x1_stage("x1d", orow)
            x1_stage("x1s", None)

            def dense(i, us):
                turn_x("dense", i, us)
                hidden("dense", i, us)
                for u, p in us:
                    pe.wait_ge(S["hid_relu"], at("hid_relu", "dense", i * U + u + 1))
                    rows_out(bank[2 * u], aT[u], w2n, bias3[0], p).then_inc(S["y_ready"], 1)
                for u, p in us:
                    pe.wait_ge(S["x1_ready"], at("x1_ready", "dense", i * U + u + 1))
                    turn(bank[2 * u + 1], vr[u], p).then_inc(S["x1_turned"], 1)
                for u, p in us:
                    pe.wait_ge(S["x1_copied"], at("x1_copied", "dense", i * U + u + 1))
                    mm(bank[2 * u][:, 0:4 * p], root[0][:, :], xT[u][:, 0:4 * p], start=True, stop=True).then_inc(S["r0_ready"], 1)
                for u, p in us:
                    pe.wait_ge(S["r0_relu"], at("r0_relu", "dense", i * U + u + 1))
                    mm(bank[2 * u + 1][:, 0:4 * p], root[1][:, :], aT[u][:, 0:4 * p], start=True, stop=True).then_inc(S["r1_ready"], 1)
                for u, p in us:
                    pe.wait_ge(S["r1_relu"], at("r1_relu", "dense", i * U + u + 1))
                    rows_out(bank[2 * u], xT[u], root[2], bias3[3], p).then_inc(S["r2_ready"], 1)
            rounds(pe, GD, U, dense, last=REST)

            pe.wait_ge(s_dve, DV["rec_ready"])
            for h in range(2):
                ins = pe.transpose(bank[0][0:HALF, h * P:(h + 1) * P],
                                   slot_rec[:, h * HALF:(h + 1) * HALF, 2], ident[:, :])
            done(ins)
            pe.wait_ge(s_dve, DV["run_ends"])
            for h in range(2):
                mm(bank[1][0:1, h * HALF:(h + 1) * HALF], runS[:, (h + 1) * P - 1:(h + 1) * P], ident[0:HALF, 0:HALF],
                   start=True, stop=True)
                ins = mm(bank[2][0:1, h * HALF:(h + 1) * HALF], runE[:, h * P:h * P + 1], ident[0:HALF, 0:HALF],
                         start=True, stop=True)
            done(ins)
            pe.wait_ge(s_dve, DV["run_carry"])
            for h in range(2):
                mm(bank[3][0:HALF, h:h + 1], line[0:1, 2, h * HALF:(h + 1) * HALF], ones[0:1, 0:1], start=True, stop=True)
                ins = mm(bank[3][0:HALF, 2 + h:3 + h], line[0:1, 3, 1 + h * HALF:1 + (h + 1) * HALF], ones[0:1, 0:1],
                         start=True, stop=True)
            done(ins)
            pe.wait_ge(s_dve, DV["run_inv"])
            for h in range(2):
                ins = pe.transpose(bank[4][:, h * HALF:(h + 1) * HALF], runX[:, h * P:(h + 1) * P], ident[0:HALF, 0:HALF])
            done(ins)
            pe.wait_ge(s_dve, DV["slots_ready"])
            pe.sem_inc(S["s_turned"], 2)

            for l in range(L):
                stage = SL[l]

                def slots(i, us, l=l, stage=stage):
                    for h, _ in us:
                        pe.wait_ge(S[f"fetched{h}"], at(f"fetched{h}", stage, 16 * T * (i + 1)))
                        pe.sem_inc(s_pad_pe, 1)
                        for k in range(T):
                            b = bank[4 * h + k // 4]
                            ins = pe.transpose(b[0:D, (k % 4) * P:(k % 4 + 1) * P], wide[h][:, k, 0:D], ident[:, :])
                        ins.then_inc(S["s_turned"], 1)
                    for h, _ in us:
                        g = i * 2 + h
                        pe.wait_ge(S["s_copied_a"], at("s_copied_a", stage, g + 1))
                        pe.wait_ge(S["s_copied_b"], at("s_copied_b", stage, g + 1))
                        for k in range(T):
                            r = pe.value_load(rel_tab[0:1, bass.ds(g * T + k, 1)], min_val=0, max_val=R - 1)
                            lhs = aT[2 * h + k // 4][0:D, (k % 4) * P:(k % 4 + 1) * P]
                            ins = mm(bank[4 * h + 2][:, k * D:(k + 1) * D], lhs,
                                     rel_w[:, bass.ds((r + l * R) * D, D)], start=True, stop=True)
                        ins.then_inc(S["msg_sums"], 1)
                        if l < L - 1:
                            b = bank[4 * h + 3]
                            mm(b[:, :], pick3[:, :], bias3[1 + l][:, :], start=True, stop=False, skip_group_check=True)
                            for k in range(T):
                                lhs = aT[2 * h + k // 4][0:D, (k % 4) * P:(k % 4 + 1) * P]
                                ins = mm(b[:, k * D:(k + 1) * D], lhs, root[l][0:D, 0:D], start=False, stop=True,
                                         skip_group_check=True)
                            ins.then_inc(S["base_ready"], 1)
                rounds(pe, GS, 2, slots)
                carry_turns(f"m{l}")
                stage = f"d{l}"

                def dst_stage(i, us, l=l, stage=stage):
                    turn_x(stage, i, us)
                    for u, p in us:
                        pe.wait_ge(S["x_copied"], at("x_copied", stage, i * U + u + 1))
                        rows_out(bank[2 * u + 1], xT[u], root[l], bias3[1 + l], p).then_inc(S["y_ready"], 1)
                rounds(pe, GE, U, dst_stage)



_INS = ['x', 'src', 'dst', 'edge_type_50', 'L0_gnn_W1', 'L0_gnn_b1', 'L0_gnn_W2', 'L0_gnn_b2', 'L0_gnn_gamma',
        'L0_gnn_beta', 'L0_gnn_eps', 'L1_gnn_w0_rel', 'L1_gnn_w0_root', 'L1_gnn_b0', 'L1_gnn_w1_rel',
        'L1_gnn_w1_root', 'L1_gnn_b1', 'L1_gnn_w2_rel', 'L1_gnn_w2_root', 'L1_gnn_b2']


def kernel(**inputs):
    import concourse.bacc as _bacc
    from concourse.bass_utils import run_bass_kernel_spmd as _run

    nc = _bacc.Bacc("TRN2", target_bir_lowering=False, num_devices=1)
    arrays, args = {}, []
    for name in _INS:
        a = np.ascontiguousarray(inputs[name])
        arrays[f"in_{name}_dram"] = a
        args.append(nc.dram_tensor(f"in_{name}_dram", a.shape, mybir.dt.from_np(a.dtype), kind="ExternalInput").ap())
    out = nc.dram_tensor("out_0_dram", (N, D), F32, kind="ExternalOutput").ap()
    build(nc, *args, out)
    r = _run(nc, [arrays], core_ids=[0])
    return r.results[0]["out_0_dram"]
```

```python
import numpy as np
import concourse.bass as bass
from concourse import mybir
from contextlib import ExitStack

F32 = mybir.dt.float32
BF16 = mybir.dt.bfloat16
I32 = mybir.dt.int32
ALU = mybir.AluOpType
ACT = mybir.ActivationFunctionType
AX = mybir.AxisListType

N, E, D, R = 100000, 25000, 64, 50
L = 3
P = 128
T = 8
TE = -(-E // (P * T)) * T
EP = P * TE
PE_FULL = E // TE
GE = TE // T
TS = -(-(E // P + R) // T) * T
NS = P * TS
GS = TS // T
ROWS = P * T
GD_FULL = N // ROWS
REST = (N - GD_FULL * ROWS) // T
GD = GD_FULL + 1
GM = GS // 2
U = 4
W = T * D
REC = 4
WD = D + REC
BIG = 1 << 23
BINS = 10
DIGIT = 5
RADIX = 1 << DIGIT
PASSES = -(-(N - 1).bit_length() // DIGIT)
HALF = TS // 2
EPS = 1e-5
DENSE_ONLY = GD - 2 * GM * 3
FIRST = dict(stats=0, dense=2 * GM * 3, mix0=0, mix1=2 * GM, mix2=4 * GM)

assert PE_FULL * TE == E and REST * T + GD_FULL * ROWS == N and HALF <= P and GS % 2 == 1


def iters(n, u):
    return -(-n // u)


def width(stage):
    return 2 if stage.startswith("mix") else U


def per_buffer(n, u, k):
    return (n - k + u - 1) // u


class Signals:

    def __init__(self, make, plan):
        self.sem, self.base = {}, {}
        for name, uses in plan.items():
            self.sem[name] = make(name)
            done = 0
            for stage, count in uses:
                self.base[name, stage] = done
                done += count

    def at(self, name, stage, count):
        return self.base[name, stage] + count


def rounds(eng, n, u, body, last=P):
    full, rest = divmod(n, u)
    if not rest and last != P:
        full, rest = full - 1, u
    with eng.Fori(0, full) as i:
        body(i, [(k, P) for k in range(u)])
    if rest:
        body(full, [(k, P if k < rest - 1 else last) for k in range(rest)])


def build(nc, x, src, dst, etype, W1, b1, W2, b2, gamma, beta, eps, w0_rel, w0_root, b0, w1_rel,
          w1_root, c1, w2_rel, w2_root, c2, out):
    ctx = ExitStack()
    with ctx:
        def sb(name, shape, dt=F32):
            return ctx.enter_context(nc.sbuf_tensor(name, shape, dt))

        def dram(name, shape, dt=F32):
            return nc.dram_tensor(name, shape, dt, kind="Internal").ap()

        def sem(name):
            return ctx.enter_context(nc.semaphore(name))

        src_x = dram("src_x", (EP, D))
        dst_x = dram("dst_x", (EP, D))
        dst_rows = [dram(f"dst_rows{l}", (EP, D)) for l in range(L)]
        src_x1 = dram("src_x1", (EP, D))
        slot_rows = [dram("slot_rows0", (NS, WD))] + [dram(f"slot_rows{l}", (NS, D)) for l in (1, 2)]
        msg_rows = dram("msg_rows", (EP, D))
        node_table = dram("node_table", (N, 1))
        edge_rec = dram("edge_rec", (E, 4), I32)
        key_line = dram("key_line", (NS + 1,))

        agg = sb("agg", [P, TE * D])
        aggv = agg[:, :].rearrange("p (t d) -> p t d", d=D)
        rel_w = sb("rel_w", [D, L * R * D])
        ident = sb("ident", [P, P])
        before = sb("before", [P, P])
        ones = sb("ones", [P, P])
        pick3 = sb("pick3", [P, P], BF16)
        fold = sb("fold", [P, D])
        bins = sb("bins", [P, R])
        tile_no = sb("tile_no", [HALF, 2])
        slot_no = sb("slot_no", [HALF, 2 * P])
        edge1 = sb("edge1", [P, TE])
        zeros = sb("zeros", [P, N // PE_FULL])
        const = sb("const", [P, 2])
        eps1 = sb("eps1", [P, 1])

        w1 = sb("w1", [P, P])
        w2 = sb("w2", [P, P])
        w2n = sb("w2n", [P, P])
        root = [sb(f"root{l}", [P, P]) for l in range(L)]
        b1c = sb("b1c", [P, 1])
        rootb = [sb(f"rootb{l}", [P, 1]) for l in range(L)]
        row_v = sb("row_v", [P, 6, D])
        bias3 = [sb(f"bias3_{k}", [P, W], BF16) for k in range(L + 1)]
        split = sb("split", [P, 3, D])
        split_b = sb("split_b", [P, 3, D], BF16)

        srci = sb("srci", [P, TE], I32)
        dsti = sb("dsti", [P, TE], I32)
        reli = sb("reli", [P, TE], I32)
        dprev = sb("dprev", [P, TE], I32)
        dnext = sb("dnext", [P, TE], I32)
        dclamp = sb("dclamp", [P, TE], I32)
        last_i = sb("last_i", [P, TE], I32)
        addr_i = sb("addr_i", [P, TE], I32)
        relf = sb("relf", [P, TE])
        keep = sb("keep", [P, TE])
        last = sb("last", [P, TE])
        openk = sb("openk", [P, TE])
        slotf = sb("slotf", [P, TE])
        tmpf = sb("tmpf", [P, TE])
        lo_i = sb("lo_i", [P, TE], I32)
        hi_i = sb("hi_i", [P, TE], I32)
        rec = sb("rec", [P, TE, REC])
        edge_s = rec[:, :, :].bitcast(I32)
        ring_q = sb("ring_q", [P, T, 4], I32)
        unsorted = sb("unsorted", [1, 1], I32)
        endv = sb("endv", [P, R])
        tot = sb("tot", [P, R])
        excl = sb("excl", [P, R])
        cross = sb("cross", [P, R])
        cnt_i = sb("cnt_i", [P, R], I32)
        tiles = sb("tiles", [P, R])
        tend = sb("tend", [P, R])
        off = sb("off", [P, R])
        relge = sb("relge", [HALF, R])
        relt = sb("relt", [HALF, 2])
        rel_tab = sb("rel_tab", [1, TS], I32)
        ak = sb("ak", [P, D])
        akT = sb("akT", [D, P])
        endT = sb("endT", [D, P])
        carT = sb("carT", [D, P + 1])
        carry = sb("carry", [P, D])

        xr = [sb(f"xr{u}", [P, W]) for u in range(U)]
        xT = [sb(f"xT{u}", [P, W]) for u in range(U)]
        aT = [sb(f"aT{u}", [P, W]) for u in range(U)]
        vr = [sb(f"vr{u}", [P, W]) for u in range(U)]
        orow = [sb(f"orow{u}", [P, W]) for u in range(U)]
        ybn = sb("ybn", [P, GD * 6])
        mom = sb("mom", [P, 2, D])
        sums = sb("sums", [P, 12])
        st = sb("st", [P, U * T, 6])
        lns = sb("lns", [P, 6, U * T])
        lnb = sb("lnb", [P, U * T])
        st2 = sb("st2", [P, U * T, 6])
        lns2 = sb("lns2", [P, 6, U * T])
        lnb2 = sb("lnb2", [P, U * T])
        moment_rhs = sb("moment_rhs", [P, 4, D])
        st_rhs = [moment_rhs[:, k, :] for k in range(2)]
        corr_rhs = [moment_rhs[:, 2 + k, :] for k in range(2)]
        primer = sb("primer", [1, 32])
        out_of_order = sb("out_of_order", [P, 1])
        runc = sb("runc", [HALF, 4])
        ring_s = [sb(f"ring_s{h}", [P, W]) for h in range(2)]
        ring_d = [sb(f"ring_d{h}", [P, W]) for h in range(2)]
        wide = [sb(f"wide{h}", [P, T, WD]) for h in range(2)]
        idx_a = [sb(f"idx_a{h}", [P, T], I32) for h in range(U)]
        idx_b = [sb(f"idx_b{h}", [P, T], I32) for h in range(2)]
        val = [sb(f"val{h}", [P, T]) for h in range(U)]
        inv = sb("inv", [P, TS])
        slot_rec = sb("slot_rec", [P, TS, 3])
        qidx = sb("qidx", [P, TS], I32)
        lidx = sb("lidx", [P, TS], I32)

        bank = [ctx.enter_context(nc.psum_tensor(f"bank{k}", [P, 512], F32)) for k in range(8)]

        cum = agg[:, 0:R * TE]
        hot = agg[:, R * TE:R * TE + BINS * TE]
        keyT = agg[0:HALF, 0:2 * P]
        keyP = agg[0:HALF, 2 * P:4 * P]
        runS = agg[0:HALF, 4 * P:6 * P]
        runF = agg[0:HALF, 6 * P:8 * P]
        runE = agg[0:HALF, 8 * P:10 * P]
        runX = agg[0:HALF, 10 * P:12 * P]
        line = agg[0:1, 12 * P:12 * P + 4 * (TS + 1)].rearrange("p (k t) -> p k t", k=4)
        rec_in = agg[:, 0:HALF * WD]
        acc = [vr[2], vr[3]]
        srow = [wide[h][:, :, :] for h in range(2)]
        sT = [(aT[2], aT[3]), (xT[2], xT[3])]

        def edge_rows(a, g, n=1):
            return a.rearrange("(p t) d -> p (t d)", p=P)[:, bass.ds(g * W, W)]

        def node_rows(a, g, p):
            if p != P:
                return a[GD_FULL * ROWS:N, :].rearrange("(p j) d -> p (j d)", j=T)
            return a[0:GD_FULL * ROWS, :].rearrange("(g p j) d -> g p (j d)", p=P, j=T)[bass.ds(g, 1)] \
                .rearrange("o p w -> (o p) w")

        def slot_view(l, g):
            w = WD if l == 0 else D
            return slot_rows[l].rearrange("(p t) w -> p t w", p=P)[:, bass.ds(g * T, T), :]

        per_group = {
            "x_turned": ["stats", "x1d", "x1s", "dense", "d0", "d1", "d2"],
            "x_copied": ["stats", "x1d", "x1s", "dense", "d0", "d1", "d2"],
            "hid_ready": ["stats", "x1d", "x1s", "dense"],
            "hid_relu": ["stats", "x1d", "x1s", "dense"],
            "y_ready": ["stats", "x1d", "x1s", "dense", "d0", "d1", "d2"],
            "y_counted": ["stats"],
            "x0_ready": ["x1d"],
            "v_ready": ["x1d", "x1s", "dense", "d0", "d1", "d2"],
            "v_final": ["d2"],
            "v_stats": ["x1d", "x1s", "dense", "d2"],
            "x1_ready": ["x1d", "x1s", "dense", "d0", "d1", "d2"],
            "x1_turned": ["dense"], "x1_copied": ["dense"], "r0_ready": ["dense"], "r0_relu": ["dense"],
            "r1_ready": ["dense"], "r1_relu": ["dense"], "r2_ready": ["dense"],
            "v2_ready": ["dense"], "v2_stats": ["dense"], "out_ready": ["dense"],
        }
        size = dict(stats=GD, x1s=GE, x1d=GE, dense=DENSE_ONLY, mix0=2 * GM, d0=GE, mix1=2 * GM, d1=GE, mix2=2 * GM,
                    d2=GE)

        def in_turn(stages):
            return [s for s in size if s in stages or (s.startswith("mix") and "dense" in stages)]

        def uses(stage, u):
            return per_buffer(size[stage], width(stage), u) if u < width(stage) else 0
        plan = {k: [(s, size[s]) for s in in_turn(v)] for k, v in per_group.items()}
        ln_stages = in_turn(["x1d", "x1s", "dense", "d2"])
        plan["ln_step"] = [(s, 4 * iters(size[s], width(s))) for s in ln_stages]
        plan["var_ready"] = [(s, iters(size[s], width(s))) for s in ln_stages]
        plan["std_ready"] = [(s, iters(size[s], width(s))) for s in ln_stages]
        for k, c in (("ln2_step", 4), ("var2_ready", 1), ("std2_ready", 1)):
            plan[k] = [(s, c * iters(size[s], width(s))) for s in in_turn(["dense"])]
        for u in range(U):
            plan[f"loaded{u}"] = [(s, 16 * uses(s, u)) for s in in_turn(per_group["x_turned"])]
            plan[f"stored{u}"] = [(s, 16 * uses(s, u)) for s in ("x1s", "x1d", "dense", "d0", "d1")]
            plan[f"x1_loaded{u}"] = [("d2", 16 * per_buffer(GE, U, u))]
            plan[f"scattered{u}"] = [("d2", 16 * T * per_buffer(GE, U, u))]
        SL = [f"s{l}" for l in range(L)]
        for k in ("s_turned", "s_copied", "msg_sums", "msg_ready", "msg_idx"):
            plan[k] = [(s, GS) for s in SL]
        for k in ("base_ready", "base_relu"):
            plan[k] = [(s, GS) for s in SL[:2]]
        for h in range(2):
            plan[f"out_stored{h}"] = [(f"mix{l}", 16 * GM) for l in range(L)]
            plan[f"slot_loaded{h}"] = [(s, 16 * per_buffer(GS, 2, h)) for s in SL]
            plan[f"fetched{h}"] = [(s, 16 * T * per_buffer(GS, 2, h)) for s in SL]
            plan[f"msg_out{h}"] = [(s, 16 * T * per_buffer(GS, 2, h)) for s in SL]
            plan[f"slot_stored{h}"] = [(s, 16 * per_buffer(GS, 2, h)) for s in SL[:2]]
        plan["slot_idx"] = [(s, GS) for s in SL]
        seg_uses = ["neigh"] + [f"m{l}" for l in range(L)]
        plan["agg_loaded"] = [(s, 16) for s in seg_uses]
        plan["scanned"] = [(s, D) for s in seg_uses]
        plan["carried"] = [(s, D) for s in seg_uses]
        plan["end_turned"] = [(s, 1) for s in seg_uses]
        plan["carry_step"] = [(s, 3) for s in seg_uses]
        plan["carry_turned"] = [(s, 1) for s in seg_uses]
        SG = Signals(sem, plan)
        S, at = SG.sem, SG.at

        def free(name, stage, i, u):
            return at(name, stage, U - width(stage) + i * width(stage) + u + 1)

        def nth(name, stage, i, u):
            return at(name, stage, i * width(stage) + u + 1)

        def nth_after_free(name, stage, i, u):
            return at(name, stage, U + i * width(stage) + u + 1)

        s_q = {k: sem("radix_" + k) for k in ("step", "counted", "summed", "placed", "copied", "scattered",
                                              "loaded", "shifted")}
        s_fill = sem("filled")
        s_idx = sem("indices_loaded")
        s_wts = sem("weights_loaded")
        s_zero = sem("scratch_zeroed")
        s_dve = sem("vector_step")
        s_pe = sem("tensor_step")
        s_rows = [sem(f"rows_gathered{h}") for h in range(2)]
        s_rst = [sem(f"gathered_stored{h}") for h in range(2)]
        s_cp = sem("index_copied")
        s_pad = sem("pool_pad")
        s_pad_pe = sem("tensor_pad")
        s_tab = [sem(f"table_written{h}") for h in range(2)]
        s_look = [sem(f"table_read{h}") for h in range(U)]
        s_lc = sem("looked_up")
        s_wl = [sem(f"wide_loaded{h}") for h in range(2)]
        s_ws = [sem(f"wide_scattered{h}") for h in range(2)]
        s_e = {k: sem("edge_" + k) for k in ("loaded", "x0", "turned", "copied", "hid", "relu", "y", "base",
                                             "diff", "acc")}
        s_rin = sem("records_loaded")
        s_key = sem("keys_moved")
        s_std = sem("y_std")
        RADIX_STEPS = 2 + 2 * RADIX // 8 + 3 + 1 + 6 + 5 * RADIX // 8 - 1 + 2
        DV = {}
        WTS = 16 * 34

        PAIR = [(0, P), (1, P)]
        GA = 2 * 16 * T

        block = ctx.enter_context(nc.Block())

        @block.vector
        def _(dve):
            steps = [0]

            def step(ins, name=None):
                steps[0] += 1
                ins.then_inc(s_dve, 1)
                dve.wait_ge(s_dve, steps[0])
                if name:
                    DV[name] = steps[0]

            tt, ts, stt, scan = dve.tensor_tensor, dve.tensor_scalar, dve.scalar_tensor_tensor, dve.tensor_tensor_scan
            dve.sem_inc(S["v_ready"], U)
            dve.sem_inc(S["v2_ready"], U)
            dve.sem_inc(S["v_final"], U)
            dve.sem_inc(S["y_counted"], U)
            dve.sem_inc(S["msg_ready"], 1)
            dve.memset(const[:, 0:1], EPS / 4)
            dve.memset(const[:, 1:2], EPS)
            dve.memset(pick3[:, :], 0.0)
            for k in range(L + 1):
                ins = dve.memset(bias3[k][:, :], 0.0)
            step(ins, "consts")
            for k in range(3):
                ins = dve.memset(pick3[32 * k:32 * k + 1, :], 1.0)
            step(ins)

            hotv = hot.rearrange("p (r t) -> p r t", t=TE)
            cumv = cum.rearrange("p (r t) -> p r t", t=TE)

            def mark(step, keyf, c, nb, n=P):
                step(tt(hotv[0:n, 0:nb], keyf[0:n, :].unsqueeze(1).to_broadcast([n, nb, TE]),
                        bins[0:n, c * nb:(c + 1) * nb].unsqueeze(2).to_broadcast([n, nb, TE]), ALU.is_equal))

            def count(step, keyf, total, nb, n=P):
                for c in range(total // nb):
                    mark(step, keyf, c, nb, n)
                    lo = c * nb * TE
                    step(scan(cum[0:n, lo:lo + nb * TE], ones[0:n, 0:1].to_broadcast([n, nb * TE]), hot[0:n, 0:nb * TE],
                              0.0 if c == 0 else cum[0:n, lo - 1:lo], ALU.mult, ALU.add))
                dve.memset(excl[0:n, 0:1], 0.0)
                step(dve.tensor_copy(endv[0:n, 0:total], cumv[0:n, 0:total, TE - 1]))
                step(dve.tensor_copy(excl[0:n, 1:total], endv[0:n, 0:total - 1]))
                step(tt(tot[0:n, 0:total], endv[0:n, 0:total], excl[0:n, 0:total], ALU.subtract))

            def place(step, keyf, total, nb, n=P):
                for c in range(total // nb):
                    mark(step, keyf, c, nb, n)
                    part = cumv[0:n, c * nb:(c + 1) * nb, :]
                    step(tt(part, part, off[0:n, c * nb:(c + 1) * nb].unsqueeze(2).to_broadcast([n, nb, TE]), ALU.add))
                    step(tt(part, part, hotv[0:n, 0:nb], ALU.mult))
                    step(dve.tensor_reduce((slotf if c == 0 else tmpf)[0:n, :], part.rearrange("p r t -> p t r"), AX.X, ALU.add))
                    if c:
                        step(tt(slotf[0:n, :], slotf[0:n, :], tmpf[0:n, :], ALU.add))

            dve.wait_ge(s_fill, 5)
            dve.wait_ge(s_idx, 16 * 7)
            step(tt(tmpf[:, :], dprev[:, :], dsti[:, :], ALU.is_gt))
            step(dve.tensor_reduce(out_of_order[:, :], tmpf[:, :], AX.X, ALU.max), "order_seen")
            dve.wait_ge(s_pe, 1)
            step(ts(unsorted[:, :], bank[0][0:1, 0:1], 1.0, None, ALU.min), "order_known")
            flag = dve.value_load(unsorted[0:1, 0:1], min_val=0, max_val=1)
            with dve.If(flag > 0):
                n = PE_FULL
                dve.tensor_copy(edge_s[0:n, :, 0], srci[0:n, :])
                dve.tensor_copy(edge_s[0:n, :, 1], dsti[0:n, :])
                dve.tensor_copy(edge_s[0:n, :, 2], reli[0:n, :])
                dve.tensor_copy(edge_s[0:n, :, 3], dsti[0:n, :]).then_inc(s_q["step"], 1)
                dve.wait_ge(s_q["step"], 1)
                with dve.Fori(0, PASSES) as k:
                    done = [0]

                    def link(ins):
                        done[0] += 1
                        ins.then_inc(s_q["step"], 1)
                        dve.wait_ge(s_q["step"], k * RADIX_STEPS + done[0] + 1)
                    link(ts(lo_i[0:n, :], edge_s[0:n, :, 3], RADIX - 1, None, ALU.bitwise_and))
                    link(dve.tensor_copy(relf[0:n, :], lo_i[0:n, :]))
                    count(link, relf, RADIX, 8, n)
                    link(dve.memset(slotf[0:1, 0:1], 0.0))
                    dve.sem_inc(s_q["counted"], 1)
                    dve.wait_ge(s_q["summed"], k + 1)
                    link(dve.tensor_copy(tiles[0:n, 0:RADIX], bank[0][0:n, RADIX:2 * RADIX]))
                    link(dve.tensor_copy(cross[0:n, 0:RADIX], bank[0][0:n, 0:RADIX]))
                    link(scan(tend[0:n, 0:RADIX], ones[0:n, 0:RADIX], tiles[0:n, 0:RADIX], 0.0, ALU.mult, ALU.add))
                    link(tt(off[0:n, 0:RADIX], tend[0:n, 0:RADIX], tiles[0:n, 0:RADIX], ALU.subtract))
                    link(tt(off[0:n, 0:RADIX], off[0:n, 0:RADIX], cross[0:n, 0:RADIX], ALU.add))
                    link(stt(off[0:n, 0:RADIX], off[0:n, 0:RADIX], -1.0, excl[0:n, 0:RADIX], ALU.add, ALU.subtract))
                    place(link, relf, RADIX, 8, n)
                    link(dve.tensor_copy(hi_i[0:n, :], slotf[0:n, :]))
                    link(ts(edge_s[0:n, :, 3], edge_s[0:n, :, 3], DIGIT, None, ALU.logical_shift_right))
                    dve.sem_inc(s_q["placed"], 1)
                    dve.wait_ge(s_q["loaded"], 16 * (k + 1))
                    assert done[0] == RADIX_STEPS
                dve.tensor_copy(srci[0:n, :], edge_s[0:n, :, 0])
                dve.tensor_copy(dsti[0:n, :], edge_s[0:n, :, 1])
                dve.tensor_copy(reli[0:n, :], edge_s[0:n, :, 2]).then_inc(s_q["step"], 1)
                dve.wait_ge(s_q["step"], PASSES * RADIX_STEPS + 2)
                dve.wait_ge(s_q["shifted"], 16 * 4)

            ts(dclamp[:, :], dsti[:, :], float(N - 1), None, ALU.min)
            tt(keep[:, :], dsti[:, :], dprev[:, :], ALU.is_equal)
            tt(last[:, :], dsti[:, :], dnext[:, :], ALU.not_equal)
            dve.tensor_copy(relf[:, :], reli[:, :])
            step(dve.memset(rec[:, :, :], 0.0), "dst_clamped")
            scan(openk[:, :], keep[:, :], keep[:, :], 1.0, ALU.min, ALU.min)
            step(stt(tmpf[:, :], last[:, :], -float(BIG), dsti[:, :], ALU.mult, ALU.add))
            step(ts(last_i[:, :], tmpf[:, :], float(BIG), None, ALU.add))
            step(ts(tmpf[:, :], dsti[:, :], 1.0, float(R), ALU.add, ALU.mult))
            tt(rec[:, :, 2], tmpf[:, :], relf[:, :], ALU.add)
            dve.tensor_copy(rec[:, :, 0], edge1[:, :])
            step(dve.tensor_copy(ak[:, :], openk[:, TE - 1:TE].to_broadcast([P, D])))

            count(step, relf, R, BINS)
            DV["counted"] = steps[0]
            dve.wait_ge(s_pe, 2)
            ts(cnt_i[:, :], bank[0][:, R:2 * R], float(P - 1), None, ALU.add)
            step(dve.tensor_copy(cross[:, :], bank[0][:, 0:R]))
            step(ts(cnt_i[:, :], cnt_i[:, :], 7, None, ALU.logical_shift_right))
            step(dve.tensor_copy(tiles[:, :], cnt_i[:, :]))
            step(scan(tend[:, :], ones[:, 0:R], tiles[:, :], 0.0, ALU.mult, ALU.add))
            step(tt(off[:, :], tend[:, :], tiles[:, :], ALU.subtract))
            step(stt(off[:, :], off[:, :], float(P), cross[:, :], ALU.mult, ALU.add))
            step(stt(off[:, :], off[:, :], -1.0, excl[:, :], ALU.add, ALU.subtract))
            for h in range(2):
                step(ts(relge[:, :], tend[0:HALF, :], tile_no[:, h:h + 1], None, ALU.is_le))
                step(dve.tensor_reduce(relt[:, h:h + 1], relge[:, :], AX.X, ALU.add))
            step(ts(relt[:, :], relt[:, :], float(R - 1), None, ALU.min), "tile_rel")
            place(step, relf, R, BINS)
            step(ts(tmpf[:, :], relf[:, :], float(R), float(BIG), ALU.is_ge, ALU.mult))
            step(tt(hi_i[:, :], slotf[:, :], tmpf[:, :], ALU.add))
            step(ts(lo_i[:, :], hi_i[:, :], P - 1, None, ALU.bitwise_and))
            step(ts(hi_i[:, :], hi_i[:, :], 7, None, ALU.logical_shift_right))
            step(stt(addr_i[:, :], lo_i[:, :], float(TS), hi_i[:, :], ALU.mult, ALU.add))
            dve.wait_ge(s_pe, 4)
            dve.tensor_copy(akT[:, :], bank[2][0:D, 0:P])
            dve.memset(carT[:, 0:1], 0.0)
            step(dve.tensor_copy(rel_tab[:, :], bank[1][0:1, 0:TS]), "sorted")

            def norm_bias(k, row):
                step(dve.tensor_copy(split_b[:, 0, :], row))
                step(tt(split[:, 0, :], row, split_b[:, 0, :], ALU.subtract))
                step(dve.tensor_copy(split_b[:, 1, :], split[:, 0, :]))
                step(tt(split[:, 1, :], split[:, 0, :], split_b[:, 1, :], ALU.subtract))
                step(dve.tensor_copy(split_b[:, 2, :], split[:, 1, :]))
                for r in range(3):
                    q = slice(32 * r, 32 * r + 1)
                    ins = dve.tensor_copy(bias3[k][q, :].rearrange("p (t d) -> p t d", d=D),
                                          split_b[q, r, :].unsqueeze(1).to_broadcast([1, T, D]))
                step(ins)
            dve.wait_ge(s_wts, WTS)
            for k in range(L):
                norm_bias(1 + k, row_v[:, 3 + k, :])
            step(ts(eps1[:, :], eps1[:, :], 1.0, None, ALU.add), "eps")

            def stats(i, us):
                for u, p in us:
                    dve.wait_ge(S["x_turned"], at("x_turned", "stats", U + i * U + u + 1))
                    dve.tensor_copy(xT[u][:, 0:4 * p], bank[2 * u][:, 0:4 * p]).then_inc(S["x_copied"], 1)
                for u, p in us:
                    dve.wait_ge(S["y_ready"], at("y_ready", "stats", i * U + u + 1))
                    dve.bn_stats(ybn[:, bass.ds((i * U + u) * 6, 6)], bank[2 * u][:, 0:4 * p]).then_inc(S["y_counted"], 1)
            rounds(dve, GD, U, stats, last=REST)
            dve.wait_ge(S["y_counted"], at("y_counted", "stats", GD + U))

            def segment_sum(use):
                dve.wait_ge(S["agg_loaded"], at("agg_loaded", use, 16))
                with dve.Fori(0, D // 4) as i:
                    for k in range(4):
                        col = aggv[:, :, bass.ds(i * 4 + k, 1)].rearrange("p t o -> p (t o)")
                        scan(col, keep[:, :], col, 0.0, ALU.mult, ALU.add).then_inc(S["scanned"], 1)
                dve.wait_ge(S["end_turned"], at("end_turned", use, 1))
                dve.tensor_copy(endT[:, :], bank[4][0:D, 0:P]).then_inc(S["carry_step"], 1)
                dve.wait_ge(S["carry_step"], at("carry_step", use, 1))
                scan(carT[:, 1:P + 1], akT[:, :], endT[:, :], 0.0, ALU.mult, ALU.add).then_inc(S["carry_step"], 1)
                dve.wait_ge(S["carry_turned"], at("carry_turned", use, 1))
                dve.tensor_copy(carry[:, :], bank[5][:, 0:D]).then_inc(S["carry_step"], 1)
                dve.wait_ge(S["carry_step"], at("carry_step", use, 3))
                dve.wait_ge(S["scanned"], at("scanned", use, D))
                with dve.Fori(0, D // 4) as i:
                    for k in range(4):
                        col = aggv[:, :, bass.ds(i * 4 + k, 1)].rearrange("p t o -> p (t o)")
                        stt(col, openk[:, :], carry[:, bass.ds(i * 4 + k, 1)], col, ALU.mult, ALU.add).then_inc(S["carried"], 1)
                dve.wait_ge(S["carried"], at("carried", use, D))
            segment_sum("neigh")

            def agg_group(g):
                return agg[:, bass.ds(g * W, W)]

            dve.memset(acc[0][:, :], 0.0)
            step(dve.memset(acc[1][:, :], 0.0))
            dve.sem_inc(s_e["acc"], 1)
            with dve.Fori(0, GE) as g:
                dve.wait_ge(s_e["loaded"], 16 * (g + 1))
                dve.wait_ge(s_e["turned"], g + 1)
                stt(xr[1][:, :], xr[0][:, :], eps1[:, 0:1], agg_group(g), ALU.mult, ALU.add).then_inc(s_e["x0"], 1)
                dve.wait_ge(s_e["turned"], g + 2)
                dve.tensor_copy(xT[0][:, :], bank[0][:, :])
                dve.tensor_copy(xT[1][:, :], bank[2][:, :]).then_inc(s_e["copied"], 1)
                dve.wait_ge(s_e["base"], g + 1)
                dve.wait_ge(s_e["acc"], 2 * g + 1)
                tt(orow[1][:, :], bank[2][:, :], orow[0][:, :], ALU.subtract)
                tt(orow[2][:, :], bank[2][:, :], orow[0][:, :], ALU.add).then_inc(s_e["diff"], 1)
                dve.wait_ge(s_e["diff"], 2 * g + 1)
                tt(orow[1][:, :].rearrange("p (t d) -> p t d", d=D), orow[1][:, :].rearrange("p (t d) -> p t d", d=D),
                   last[:, bass.ds(g * T, T)].unsqueeze(2).to_broadcast([P, T, D]), ALU.mult).then_inc(s_e["diff"], 1)
                dve.wait_ge(s_e["diff"], 2 * g + 2)
                tt(acc[0][:, :], acc[0][:, :], orow[1][:, :], ALU.add)
                tt(orow[2][:, :], orow[2][:, :], orow[1][:, :], ALU.mult).then_inc(s_e["acc"], 1)
                dve.wait_ge(s_e["acc"], 2 * g + 2)
                tt(acc[1][:, :], acc[1][:, :], orow[2][:, :], ALU.add).then_inc(s_e["acc"], 1)
            dve.wait_ge(s_e["acc"], 2 * GE + 1)

            for k in range(2):
                ins = dve.tensor_reduce(corr_rhs[k], acc[k][:, :].rearrange("p (t d) -> p d t", d=D), AX.X, ALU.add)
            step(dve.bn_aggr(sums[:, 0:2], ybn[:, :]))
            step(tt(sums[:, 2:3], sums[:, 0:1], sums[:, 0:1], ALU.mult))
            step(tt(sums[:, 3:4], sums[:, 1:2], sums[:, 2:3], ALU.add))
            for k in range(2):
                ins = ts(st_rhs[k], fold[:, :], sums[:, (0, 3)[k]:(0, 3)[k] + 1], float(N // 2), ALU.mult, ALU.mult)
            step(ins, "moments")
            dve.wait_ge(s_pe, 5)
            ts(mom[:, 0, :], bank[4][:, 0:D], 1.0 / N, None, ALU.mult)
            step(ts(mom[:, 1, :], bank[4][:, D:2 * D], 1.0 / N, None, ALU.mult))
            step(tt(split[:, 0, :], mom[:, 0, :], mom[:, 0, :], ALU.mult))
            step(tt(mom[:, 1, :], mom[:, 1, :], split[:, 0, :], ALU.subtract), "y_var")
            dve.wait_ge(s_std, 1)
            step(dve.reciprocal(mom[:, 1, :], mom[:, 1, :]))
            step(tt(mom[:, 1, :], mom[:, 1, :], row_v[:, 1, :], ALU.mult))
            step(tt(mom[:, 0, :], mom[:, 0, :], row_v[:, 0, :], ALU.add))
            step(tt(mom[:, 0, :], row_v[:, 0, :], mom[:, 0, :], ALU.subtract))
            step(tt(mom[:, 0, :], mom[:, 0, :], mom[:, 1, :], ALU.mult))
            step(tt(mom[:, 0, :], mom[:, 0, :], row_v[:, 2, :], ALU.add))
            step(ts(mom[:, 0, :], mom[:, 0, :], 0.5, None, ALU.mult))
            norm_bias(0, mom[:, 0, :])
            for h in range(2):
                q = slice(h * D, (h + 1) * D)
                ins = stt(w2n[:, q], w2[:, q], 0.5, mom[:, 1, :], ALU.mult, ALU.mult)
            step(ins, "w2n")

            def layer_norm(stage, i, us, buf, stats_, small, nb, names):
                seen, inner, var, std, final = names
                n = T * len(us)
                for u, p in us:
                    for j in range(T):
                        ins = dve.bn_stats(stats_[0:p, u * T + j, :], buf[u][0:p, j * D:(j + 1) * D])
                    ins.then_inc(S[seen], 1)
                c = lambda k: at(inner, stage, i * 4 + k)
                dve.wait_ge(S[seen], nth(seen, stage, i, len(us) - 1))
                me, m2e, mo, m2o = (stats_[:, 0:n, k] for k in (1, 2, 4, 5))
                tt(small[:, 0, 0:n], me, mo, ALU.add)
                tt(small[:, 1, 0:n], me, mo, ALU.subtract)
                tt(small[:, 2, 0:n], m2e, m2o, ALU.add).then_inc(S[inner], 1)
                dve.wait_ge(S[inner], c(1))
                stt(small[:, 1, 0:n], small[:, 1, 0:n], D / 4.0, small[:, 1, 0:n], ALU.mult, ALU.mult).then_inc(S[inner], 1)
                dve.wait_ge(S[inner], c(2))
                tt(small[:, 3, 0:n], small[:, 1, 0:n], small[:, 2, 0:n], ALU.add).then_inc(S[var], 1)
                dve.wait_ge(S[std], at(std, stage, i + 1))
                dve.reciprocal(small[:, 5, 0:n], small[:, 4, 0:n]).then_inc(S[inner], 1)
                dve.wait_ge(S[inner], c(3))
                stt(nb[:, 0:n], small[:, 0, 0:n], -0.5, small[:, 5, 0:n], ALU.mult, ALU.mult).then_inc(S[inner], 1)
                dve.wait_ge(S[inner], c(4))
                for u, p in us:
                    for j in range(T):
                        k = u * T + j
                        ins = ts(buf[u][0:p, j * D:(j + 1) * D], buf[u][0:p, j * D:(j + 1) * D], small[0:p, 5, k:k + 1],
                                 nb[0:p, k:k + 1], ALU.mult, ALU.add)
                    ins.then_inc(S[final], 1)
            LN1 = ("v_stats", "ln_step", "var_ready", "std_ready", "x1_ready")
            LN2 = ("v2_stats", "ln2_step", "var2_ready", "std2_ready", "out_ready")

            def sum_x(stage, i, us):
                for u, p in us:
                    if stage in FIRST:
                        dve.wait_ge(S["v2_ready"], free("v2_ready", stage, i, u))
                    else:
                        dve.wait_ge(S[f"stored{u}"], at(f"stored{u}", stage, 16 * (i + 1)))
                    dve.wait_ge(S["y_ready"], nth("y_ready", stage, i, u))
                    stt(vr[u][0:p, :], bank[2 * u][0:p, :], 0.0, xr[u][0:p, :], ALU.max, ALU.add).then_inc(S["v_ready"], 1)
                dve.wait_ge(S["v_ready"], nth_after_free("v_ready", stage, i, len(us) - 1))

            def x1s(i, us):
                sum_x("x1s", i, us)
                layer_norm("x1s", i, us, vr, st, lns, lnb, LN1)
            rounds(dve, GE, U, x1s)

            def x1d(i, us):
                for u, p in us:
                    g = i * U + u
                    dve.wait_ge(S["x_turned"], at("x_turned", "x1d", g + 1))
                    dve.wait_ge(S[f"loaded{u}"], at(f"loaded{u}", "x1d", 16 * (i + 1)))
                    stt(orow[u][:, :], xr[u][:, :], eps1[:, 0:1], agg_group(g), ALU.mult, ALU.add).then_inc(S["x0_ready"], 1)
                sum_x("x1d", i, us)
                layer_norm("x1d", i, us, vr, st, lns, lnb, LN1)
            rounds(dve, GE, U, x1d)
            for u in range(U):
                dve.wait_ge(S[f"stored{u}"], at(f"stored{u}", "x1d", 16 + 16 * uses("x1d", u)))

            def dense_x1(stage, i, us):
                sum_x(stage, i, us)
                layer_norm(stage, i, us, vr, st, lns, lnb, LN1)

            def dense_out(stage, i, us):
                for u, p in us:
                    sm = f"stored{u}" if stage == "dense" else f"out_stored{u}"
                    dve.wait_ge(S["r2_ready"], nth("r2_ready", stage, i, u))
                    dve.wait_ge(S[sm], at(sm, stage, 16 * (i + 1)))
                    dve.wait_ge(S["x1_ready"], nth("x1_ready", stage, i, u))
                    tt(orow[u][0:p, :], bank[2 * u][0:p, :], vr[u][0:p, :], ALU.add).then_inc(S["v2_ready"], 1)
                dve.wait_ge(S["v2_ready"], nth_after_free("v2_ready", stage, i, len(us) - 1))
                layer_norm(stage, i, us, orow, st2, lns2, lnb2, LN2)

            def dense(i, us):
                dense_x1("dense", i, us)
                dense_out("dense", i, us)
            rounds(dve, DENSE_ONLY, U, dense, last=REST)

            riv = rec_in.rearrange("p (t w) -> p t w", w=WD)
            for h in range(2):
                dve.wait_ge(s_rin, 16 * (h + 1))
                step(dve.tensor_copy(slot_rec[:, h * HALF:(h + 1) * HALF, :], riv[:, :, D:D + 3]),
                     ("half_read", "rec_ready")[h])
            for out_i, k in ((qidx, 0), (lidx, 1)):
                step(ts(inv[:, :], slot_rec[:, :, k], 0.0, float(BIG), ALU.is_equal, ALU.mult))
                step(stt(out_i[:, :], slot_rec[:, :, k], -1.0, inv[:, :], ALU.add, ALU.add))
            dve.wait_ge(s_pe, 6)
            step(dve.tensor_copy(keyT, bank[0][0:HALF, 0:2 * P]), "key_turned")
            dve.wait_ge(s_key, 32)
            step(tt(runF, keyT, keyP, ALU.not_equal))
            tt(runS, runF, slot_no[:, :], ALU.mult)
            step(ts(runX, slot_no[:, :], -float(BIG), None, ALU.add))
            step(tt(runX, runX, runF, ALU.mult))
            step(ts(runE, runX, float(BIG), None, ALU.add))
            for h in range(2):
                q = slice(h * P, (h + 1) * P)
                scan(runS[:, q], runS[:, q], runS[:, q], 0.0, ALU.max, ALU.max)
                e = runE[:, q][:, ::-1]
                ins = scan(e, e, e, float(BIG), ALU.min, ALU.min)
            step(ins, "run_ends")
            dve.wait_ge(s_pe, 7)
            dve.tensor_copy(line[:, 0, 0:TS], bank[1][0:1, 0:TS])
            dve.tensor_copy(line[:, 1, 0:TS], bank[2][0:1, 0:TS])
            dve.memset(line[:, 2, 0:1], 0.0)
            step(dve.memset(line[:, 3, TS:TS + 1], float(BIG)))
            scan(line[:, 2, 1:TS + 1], line[:, 0, 0:TS], line[:, 0, 0:TS], 0.0, ALU.max, ALU.max)
            step(scan(line[:, 3, 0:TS][:, ::-1], line[:, 1, 0:TS][:, ::-1], line[:, 1, 0:TS][:, ::-1], float(BIG),
                      ALU.min, ALU.min), "run_carry")
            dve.wait_ge(s_pe, 8)
            step(dve.tensor_copy(runc[:, :], bank[3][0:HALF, 0:4]))
            for h in range(2):
                q = slice(h * P, (h + 1) * P)
                ts(runS[:, q], runS[:, q], runc[:, h:h + 1], None, ALU.max)
                ts(runX[:, h * P:(h + 1) * P - 1], runE[:, h * P + 1:(h + 1) * P], runc[:, 2 + h:3 + h], None, ALU.min)
                ins = dve.tensor_copy(runX[:, (h + 1) * P - 1:(h + 1) * P], runc[:, 2 + h:3 + h])
            step(ins)
            step(tt(runX, runX, runS, ALU.subtract))
            step(dve.reciprocal(runX, runX), "run_inv")
            dve.wait_ge(s_pe, 9)
            step(dve.tensor_copy(inv[:, :], bank[4][:, 0:TS]), "slots_ready")

            for l in range(L):
                stage = SL[l]

                def mean(i, h, stage=stage):
                    g = i * 2 + h
                    dve.wait_ge(S["msg_sums"], at("msg_sums", stage, g + 1))
                    dve.wait_ge(S[f"msg_out{h}"], at(f"msg_out{h}", stage, 16 + 16 * T * i))
                    tt(ring_d[h][:, :].rearrange("p (t d) -> p t d", d=D),
                       bank[6][:, :].rearrange("p (t d) -> p t d", d=D),
                       inv[:, bass.ds(g * T, T)].unsqueeze(2).to_broadcast([P, T, D]), ALU.mult).then_inc(S["msg_ready"], 1)
                for u in range(2):
                    prev = f"d{l - 1}" if l else "dense"
                    dve.wait_ge(S[f"stored{u}"], at(f"stored{u}", prev, 16 + 16 * uses(prev, u)))
                with dve.Fori(0, GM) as i:
                    mean(i, 0)
                    dense_x1(f"mix{l}", i, PAIR)
                    mean(i, 1)
                    dense_out(f"mix{l}", i, PAIR)
                mean(GM, 0)
                segment_sum(f"m{l}")
                stage = f"d{l}"

                def dst_stage(i, us, l=l, stage=stage):
                    free = "scattered" if l == L - 1 else "stored"
                    for u, p in us:
                        dve.wait_ge(S[f"{free}{u}"], at(f"{free}{u}", stage, 16 + (16 * T if l == L - 1 else 16) * i))
                        dve.wait_ge(S["y_ready"], at("y_ready", stage, i * U + u + 1))
                        tt(vr[u][:, :], bank[2 * u + 1][:, :], agg_group(i * U + u), ALU.add).then_inc(S["v_ready"], 1)
                    if l == L - 1:
                        for u, p in us:
                            dve.wait_ge(S["v_ready"], at("v_ready", stage, U + i * U + u + 1))
                            dve.wait_ge(S[f"x1_loaded{u}"], at(f"x1_loaded{u}", stage, 16 * (i + 1)))
                            tt(vr[u][:, :], vr[u][:, :], aT[u][:, :], ALU.add).then_inc(S["v_final"], 1)
                        dve.wait_ge(S["v_final"], at("v_final", stage, U + i * U + len(us)))
                        layer_norm(stage, i, us, vr, st, lns, lnb, LN1)
                rounds(dve, GE, U, dst_stage)

        @block.sync
        def _(sp):
            for k, sm in enumerate(s_rst + [S[f"out_stored{h}"] for h in range(2)]):
                sp.dma_start(primer[:, 24 + k:25 + k], eps.rearrange("(p o) -> p o", p=1)).then_inc(sm, 16)
            sp.wait_ge(s_fill, 1)
            v2 = lambda a, n: a[0:n * TE].rearrange("(p t) -> p t", t=TE)
            sp.dma_start(srci[0:PE_FULL, :], v2(src, PE_FULL)).then_inc(s_idx, 16)
            sp.dma_start(dsti[0:PE_FULL, :], v2(dst, PE_FULL)).then_inc(s_idx, 16)
            sp.dma_start(reli[0:PE_FULL, :], v2(etype, PE_FULL)).then_inc(s_idx, 16)
            sp.dma_start(dprev[1:PE_FULL, :], dst[TE - 1:E - 1].rearrange("(p t) -> p t", t=TE)).then_inc(s_idx, 16)
            sp.dma_start(dprev[0:1, 1:TE], dst[0:TE - 1].rearrange("(p t) -> p t", p=1)).then_inc(s_idx, 16)
            sp.dma_start(dnext[0:PE_FULL - 1, :], dst[1:E - TE + 1].rearrange("(p t) -> p t", t=TE)).then_inc(s_idx, 16)
            sp.dma_start(dnext[PE_FULL - 1:PE_FULL, 0:TE - 1],
                         dst[E - TE + 1:E].rearrange("(p t) -> p t", p=1)).then_inc(s_idx, 16)
            sp.wait_ge(s_dve, DV["order_known"])
            flag = sp.value_load(unsorted[0:1, 0:1], min_val=0, max_val=1)
            with sp.If(flag > 0):
                with sp.Fori(0, PASSES) as k:
                    sp.wait_ge(s_q["scattered"], 16 * TE * (k + 1))
                    sp.dma_start(edge_s[0:PE_FULL, :, :], edge_rec.rearrange("(p t) w -> p t w", t=TE)).then_inc(s_q["loaded"], 16)
                sp.wait_ge(s_q["loaded"], 16 * PASSES)
                ds_ = edge_rec[:, 1:2]
                with nc.allow_non_contiguous_dma(reason="one word of every edge record"):
                    sp.dma_start(dprev[1:PE_FULL, :], ds_[TE - 1:E - 1, :].rearrange("(p t) o -> p (t o)", t=TE)).then_inc(s_q["shifted"], 16)
                    sp.dma_start(dprev[0:1, 1:TE], ds_[0:TE - 1, :].rearrange("(p t) o -> p (t o)", p=1)).then_inc(s_q["shifted"], 16)
                    sp.dma_start(dnext[0:PE_FULL - 1, :], ds_[1:E - TE + 1, :].rearrange("(p t) o -> p (t o)", t=TE)).then_inc(s_q["shifted"], 16)
                    sp.dma_start(dnext[PE_FULL - 1:PE_FULL, 0:TE - 1],
                                 ds_[E - TE + 1:E, :].rearrange("(p t) o -> p (t o)", p=1)).then_inc(s_q["shifted"], 16)
            for h in range(2):
                q = slice(h * D, (h + 1) * D)
                for tile, w in ((w1, W1), (w2, W2), (root[0], w0_root), (root[1], w1_root), (root[2], w2_root)):
                    sp.dma_start(tile[q, q], w[:, :]).then_inc(s_wts, 16)
                for tile, b in ((b1c, b1), (rootb[0], b0), (rootb[1], c1), (rootb[2], c2)):
                    sp.dma_start(tile[q, :], b.rearrange("(d o) -> d o", o=1)).then_inc(s_wts, 16)
            for k, b in enumerate((b2, gamma, beta, b0, c1, c2)):
                sp.dma_start(row_v[:, k, :], b.partition_broadcast(P)).then_inc(s_wts, 16)
            sp.dma_start(eps1[:, :], eps.partition_broadcast(P)).then_inc(s_wts, 16)
            wv = rel_w[:, :].rearrange("d (l r o) -> d l r o", l=L, r=R)
            nb = w0_rel.shape[1]
            db = D // nb
            for l, w in ((0, w0_rel), (1, w1_rel)):
                for b in range(nb):
                    q = slice(b * db, (b + 1) * db)
                    sp.dma_start(wv[q, l, :, q], w[:, b].rearrange("r d o -> d r o")).then_inc(s_wts, 16)
            sp.dma_start(wv[:, 2], w2_rel.rearrange("r d o -> d r o")).then_inc(s_wts, 16)

            def load_nodes(stage, i, us):
                for u, p in us:
                    name = "x_turned" if stage == "stats" else "v_ready"
                    sp.wait_ge(S[name], free(name, stage, i, u))
                    sp.dma_start(xr[u][0:p, :], node_rows(x, FIRST[stage] + i * width(stage) + u, p)).then_inc(S[f"loaded{u}"], 16)

            def store_gathered(i, h):
                sp.wait_ge(s_rows[h], GA * (i + 1))
                g = i * 2 + h
                sp.dma_start(edge_rows(src_x, g), ring_s[h][:, :]).then_inc(s_rst[h], 16)
                sp.dma_start(edge_rows(dst_x, g), ring_d[h][:, :]).then_inc(s_rst[h], 16)

            with sp.Fori(0, GE // 2) as i:
                for h in range(2):
                    load_nodes("stats", i * 2 + h, [(u, P) for u in range(U)])
                    store_gathered(i, h)
            load_nodes("stats", GD // U, [(0, P), (1, REST)])
            store_gathered(GE // 2, 0)

            sp.wait_ge(s_fill, 2)
            sp.dma_start(node_table.rearrange("(p t) o -> p (t o)", p=PE_FULL), zeros[0:PE_FULL, :]).then_inc(s_zero, 16)
            sp.dma_start(msg_rows[E:EP, :].rearrange("(p t) d -> p (t d)", p=120),
                         zeros[0:120, 0:(EP - E) * D // 120]).then_inc(s_zero, 16)
            sp.dma_start(key_line[0:1].rearrange("(p o) -> p o", p=1), zeros[0:1, 0:1]).then_inc(s_zero, 16)
            with sp.Fori(0, GS) as g:
                sp.dma_start(slot_view(0, g), zeros[:, 0:T * WD].rearrange("p (t w) -> p t w", t=T)).then_inc(s_zero, 16)

            sp.wait_ge(s_rst[0], 16 + 32 * per_buffer(GE, 2, 0))
            sp.wait_ge(s_rst[1], 16 + 32 * per_buffer(GE, 2, 1))
            sp.wait_ge(s_dve, DV["sorted"])
            sp.dma_start(agg[:, :], src_x.rearrange("(p t) d -> p (t d)", p=P)).then_inc(S["agg_loaded"], 16)
            with sp.Fori(0, GE) as g:
                sp.wait_ge(s_e["turned"], g + 1)
                sp.dma_start(xr[0][:, :], edge_rows(dst_x, g)).then_inc(s_e["loaded"], 16)

            def load_edges(stage, rows, extra=None):
                def body(i, us):
                    for u, p in us:
                        sp.wait_ge(S["v_ready"], at("v_ready", stage, i * U + u + 1))
                        sp.dma_start(xr[u][:, :], edge_rows(rows, i * U + u)).then_inc(S[f"loaded{u}"], 16)
                        if extra is not None:
                            sp.wait_ge(S["v_final"], at("v_final", stage, i * U + u + 1))
                            sp.dma_start(aT[u][:, :], edge_rows(extra, i * U + u)).then_inc(S[f"x1_loaded{u}"], 16)
                rounds(sp, GE, U, body)

            sp.wait_ge(s_e["acc"], 2 * GE + 1)
            load_edges("x1s", src_x)
            sp.wait_ge(S["v_ready"], at("v_ready", "x1s", GE + U))
            load_edges("x1d", dst_x)
            sp.wait_ge(S["v_ready"], at("v_ready", "x1d", GE + U))
            rounds(sp, DENSE_ONLY, U, lambda i, us: load_nodes("dense", i, us), last=REST)

            for h in range(2):
                sp.wait_ge(s_ws[h], 16 + 16 * T * per_buffer(GE, 2, h))
            sv = slot_rows[0].rearrange("(p t) w -> p t w", p=P)
            sp.wait_ge(S["x0_ready"], at("x0_ready", "x1d", GE))
            for h in range(2):
                if h:
                    sp.wait_ge(s_dve, DV["half_read"])
                sp.dma_start(rec_in.rearrange("p (t w) -> p t w", w=WD), sv[:, h * HALF:(h + 1) * HALF, :]).then_inc(s_rin, 16)
            sp.wait_ge(s_dve, DV["key_turned"])
            kl = key_line[1:NS + 1].rearrange("(h t c) -> t h c", h=2, c=P)
            sp.dma_start(kl, keyT.rearrange("t (h c) -> t h c", h=2)).then_inc(s_key, 16)
            sp.wait_ge(s_key, 16)
            sp.dma_start(keyP.rearrange("t (h c) -> t h c", h=2),
                         key_line[0:NS].rearrange("(h t c) -> t h c", h=2, c=P)).then_inc(s_key, 16)

            for l in range(L):
                stage = SL[l]

                def load_slots(i, h, l=l, stage=stage):
                    sp.wait_ge(S["s_turned"], at("s_turned", stage, i * 2 + h + 1))
                    dest = srow[h] if l == 0 else srow[h][:, :, 0:D]
                    sp.dma_start(dest, slot_view(l, i * 2 + h)).then_inc(S[f"slot_loaded{h}"], 16)

                def store_out(i, mix):
                    for u, p in PAIR:
                        sp.wait_ge(S["out_ready"], nth("out_ready", mix, i, u))
                        sp.dma_start(node_rows(out, FIRST[mix] + i * 2 + u, p), orow[u][:, :]).then_inc(S[f"out_stored{u}"], 16)
                mix = f"mix{l}"
                if l:
                    for h in range(2):
                        sp.wait_ge(S[f"slot_stored{h}"], at(f"slot_stored{h}", SL[l - 1], 16 + 16 * per_buffer(GS, 2, h)))
                load_slots(0, 0)
                load_slots(0, 1)
                sp.wait_ge(S["v_ready"], at("v_ready", mix, U))
                load_nodes(mix, 0, PAIR)
                with sp.Fori(0, GM - 1) as i:
                    load_slots(i + 1, 0)
                    load_nodes(mix, i + 1, PAIR)
                    load_slots(i + 1, 1)
                    store_out(i, mix)
                load_slots(GM, 0)
                store_out(GM - 1, mix)
                for h in range(2):
                    sp.wait_ge(S[f"msg_out{h}"], at(f"msg_out{h}", stage, 16 + 16 * T * per_buffer(GS, 2, h)))
                sp.wait_ge(S["v_ready"], at("v_ready", mix, 2 * GM + U))
                sp.wait_ge(S["v2_ready"], at("v2_ready", mix, 2 * GM + U))
                if l == 0:
                    sp.wait_ge(s_dve, DV["slots_ready"])
                sp.dma_start(agg[:, :], msg_rows.rearrange("(p t) d -> p (t d)", p=P)).then_inc(S["agg_loaded"], 16)
                load_edges(f"d{l}", dst_rows[l], dst_rows[0] if l == L - 1 else None)

        @block.gpsimd
        def _(pool):
            def pad():
                pool.sem_inc(s_pad, 1)

            for w_ in (w1, w2, root[0], root[1], root[2], rel_w):
                pool.memset(w_[:, :], 0.0)
            for t_, v_ in ((srci, 0), (dsti, N), (reli, R), (dprev, -1)):
                pool.memset(t_[:, :], v_)
            pool.memset(dnext[:, :], N).then_inc(s_fill, 1)
            pool.memset(zeros[:, :], 0.0).then_inc(s_fill, 1)
            for k, sm in enumerate(s_tab + s_ws + [S[f"msg_out{h}"] for h in range(2)] + [S[f"scattered{u}"] for u in range(U)]):
                pool.dma_start(primer[:, k:k + 1], eps.rearrange("(p o) -> p o", p=1)).then_inc(sm, 16)
            pool.iota(bins[:, :], [[1, R]], base=0, channel_multiplier=0, allow_small_or_imprecise_dtypes=True)
            pool.iota(tile_no[:, :], [[HALF, 2]], base=0, channel_multiplier=1, allow_small_or_imprecise_dtypes=True)
            pool.iota(slot_no[:, :], [[HALF * P, 2], [1, P]], base=0, channel_multiplier=P,
                      allow_small_or_imprecise_dtypes=True)
            pool.iota(edge1[:, :], [[1, TE]], base=1, channel_multiplier=TE, allow_small_or_imprecise_dtypes=True)
            pool.memset(ident[:, :], 0.0)
            pool.memset(fold[:, :], 0.0)
            pool.memset(before[:, :], 1.0)
            pool.memset(ones[:, :], 1.0).then_inc(s_fill, 1)
            pool.wait_ge(s_fill, 3)
            pool.affine_select(out=ident[:, :], in_=ident[:, :], compare_op=ALU.not_equal, fill=1.0, base=0,
                               pattern=[[-1, P]], channel_multiplier=1)
            pool.affine_select(out=before[:, :], in_=before[:, :], compare_op=ALU.is_gt, fill=0.0, base=0,
                               pattern=[[1, P]], channel_multiplier=-1)
            pool.affine_select(out=fold[:, :], in_=fold[:, :], compare_op=ALU.not_equal, fill=1.0, base=0,
                               pattern=[[-1, D]], channel_multiplier=1).then_inc(s_fill, 1)
            pool.wait_ge(s_fill, 4)
            pool.affine_select(out=fold[:, :], in_=fold[:, :], compare_op=ALU.not_equal, fill=1.0, base=-D,
                               pattern=[[-1, D]], channel_multiplier=1).then_inc(s_fill, 1)

            pool.wait_ge(s_dve, DV["order_known"])
            flag = pool.value_load(unsorted[0:1, 0:1], min_val=0, max_val=1)
            with pool.If(flag > 0):
                with pool.Fori(0, PASSES) as k:
                    pool.wait_ge(s_q["placed"], k + 1)
                    pad()
                    with pool.Fori(0, GE) as g:
                        pool.tensor_copy(idx_a[0][0:PE_FULL, :], hi_i[0:PE_FULL, bass.ds(g * T, T)])
                        pool.tensor_copy(ring_q[0:PE_FULL, :, :], edge_s[0:PE_FULL, bass.ds(g * T, T), :]).then_inc(s_q["copied"], 1)
                        pool.wait_ge(s_q["copied"], k * GE + g + 1)
                        pad()
                        for j in range(T):
                            pool.indirect_dma_start(
                                out=edge_rec[:, :],
                                out_offset=bass.IndirectOffsetOnAxis(ap=idx_a[0][0:PE_FULL, j:j + 1], axis=0),
                                in_=ring_q[0:PE_FULL, j, :], in_offset=None).then_inc(s_q["scattered"], 16)
                        pool.wait_ge(s_q["scattered"], (k * GE + g + 1) * T * 16)
                        pad()

            pool.wait_ge(s_idx, 16 * 7)
            pool.wait_ge(s_dve, DV["dst_clamped"])

            def gather_x(i, us):
                for h, _ in us:
                    g = i * 2 + h
                    pool.wait_ge(s_rst[h], 16 + 32 * i)
                    pad()
                    pool.tensor_copy(idx_a[h][:, :], srci[:, bass.ds(g * T, T)])
                    pool.tensor_copy(idx_b[h][:, :], dclamp[:, bass.ds(g * T, T)]).then_inc(s_cp, 1)
                    pool.wait_ge(s_cp, g + 1)
                    pad()
                    for k in range(T):
                        for ring, idx in ((ring_s, idx_a), (ring_d, idx_b)):
                            pool.indirect_dma_start(
                                out=ring[h][:, k * D:(k + 1) * D], out_offset=None, in_=x[:, :],
                                in_offset=bass.IndirectOffsetOnAxis(ap=idx[h][:, k:k + 1], axis=0)
                            ).then_inc(s_rows[h], 16)
            rounds(pool, GE, 2, gather_x)

            pool.wait_ge(s_zero, 16 * (3 + GS))
            pool.wait_ge(s_dve, DV["sorted"])
            for h in range(2):
                pool.wait_ge(s_rows[h], GA * per_buffer(GE, 2, h))

            def write_table(i, us):
                for h, _ in us:
                    g = i * 2 + h
                    pool.wait_ge(s_tab[h], 16 + 16 * T * i)
                    pad()
                    pool.tensor_copy(idx_a[h][:, :], last_i[:, bass.ds(g * T, T)])
                    pool.tensor_copy(val[h][:, :], edge1[:, bass.ds(g * T, T)]).then_inc(s_cp, 1)
                    pool.wait_ge(s_cp, GE + g + 1)
                    pad()
                    for k in range(T):
                        pool.indirect_dma_start(
                            out=node_table[:, :], out_offset=bass.IndirectOffsetOnAxis(ap=idx_a[h][:, k:k + 1], axis=0),
                            in_=val[h][:, k:k + 1], in_offset=None, bounds_check=N - 1, oob_is_err=False
                        ).then_inc(s_tab[h], 16)
            rounds(pool, GE, 2, write_table)
            for h in range(2):
                pool.wait_ge(s_tab[h], 16 + 16 * T * per_buffer(GE, 2, h))

            def read_table(i, us):
                def fetch(u):
                    g = i * U + u
                    pool.wait_ge(s_lc, g + 1)
                    pad()
                    pool.tensor_copy(idx_a[u][:, :], srci[:, bass.ds(g * T, T)]).then_inc(s_cp, 1)
                    pool.wait_ge(s_cp, 2 * GE + g + 1)
                    pad()
                    for k in range(T):
                        pool.indirect_dma_start(
                            out=val[u][:, k:k + 1], out_offset=None, in_=node_table[:, :],
                            in_offset=bass.IndirectOffsetOnAxis(ap=idx_a[u][:, k:k + 1], axis=0)
                        ).then_inc(s_look[u], 16)

                def keep_value(u):
                    pool.wait_ge(s_look[u], 16 * T * (i + 1))
                    pad()
                    pool.tensor_copy(rec[:, bass.ds((i * U + u) * T, T), 1], val[u][:, :]).then_inc(s_lc, 1)
                ks = [u for u, _ in us]
                for u in ks:
                    fetch(u)
                    if u:
                        keep_value(u - 1)
                keep_value(ks[-1])
            pool.sem_inc(s_lc, U)
            rounds(pool, GE, U, read_table)
            pool.wait_ge(s_lc, GE + U)

            for u in range(U):
                pool.wait_ge(S[f"stored{u}"], at(f"stored{u}", "x1s", 16 + 16 * per_buffer(GE, U, u)))

            def to_slots(i, us):
                for h, _ in us:
                    g = i * 2 + h
                    pool.wait_ge(s_ws[h], 16 + 16 * T * i)
                    pad()
                    pool.dma_start(wide[h][:, :, 0:D], edge_rows(src_x1, g).rearrange("p (t d) -> p t d", d=D)).then_inc(s_wl[h], 16)
                    pool.tensor_copy(wide[h][:, :, D:WD], rec[:, bass.ds(g * T, T), :])
                    pool.tensor_copy(idx_a[h][:, :], addr_i[:, bass.ds(g * T, T)]).then_inc(s_cp, 1)
                for h, _ in us:
                    g = i * 2 + h
                    pool.wait_ge(s_cp, 3 * GE + g + 1)
                    pool.wait_ge(s_wl[h], 16 * (i + 1))
                    pad()
                    for k in range(T):
                        pool.indirect_dma_start(
                            out=slot_rows[0][:, :], out_offset=bass.IndirectOffsetOnAxis(ap=idx_a[h][:, k:k + 1], axis=0),
                            in_=wide[h][:, k, :], in_offset=None, bounds_check=NS - 1, oob_is_err=False
                        ).then_inc(s_ws[h], 16)
            rounds(pool, GE, 2, to_slots)

            for h in range(2):
                pool.wait_ge(s_ws[h], 16 + 16 * T * per_buffer(GE, 2, h))
            pool.wait_ge(s_dve, DV["slots_ready"])
            for l in range(L):
                stage = SL[l]
                if l == 0:
                    for u in range(U):
                        pool.wait_ge(S[f"stored{u}"], at(f"stored{u}", "x1d", 16 + 16 * per_buffer(GE, U, u)))
                else:
                    for u in range(U):
                        pool.wait_ge(S[f"stored{u}"], at(f"stored{u}", f"d{l - 1}", 16 + 16 * per_buffer(GE, U, u)))
                    pool.wait_ge(S["agg_loaded"], at("agg_loaded", f"m{l - 1}", 16))

                def fetch(i, h, l=l, stage=stage):
                    pool.wait_ge(S[f"slot_loaded{h}"], at(f"slot_loaded{h}", stage, 16 * (i + 1)))
                    pad()
                    pool.tensor_copy(idx_a[h][:, :], lidx[:, bass.ds((i * 2 + h) * T, T)]).then_inc(S["slot_idx"], 1)
                    pool.wait_ge(S["slot_idx"], at("slot_idx", stage, i * 2 + h + 1))
                    pad()
                    for k in range(T):
                        pool.indirect_dma_start(
                            out=wide[h][:, k, 0:D], out_offset=None, in_=dst_rows[l][:, :],
                            in_offset=bass.IndirectOffsetOnAxis(ap=idx_a[h][:, k:k + 1], axis=0),
                            bounds_check=EP - 1, oob_is_err=False).then_inc(S[f"fetched{h}"], 16)

                def send(i, h, stage=stage):
                    pool.wait_ge(S[f"msg_out{h}"], at(f"msg_out{h}", stage, 16 + 16 * T * i))
                    pad()
                    pool.tensor_copy(idx_b[h][:, :], qidx[:, bass.ds((i * 2 + h) * T, T)]).then_inc(S["msg_idx"], 1)
                    pool.wait_ge(S["msg_idx"], at("msg_idx", stage, i * 2 + h + 1))
                    pool.wait_ge(S["msg_ready"], at("msg_ready", stage, 1 + i * 2 + h + 1))
                    pad()
                    for k in range(T):
                        pool.indirect_dma_start(
                            out=msg_rows[:, :],
                            out_offset=bass.IndirectOffsetOnAxis(ap=idx_b[h][:, k:k + 1], axis=0),
                            in_=ring_d[h][:, k * D:(k + 1) * D], in_offset=None, bounds_check=EP - 1,
                            oob_is_err=False).then_inc(S[f"msg_out{h}"], 16)
                fetch(0, 0)
                fetch(0, 1)
                with pool.Fori(0, GM - 1) as i:
                    for h in range(2):
                        send(i, h)
                        fetch(i + 1, h)
                send(GM - 1, 0)
                fetch(GM, 0)
                send(GM - 1, 1)
                send(GM, 0)

            for u in range(U):
                pool.wait_ge(S[f"stored{u}"], at(f"stored{u}", "dense", 16 + 16 * uses("dense", u)))
            for u in range(2):
                pool.wait_ge(S[f"out_stored{u}"], at(f"out_stored{u}", "mix2", 16 + 16 * GM))
            for h in range(2):
                pool.wait_ge(S[f"msg_out{h}"], at(f"msg_out{h}", SL[-1], 16 + 16 * T * per_buffer(GS, 2, h)))

            def write_out(i, us):
                for u, _ in us:
                    g = i * U + u
                    pool.wait_ge(S[f"scattered{u}"], at(f"scattered{u}", "d2", 16 + 16 * T * i))
                    pad()
                    pool.tensor_copy(idx_a[u][:, :], last_i[:, bass.ds(g * T, T)]).then_inc(s_cp, 1)
                    pool.wait_ge(s_cp, 4 * GE + g + 1)
                    pool.wait_ge(S["x1_ready"], at("x1_ready", "d2", g + 1))
                    pad()
                    for k in range(T):
                        pool.indirect_dma_start(
                            out=out[:, :], out_offset=bass.IndirectOffsetOnAxis(ap=idx_a[u][:, k:k + 1], axis=0),
                            in_=vr[u][:, k * D:(k + 1) * D], in_offset=None, bounds_check=N - 1,
                            oob_is_err=False).then_inc(S[f"scattered{u}"], 16)
            rounds(pool, GE, U, write_out)
            for u in range(U):
                pool.wait_ge(S[f"scattered{u}"], at(f"scattered{u}", "d2", 16 + 16 * T * per_buffer(GE, U, u)))

        @block.scalar
        def _(act):
            for u in range(U):
                act.dma_start(primer[:, 16 + u:17 + u], eps.rearrange("(p o) -> p o", p=1)).then_inc(S[f"stored{u}"], 16)
            for h in range(2):
                act.dma_start(primer[:, 28 + h:29 + h], eps.rearrange("(p o) -> p o", p=1)).then_inc(S[f"slot_stored{h}"], 16)
            act.sem_inc(S["base_relu"], 1)
            act.wait_ge(s_wts, WTS)
            act.wait_ge(s_dve, DV["eps"])

            def relu_hidden(stage, i, us, scale):
                for u, p in us:
                    act.wait_ge(S["hid_ready"], nth("hid_ready", stage, i, u))
                    act.activation(aT[u][:, 0:4 * p], bank[2 * u + 1][:, 0:4 * p], ACT.Relu, bias=b1c[:, 0:1],
                                   scale=scale).then_inc(S["hid_relu"], 1)

            def root_std(stage, var, std, i, us, k):
                act.wait_ge(S[var], at(var, stage, i + 1))
                n = T * len(us)
                small = lns2 if var == "var2_ready" else lns
                act.activation(small[:, 4, 0:n], small[:, 3, 0:n], ACT.Sqrt, bias=const[:, k:k + 1],
                               scale=1.0 / D).then_inc(S[std], 1)

            def copy_x(stage, i, us):
                for u, p in us:
                    act.wait_ge(S["x_turned"], nth_after_free("x_turned", stage, i, u))
                    act.activation(xT[u][:, 0:4 * p], bank[2 * u][:, 0:4 * p], ACT.Copy).then_inc(S["x_copied"], 1)

            rounds(act, GD, U, lambda i, us: relu_hidden("stats", i, us, eps1[:, 0:1]), last=REST)

            with act.Fori(0, GE) as g:
                act.wait_ge(s_e["hid"], g + 1)
                act.activation(aT[0][:, :], bank[1][:, :], ACT.Relu, bias=b1c[:, 0:1], scale=eps1[:, 0:1])
                act.activation(aT[1][:, :], bank[3][:, :], ACT.Relu, bias=b1c[:, 0:1]).then_inc(s_e["relu"], 1)
                act.wait_ge(s_e["y"], g + 1)
                act.wait_ge(s_e["acc"], 2 * g + 1)
                act.activation(orow[0][:, :], bank[0][:, :], ACT.Copy).then_inc(s_e["base"], 1)

            act.wait_ge(s_dve, DV["y_var"])
            act.activation(mom[:, 1, :], mom[:, 1, :], ACT.Sqrt, bias=const[:, 1:2]).then_inc(s_std, 1)

            def x1_stage(stage, scale, dest):
                def body(i, us):
                    copy_x(stage, i, us)
                    relu_hidden(stage, i, us, scale)
                    root_std(stage, "var_ready", "std_ready", i, us, 0)
                    for u, p in us:
                        act.wait_ge(S["x1_ready"], at("x1_ready", stage, i * U + u + 1))
                        act.dma_start(edge_rows(dest, i * U + u), vr[u][:, :]).then_inc(S[f"stored{u}"], 16)
                rounds(act, GE, U, body)
            x1_stage("x1s", eps1[:, 0:1], src_x1)
            x1_stage("x1d", 1.0, dst_rows[0])

            def root_relus(stage, i, us):
                for u, p in us:
                    act.wait_ge(S["x1_turned"], nth("x1_turned", stage, i, u))
                    act.activation(xT[u][:, 0:4 * p], bank[2 * u + 1][:, 0:4 * p], ACT.Copy).then_inc(S["x1_copied"], 1)
                for u, p in us:
                    act.wait_ge(S["r0_ready"], nth("r0_ready", stage, i, u))
                    act.activation(aT[u][:, 0:4 * p], bank[2 * u][:, 0:4 * p], ACT.Relu, bias=rootb[0][:, 0:1]).then_inc(S["r0_relu"], 1)
                for u, p in us:
                    act.wait_ge(S["r1_ready"], nth("r1_ready", stage, i, u))
                    act.activation(xT[u][:, 0:4 * p], bank[2 * u + 1][:, 0:4 * p], ACT.Relu, bias=rootb[1][:, 0:1]).then_inc(S["r1_relu"], 1)

            def dense(i, us):
                copy_x("dense", i, us)
                relu_hidden("dense", i, us, eps1[:, 0:1])
                root_std("dense", "var_ready", "std_ready", i, us, 0)
                root_relus("dense", i, us)
                root_std("dense", "var2_ready", "std2_ready", i, us, 1)
                for u, p in us:
                    act.wait_ge(S["out_ready"], nth("out_ready", "dense", i, u))
                    act.dma_start(node_rows(out, FIRST["dense"] + i * U + u, p), orow[u][0:p, :]).then_inc(S[f"stored{u}"], 16)
            rounds(act, DENSE_ONLY, U, dense, last=REST)

            for l in range(L):
                stage = SL[l]

                def copy_slots(i, h, stage=stage):
                    act.wait_ge(S["s_turned"], at("s_turned", stage, 2 + i * 2 + h + 1))
                    act.activation(sT[h][0][0:D, :], bank[4][0:D, :], ACT.Copy)
                    act.activation(sT[h][1][0:D, :], bank[5][0:D, :], ACT.Copy).then_inc(S["s_copied"], 1)

                def next_rows(i, h, l=l, stage=stage):
                    if l == L - 1:
                        return
                    act.wait_ge(S["base_ready"], at("base_ready", stage, i * 2 + h + 1))
                    act.wait_ge(S[f"slot_stored{h}"], at(f"slot_stored{h}", stage, 16 * (i + 1)))
                    act.activation(ring_s[h][:, :], bank[7][:, :], ACT.Relu).then_inc(S["base_relu"], 1)
                    act.wait_ge(S["base_relu"], at("base_relu", stage, 1 + i * 2 + h + 1))
                    act.dma_start(slot_view(l + 1, i * 2 + h),
                                  ring_s[h][:, :].rearrange("p (t d) -> p t d", d=D)).then_inc(S[f"slot_stored{h}"], 16)

                def mixed(i, mix=f"mix{l}"):
                    relu_hidden(mix, i, PAIR, eps1[:, 0:1])
                    next_rows(i, 0)
                    copy_slots(i, 1)
                    root_std(mix, "var_ready", "std_ready", i, PAIR, 0)
                    next_rows(i, 1)
                    root_relus(mix, i, PAIR)
                mix = f"mix{l}"
                copy_x(mix, 0, PAIR)
                copy_slots(0, 0)
                with act.Fori(0, GM - 1) as i:
                    mixed(i)
                    copy_x(mix, i + 1, PAIR)
                    root_std(mix, "var2_ready", "std2_ready", i, PAIR, 1)
                    copy_slots(i + 1, 0)
                mixed(GM - 1)
                root_std(mix, "var2_ready", "std2_ready", GM - 1, PAIR, 1)
                copy_slots(GM, 0)
                next_rows(GM, 0)
                stage = f"d{l}"

                def dst_stage(i, us, l=l, stage=stage):
                    copy_x(stage, i, us)
                    if l == L - 1:
                        root_std(stage, "var_ready", "std_ready", i, us, 1)
                        return
                    for u, _ in us:
                        act.wait_ge(S["v_ready"], at("v_ready", stage, U + i * U + u + 1))
                        act.activation(vr[u][:, :], vr[u][:, :], ACT.Relu).then_inc(S["x1_ready"], 1)
                    for u, _ in us:
                        act.wait_ge(S["x1_ready"], at("x1_ready", stage, i * U + u + 1))
                        act.dma_start(edge_rows(dst_rows[l + 1], i * U + u), vr[u][:, :]).then_inc(S[f"stored{u}"], 16)
                rounds(act, GE, U, dst_stage)

        @block.tensor
        def _(pe):
            mm = pe.matmul
            pe.sem_inc(S["x_turned"], U)
            step = [0]

            def done(ins):
                step[0] += 1
                ins.then_inc(s_pe, 1)

            pe.wait_ge(s_fill, 5)
            pe.wait_ge(s_dve, DV["order_seen"])
            done(mm(bank[0][:, 0:1], ones[:, :], out_of_order[:, :], start=True, stop=True))
            pe.wait_ge(s_dve, DV["order_known"])
            flag = pe.value_load(unsorted[0:1, 0:1], min_val=0, max_val=1)
            with pe.If(flag > 0):
                n = PE_FULL
                with pe.Fori(0, PASSES) as k:
                    pe.wait_ge(s_q["counted"], k + 1)
                    pe.sem_inc(s_pad_pe, 1)
                    mm(bank[0][0:n, 0:RADIX], before[0:n, 0:n], tot[0:n, 0:RADIX], start=True, stop=True)
                    mm(bank[0][0:n, RADIX:2 * RADIX], ones[0:n, 0:n], tot[0:n, 0:RADIX], start=True, stop=True).then_inc(s_q["summed"], 1)
            pe.wait_ge(s_dve, DV["counted"])
            mm(bank[0][:, 0:R], before[:, :], tot[:, :], start=True, stop=True)
            done(mm(bank[0][:, R:2 * R], ones[:, :], tot[:, :], start=True, stop=True))
            pe.wait_ge(s_dve, DV["tile_rel"])
            mm(bank[1][0:1, 0:HALF], relt[:, 0:1], ident[0:HALF, 0:HALF], start=True, stop=True)
            done(mm(bank[1][0:1, HALF:TS], relt[:, 1:2], ident[0:HALF, 0:HALF], start=True, stop=True))
            done(mm(bank[2][0:D, 0:P], ak[:, :], ident[:, :], start=True, stop=True))
            pe.wait_ge(s_dve, DV["sorted"])
            pe.wait_ge(s_wts, WTS)

            def turn(dest, rows, p):
                for j in range(4):
                    ins = pe.transpose(dest[:, j * p:(j + 1) * p], rows[0:p, j * P:(j + 1) * P], ident[0:p, 0:p])
                return ins

            def turn_x(stage, i, us, rows=None):
                for u, p in us:
                    if rows is None:
                        pe.wait_ge(S[f"loaded{u}"], at(f"loaded{u}", stage, 16 * (i + 1)))
                        if stage == "stats":
                            pe.wait_ge(S["y_counted"], at("y_counted", stage, i * U + u + 1))
                        elif stage in FIRST:
                            pe.wait_ge(S["v2_ready"], free("v2_ready", stage, i, u))
                        else:
                            pe.wait_ge(S["v_ready"], at("v_ready", stage, i * U + u + 1))
                        turn(bank[2 * u], xr[u], p).then_inc(S["x_turned"], 1)
                    else:
                        pe.wait_ge(S["x0_ready"], at("x0_ready", stage, i * U + u + 1))
                        turn(bank[2 * u], rows[u], p).then_inc(S["x_turned"], 1)

            def hidden(stage, i, us):
                for u, p in us:
                    pe.wait_ge(S["x_copied"], nth("x_copied", stage, i, u))
                    mm(bank[2 * u + 1][:, 0:4 * p], w1[:, :], xT[u][:, 0:4 * p], start=True, stop=True).then_inc(S["hid_ready"], 1)

            def rows_out(dest, lhs, w, bias, p):
                if bias is not None:
                    mm(dest[0:p, :], pick3[:, 0:p], bias[:, :], start=True, stop=False, skip_group_check=True)
                for j in range(4):
                    ins = mm(dest[0:p, j * P:(j + 1) * P], lhs[:, j * p:(j + 1) * p], w[:, :], start=bias is None,
                             stop=True, skip_group_check=True)
                return ins

            def stats(i, us):
                turn_x("stats", i, us)
                hidden("stats", i, us)
                for u, p in us:
                    pe.wait_ge(S["hid_relu"], at("hid_relu", "stats", i * U + u + 1))
                    mm(bank[2 * u][:, 0:4 * p], w2[:, :], aT[u][:, 0:4 * p], start=True, stop=True).then_inc(S["y_ready"], 1)
            rounds(pe, GD, U, stats, last=REST)
            pe.wait_ge(S["y_counted"], at("y_counted", "stats", GD + U))

            def carry_turns(use):
                pe.wait_ge(S["scanned"], at("scanned", use, D))
                pe.transpose(bank[4][0:D, 0:P], agg[:, (TE - 1) * D:TE * D], ident[:, :]).then_inc(S["end_turned"], 1)
                pe.wait_ge(S["carry_step"], at("carry_step", use, 2))
                pe.transpose(bank[5][:, 0:D], carT[:, 0:P], ident[0:D, 0:D]).then_inc(S["carry_turned"], 1)
                pe.wait_ge(S["carry_step"], at("carry_step", use, 3))
            carry_turns("neigh")

            pe.sem_inc(s_e["turned"], 1)
            with pe.Fori(0, GE) as g:
                pe.wait_ge(s_e["x0"], g + 1)
                pe.wait_ge(s_e["acc"], 2 * g + 1)
                turn(bank[0], xr[0], P)
                turn(bank[2], xr[1], P).then_inc(s_e["turned"], 1)
                pe.wait_ge(s_e["copied"], g + 1)
                mm(bank[1][:, :], w1[:, :], xT[0][:, :], start=True, stop=True)
                mm(bank[3][:, :], w1[:, :], xT[1][:, :], start=True, stop=True).then_inc(s_e["hid"], 1)
                pe.wait_ge(s_e["relu"], g + 1)
                rows_out(bank[0], aT[0], w2, None, P)
                rows_out(bank[2], aT[1], w2, None, P).then_inc(s_e["y"], 1)

            pe.wait_ge(s_dve, DV["moments"])
            for k in range(2):
                mm(bank[4][:, k * D:(k + 1) * D], ones[:, :], st_rhs[k], start=True, stop=False, skip_group_check=True)
                ins = mm(bank[4][:, k * D:(k + 1) * D], ones[:, :], corr_rhs[k], start=False, stop=True, skip_group_check=True)
            done(ins)
            pe.wait_ge(s_dve, DV["w2n"])

            def x1_stage(stage, rows):
                def body(i, us):
                    turn_x(stage, i, us, rows)
                    hidden(stage, i, us)
                    for u, p in us:
                        pe.wait_ge(S["hid_relu"], at("hid_relu", stage, i * U + u + 1))
                        rows_out(bank[2 * u], aT[u], w2n, bias3[0], p).then_inc(S["y_ready"], 1)
                rounds(pe, GE, U, body)
            x1_stage("x1s", None)
            x1_stage("x1d", orow)

            def dense_y(stage, i, us):
                for u, p in us:
                    pe.wait_ge(S["hid_relu"], nth("hid_relu", stage, i, u))
                    rows_out(bank[2 * u], aT[u], w2n, bias3[0], p).then_inc(S["y_ready"], 1)

            def dense_roots(stage, i, us):
                for u, p in us:
                    pe.wait_ge(S["x1_ready"], nth("x1_ready", stage, i, u))
                    turn(bank[2 * u + 1], vr[u], p).then_inc(S["x1_turned"], 1)
                for u, p in us:
                    pe.wait_ge(S["x1_copied"], nth("x1_copied", stage, i, u))
                    mm(bank[2 * u][:, 0:4 * p], root[0][:, :], xT[u][:, 0:4 * p], start=True, stop=True).then_inc(S["r0_ready"], 1)
                for u, p in us:
                    pe.wait_ge(S["r0_relu"], nth("r0_relu", stage, i, u))
                    mm(bank[2 * u + 1][:, 0:4 * p], root[1][:, :], aT[u][:, 0:4 * p], start=True, stop=True).then_inc(S["r1_ready"], 1)
                for u, p in us:
                    pe.wait_ge(S["r1_relu"], nth("r1_relu", stage, i, u))
                    rows_out(bank[2 * u], xT[u], root[2], bias3[3], p).then_inc(S["r2_ready"], 1)

            def dense(i, us):
                turn_x("dense", i, us)
                hidden("dense", i, us)
                dense_y("dense", i, us)
                dense_roots("dense", i, us)
            rounds(pe, DENSE_ONLY, U, dense, last=REST)

            pe.wait_ge(s_dve, DV["rec_ready"])
            for h in range(2):
                ins = pe.transpose(bank[0][0:HALF, h * P:(h + 1) * P],
                                   slot_rec[:, h * HALF:(h + 1) * HALF, 2], ident[:, :])
            done(ins)
            pe.wait_ge(s_dve, DV["run_ends"])
            for h in range(2):
                mm(bank[1][0:1, h * HALF:(h + 1) * HALF], runS[:, (h + 1) * P - 1:(h + 1) * P], ident[0:HALF, 0:HALF],
                   start=True, stop=True)
                ins = mm(bank[2][0:1, h * HALF:(h + 1) * HALF], runE[:, h * P:h * P + 1], ident[0:HALF, 0:HALF],
                         start=True, stop=True)
            done(ins)
            pe.wait_ge(s_dve, DV["run_carry"])
            for h in range(2):
                mm(bank[3][0:HALF, h:h + 1], line[0:1, 2, h * HALF:(h + 1) * HALF], ones[0:1, 0:1], start=True, stop=True)
                ins = mm(bank[3][0:HALF, 2 + h:3 + h], line[0:1, 3, 1 + h * HALF:1 + (h + 1) * HALF], ones[0:1, 0:1],
                         start=True, stop=True)
            done(ins)
            pe.wait_ge(s_dve, DV["run_inv"])
            for h in range(2):
                ins = pe.transpose(bank[4][:, h * HALF:(h + 1) * HALF], runX[:, h * P:(h + 1) * P], ident[0:HALF, 0:HALF])
            done(ins)
            pe.wait_ge(s_dve, DV["slots_ready"])
            pe.sem_inc(S["s_turned"], 2)

            for l in range(L):
                stage = SL[l]

                def turn_slots(i, h, stage=stage):
                    pe.wait_ge(S[f"fetched{h}"], at(f"fetched{h}", stage, 16 * T * (i + 1)))
                    pe.sem_inc(s_pad_pe, 1)
                    for k in range(T):
                        ins = pe.transpose(bank[4 + k // 4][0:D, (k % 4) * P:(k % 4 + 1) * P], wide[h][:, k, 0:D], ident[:, :])
                    ins.then_inc(S["s_turned"], 1)

                def products(i, h, l=l, stage=stage):
                    g = i * 2 + h
                    pe.wait_ge(S["s_copied"], at("s_copied", stage, g + 1))
                    pe.wait_ge(S["msg_ready"], at("msg_ready", stage, g + 1))
                    for k in range(T):
                        r = pe.value_load(rel_tab[0:1, bass.ds(g * T + k, 1)], min_val=0, max_val=R - 1)
                        lhs = sT[h][k // 4][0:D, (k % 4) * P:(k % 4 + 1) * P]
                        ins = mm(bank[6][:, k * D:(k + 1) * D], lhs,
                                 rel_w[:, bass.ds((r + l * R) * D, D)], start=True, stop=True)
                    ins.then_inc(S["msg_sums"], 1)
                    if l < L - 1:
                        pe.wait_ge(S["base_relu"], at("base_relu", stage, g + 1))
                        mm(bank[7][:, :], pick3[:, :], bias3[1 + l][:, :], start=True, stop=False, skip_group_check=True)
                        for k in range(T):
                            lhs = sT[h][k // 4][0:D, (k % 4) * P:(k % 4 + 1) * P]
                            ins = mm(bank[7][:, k * D:(k + 1) * D], lhs, root[l][0:D, 0:D], start=False, stop=True,
                                     skip_group_check=True)
                        ins.then_inc(S["base_ready"], 1)
                mix = f"mix{l}"
                with pe.Fori(0, GM) as i:
                    turn_x(mix, i, PAIR)
                    turn_slots(i, 0)
                    hidden(mix, i, PAIR)
                    products(i, 0)
                    dense_y(mix, i, PAIR)
                    turn_slots(i, 1)
                    products(i, 1)
                    dense_roots(mix, i, PAIR)
                turn_slots(GM, 0)
                products(GM, 0)
                carry_turns(f"m{l}")
                stage = f"d{l}"

                def dst_stage(i, us, l=l, stage=stage):
                    turn_x(stage, i, us)
                    for u, p in us:
                        pe.wait_ge(S["x_copied"], at("x_copied", stage, i * U + u + 1))
                        rows_out(bank[2 * u + 1], xT[u], root[l], bias3[1 + l], p).then_inc(S["y_ready"], 1)
                rounds(pe, GE, U, dst_stage)



_INS = ['x', 'src', 'dst', 'edge_type_50', 'L0_gnn_W1', 'L0_gnn_b1', 'L0_gnn_W2', 'L0_gnn_b2', 'L0_gnn_gamma',
        'L0_gnn_beta', 'L0_gnn_eps', 'L1_gnn_w0_rel', 'L1_gnn_w0_root', 'L1_gnn_b0', 'L1_gnn_w1_rel',
        'L1_gnn_w1_root', 'L1_gnn_b1', 'L1_gnn_w2_rel', 'L1_gnn_w2_root', 'L1_gnn_b2']


def kernel(**inputs):
    import concourse.bacc as _bacc
    from concourse.bass_utils import run_bass_kernel_spmd as _run

    nc = _bacc.Bacc("TRN2", target_bir_lowering=False, num_devices=1)
    arrays, args = {}, []
    for name in _INS:
        a = np.ascontiguousarray(inputs[name])
        arrays[f"in_{name}_dram"] = a
        args.append(nc.dram_tensor(f"in_{name}_dram", a.shape, mybir.dt.from_np(a.dtype), kind="ExternalInput").ap())
    out = nc.dram_tensor("out_0_dram", (N, D), F32, kind="ExternalOutput").ap()
    build(nc, *args, out)
    r = _run(nc, [arrays], core_ids=[0])
    return r.results[0]["out_0_dram"]
```

```python
import numpy as np
import concourse.bass as bass
from concourse import mybir
from contextlib import ExitStack

F32 = mybir.dt.float32
BF16 = mybir.dt.bfloat16
I32 = mybir.dt.int32
ALU = mybir.AluOpType
ACT = mybir.ActivationFunctionType
AX = mybir.AxisListType

N, E, D, R = 100000, 25000, 64, 50
L = 3
P = 128
T = 8
TE = -(-E // (P * T)) * T
EP = P * TE
PE_FULL = E // TE
GE = TE // T
TS = -(-(E // P + R) // T) * T
NS = P * TS
GS = TS // T
ROWS = P * T
GD_FULL = N // ROWS
REST = (N - GD_FULL * ROWS) // T
GD = GD_FULL + 1
GM = GS // 2
U = 4
W = T * D
REC = 4
WD = D + REC
BIG = 1 << 23
BINS = 10
DIGIT = 5
RADIX = 1 << DIGIT
PASSES = -(-(N - 1).bit_length() // DIGIT)
HALF = TS // 2
EPS = 1e-5
SHORT = T
SORTING = 3
FASTER = 2 * SORTING
DENSE_ONLY = GD - 2 * GM * 3
FIRST = dict(stats=0, dense=2 * GM * 3, mix0=0, mix1=2 * GM, mix2=4 * GM)

assert PE_FULL * TE == E and REST * T + GD_FULL * ROWS == N and HALF <= P and GS % 2 == 1


def iters(n, u):
    return -(-n // u)


def width(stage):
    return 2 if stage.startswith("mix") else U


def norm_round(stage, i, us):
    return i * 2 + us[0][0] if stage.startswith("mix") else i


def norm_cols(us):
    return slice(us[0][0] * T, us[0][0] * T + T * len(us))


def before_half(i, h):
    return (i, 0) if h else (i - 1, 1)


def after_half(i, h):
    return (i + 1, 0) if h else (i, 1)


def per_buffer(n, u, k):
    return (n - k + u - 1) // u


class Signals:

    def __init__(self, make, plan):
        self.sem, self.base = {}, {}
        for name, uses in plan.items():
            self.sem[name] = make(name)
            done = 0
            for stage, count in uses:
                self.base[name, stage] = done
                done += count

    def at(self, name, stage, count):
        return self.base[name, stage] + count


def rounds(eng, n, u, body, last=P):
    full, rest = divmod(n, u)
    if not rest and last != P:
        full, rest = full - 1, u
    with eng.Fori(0, full) as i:
        body(i, [(k, P) for k in range(u)])
    if rest:
        body(full, [(k, P if k < rest - 1 else last) for k in range(rest)])


def build(nc, x, src, dst, etype, W1, b1, W2, b2, gamma, beta, eps, w0_rel, w0_root, b0, w1_rel,
          w1_root, c1, w2_rel, w2_root, c2, out):
    ctx = ExitStack()
    with ctx:
        def sb(name, shape, dt=F32):
            return ctx.enter_context(nc.sbuf_tensor(name, shape, dt))

        def dram(name, shape, dt=F32):
            return nc.dram_tensor(name, shape, dt, kind="Internal").ap()

        def sem(name):
            return ctx.enter_context(nc.semaphore(name))

        src_x = dram("src_x", (EP, D))
        dst_x = dram("dst_x", (EP, D))
        dst_rows = [dram(f"dst_rows{l}", (EP, D)) for l in range(L)]
        src_x1 = dram("src_x1", (EP, D))
        slot_rows = [dram("slot_rows0", (NS, WD))] + [dram(f"slot_rows{l}", (NS, D)) for l in (1, 2)]
        msg_rows = dram("msg_rows", (EP, D))
        node_table = dram("node_table", (N, 1))
        edge_rec = dram("edge_rec", (E, 4), I32)
        key_line = dram("key_line", (NS + 1,))

        agg = sb("agg", [P, TE * D])
        aggv = agg[:, :].rearrange("p (t d) -> p t d", d=D)
        rel_w = sb("rel_w", [D, L * R * D])
        ident = sb("ident", [P, P])
        before = sb("before", [P, P])
        ones = sb("ones", [P, P])
        pick3 = sb("pick3", [P, P], BF16)
        fold = sb("fold", [P, D])
        bins = sb("bins", [P, R])
        tile_no = sb("tile_no", [HALF, 2])
        slot_no = sb("slot_no", [HALF, 2 * P])
        edge1 = sb("edge1", [P, TE])
        zeros = sb("zeros", [P, N // PE_FULL])
        const = sb("const", [P, 2])
        eps1 = sb("eps1", [P, 1])

        w1 = sb("w1", [P, P])
        w2 = sb("w2", [P, P])
        w2n = sb("w2n", [P, P])
        root = [sb(f"root{l}", [P, P]) for l in range(L)]
        b1c = sb("b1c", [P, 1])
        rootb = [sb(f"rootb{l}", [P, 1]) for l in range(L)]
        row_v = sb("row_v", [P, 6, D])
        bias3 = [sb(f"bias3_{k}", [P, W], BF16) for k in range(L + 1)]
        split = sb("split", [P, 3, D])
        split_b = sb("split_b", [P, 3, D], BF16)

        srci = sb("srci", [P, TE], I32)
        dsti = sb("dsti", [P, TE], I32)
        reli = sb("reli", [P, TE], I32)
        dprev = sb("dprev", [P, TE], I32)
        dnext = sb("dnext", [P, TE], I32)
        dclamp = sb("dclamp", [P, TE], I32)
        last_i = sb("last_i", [P, TE], I32)
        addr_i = sb("addr_i", [P, TE], I32)
        relf = sb("relf", [P, TE])
        keep = sb("keep", [P, TE])
        last = sb("last", [P, TE])
        openk = sb("openk", [P, TE])
        slotf = sb("slotf", [P, TE])
        tmpf = sb("tmpf", [P, TE])
        lo_i = sb("lo_i", [P, TE], I32)
        hi_i = sb("hi_i", [P, TE], I32)
        rec = sb("rec", [P, TE, REC])
        edge_s = rec[:, :, :].bitcast(I32)
        ring_q = sb("ring_q", [P, T, 4], I32)
        long_open = sb("long_open", [1, 1], I32)
        unsorted = sb("unsorted", [1, 1], I32)
        endv = sb("endv", [P, R])
        tot = sb("tot", [P, R])
        excl = sb("excl", [P, R])
        cross = sb("cross", [P, R])
        cnt_i = sb("cnt_i", [P, R], I32)
        tiles = sb("tiles", [P, R])
        tend = sb("tend", [P, R])
        off = sb("off", [P, R])
        relge = sb("relge", [HALF, R])
        relt = sb("relt", [HALF, 2])
        rel_tab = sb("rel_tab", [1, TS], I32)
        ak = sb("ak", [P, D])
        akT = sb("akT", [D, P])
        endT = sb("endT", [D, P])
        carT = sb("carT", [D, P + 1])
        carry = sb("carry", [P, D])

        xr = [sb(f"xr{u}", [P, W]) for u in range(U)]
        xT = [sb(f"xT{u}", [P, W]) for u in range(U)]
        aT = [sb(f"aT{u}", [P, W]) for u in range(U)]
        vr = [sb(f"vr{u}", [P, W]) for u in range(U)]
        orow = [sb(f"orow{u}", [P, W]) for u in range(U)]
        ybn = sb("ybn", [P, GD * 6])
        mom = sb("mom", [P, 2, D])
        sums = sb("sums", [P, 12])
        st = sb("st", [P, U * T, 6])
        lns = sb("lns", [P, 6, U * T])
        lnb = sb("lnb", [P, U * T])
        st2 = sb("st2", [P, U * T, 6])
        lns2 = sb("lns2", [P, 6, U * T])
        lnb2 = sb("lnb2", [P, U * T])
        moment_rhs = sb("moment_rhs", [P, 4, D])
        st_rhs = [moment_rhs[:, k, :] for k in range(2)]
        corr_rhs = [moment_rhs[:, 2 + k, :] for k in range(2)]
        primer = sb("primer", [1, 32])
        out_of_order = sb("out_of_order", [P, 1])
        runc = sb("runc", [HALF, 4])
        ring_s = [sb(f"ring_s{h}", [P, W]) for h in range(2)]
        ring_d = [sb(f"ring_d{h}", [P, W]) for h in range(2)]
        wide = [sb(f"wide{h}", [P, T, WD]) for h in range(2)]
        idx_a = [sb(f"idx_a{h}", [P, T], I32) for h in range(U)]
        idx_b = [sb(f"idx_b{h}", [P, T], I32) for h in range(2)]
        val = [sb(f"val{h}", [P, T]) for h in range(U)]
        inv = sb("inv", [P, TS])
        slot_rec = sb("slot_rec", [P, TS, 3])
        qidx = sb("qidx", [P, TS], I32)
        lidx = sb("lidx", [P, TS], I32)

        bank = [ctx.enter_context(nc.psum_tensor(f"bank{k}", [P, 512], F32)) for k in range(8)]

        cum = agg[:, 0:R * TE]
        hot = agg[:, R * TE:R * TE + BINS * TE]
        keyT = agg[0:HALF, 0:2 * P]
        keyP = agg[0:HALF, 2 * P:4 * P]
        runS = agg[0:HALF, 4 * P:6 * P]
        runF = agg[0:HALF, 6 * P:8 * P]
        runE = agg[0:HALF, 8 * P:10 * P]
        runX = agg[0:HALF, 10 * P:12 * P]
        line = agg[0:1, 12 * P:12 * P + 4 * (TS + 1)].rearrange("p (k t) -> p k t", k=4)
        rec_in = agg[:, 0:HALF * WD]
        acc = [vr[2], vr[3]]
        srow = [wide[h][:, :, :] for h in range(2)]
        sT = [(aT[2], aT[3]), (xT[2], xT[3])]

        def edge_rows(a, g, n=1):
            return a.rearrange("(p t) d -> p (t d)", p=P)[:, bass.ds(g * W, W)]

        def node_rows(a, g, p):
            if p != P:
                return a[GD_FULL * ROWS:N, :].rearrange("(p j) d -> p (j d)", j=T)
            return a[0:GD_FULL * ROWS, :].rearrange("(g p j) d -> g p (j d)", p=P, j=T)[bass.ds(g, 1)] \
                .rearrange("o p w -> (o p) w")

        def slot_view(l, g):
            w = WD if l == 0 else D
            return slot_rows[l].rearrange("(p t) w -> p t w", p=P)[:, bass.ds(g * T, T), :]

        per_group = {
            "x_turned": ["stats", "x1d", "x1s", "dense", "d0", "d1", "d2"],
            "x_copied": ["stats", "x1d", "x1s", "dense", "d0", "d1", "d2"],
            "hid_ready": ["stats", "x1d", "x1s", "dense"],
            "hid_relu": ["stats", "x1d", "x1s", "dense"],
            "y_ready": ["stats", "x1d", "x1s", "dense", "d0", "d1", "d2"],
            "y_counted": ["stats"],
            "x0_ready": ["x1d"],
            "v_ready": ["x1d", "x1s", "dense", "d0", "d1", "d2"],
            "v_final": ["d2"],
            "v_stats": ["x1d", "x1s", "dense", "d2"],
            "x1_ready": ["x1d", "x1s", "dense", "d0", "d1", "d2"],
            "x1_turned": ["dense"], "x1_copied": ["dense"], "r0_ready": ["dense"], "r0_relu": ["dense"],
            "r1_ready": ["dense"], "r1_relu": ["dense"], "r2_ready": ["dense"],
            "v2_ready": ["dense"], "v2_stats": ["dense"], "out_ready": ["dense"],
        }
        size = dict(stats=GD, x1s=GE, x1d=GE, dense=DENSE_ONLY, mix0=2 * GM, d0=GE, mix1=2 * GM, d1=GE, mix2=2 * GM,
                    d2=GE)

        def in_turn(stages):
            return [s for s in size if s in stages or (s.startswith("mix") and "dense" in stages)]

        def uses(stage, u):
            return per_buffer(size[stage], width(stage), u) if u < width(stage) else 0

        def norms(stage):
            return size[stage] if stage.startswith("mix") else iters(size[stage], U)
        plan = {k: [(s, size[s]) for s in in_turn(v)] for k, v in per_group.items()}
        ln_stages = in_turn(["x1d", "x1s", "dense", "d2"])
        plan["ln_step"] = [(s, 4 * norms(s)) for s in ln_stages]
        plan["var_ready"] = [(s, norms(s)) for s in ln_stages]
        plan["std_ready"] = [(s, norms(s)) for s in ln_stages]
        for k, c in (("ln2_step", 4), ("var2_ready", 1), ("std2_ready", 1)):
            plan[k] = [(s, c * norms(s)) for s in in_turn(["dense"])]
        for u in range(U):
            plan[f"loaded{u}"] = [(s, 16 * uses(s, u)) for s in in_turn(per_group["x_turned"])]
            plan[f"stored{u}"] = [(s, 16 * uses(s, u)) for s in ("x1s", "x1d", "dense", "d0", "d1")]
            plan[f"x1_loaded{u}"] = [("d2", 16 * per_buffer(GE, U, u))]
            plan[f"scattered{u}"] = [("d2", 16 * T * per_buffer(GE, U, u))]
        SL = [f"s{l}" for l in range(L)]
        for k in ("s_turned", "s_copied", "msg_sums", "msg_ready", "msg_idx"):
            plan[k] = [(s, GS) for s in SL]
        for k in ("base_ready", "base_relu"):
            plan[k] = [(s, GS) for s in SL[:2]]
        for h in range(2):
            plan[f"out_stored{h}"] = [(f"mix{l}", 16 * GM) for l in range(L)]
            plan[f"slot_loaded{h}"] = [(s, 16 * per_buffer(GS, 2, h)) for s in SL]
            plan[f"fetched{h}"] = [(s, 16 * T * per_buffer(GS, 2, h)) for s in SL]
            plan[f"msg_out{h}"] = [(s, 16 * T * per_buffer(GS, 2, h)) for s in SL]
            plan[f"slot_stored{h}"] = [(s, 16 * per_buffer(GS, 2, h)) for s in SL[:2]]
        plan["slot_idx"] = [(s, GS) for s in SL]
        seg_uses = ["neigh"] + [f"m{l}" for l in range(L)]
        plan["agg_loaded"] = [(s, 16) for s in seg_uses]
        plan["scanned"] = [(s, D) for s in seg_uses]
        plan["carried"] = [(s, D) for s in seg_uses]
        plan["end_turned"] = [(s, 1) for s in seg_uses]
        plan["carry_step"] = [(s, 3) for s in seg_uses]
        plan["carry_turned"] = [(s, 1) for s in seg_uses]
        SG = Signals(sem, plan)
        S, at = SG.sem, SG.at

        def free(name, stage, i, u):
            return at(name, stage, U - width(stage) + i * width(stage) + u + 1)

        def nth(name, stage, i, u):
            return at(name, stage, i * width(stage) + u + 1)

        def nth_after_free(name, stage, i, u):
            return at(name, stage, U + i * width(stage) + u + 1)

        s_q = {k: sem("radix_" + k) for k in ("step", "counted", "summed", "placed", "copied", "scattered",
                                              "loaded", "shifted")}
        s_fill = sem("filled")
        s_idx = sem("indices_loaded")
        s_wts = sem("weights_loaded")
        s_zero = sem("scratch_zeroed")
        s_dve = sem("vector_step")
        s_pe = sem("tensor_step")
        s_rows = [sem(f"rows_gathered{h}") for h in range(2)]
        s_rst = [sem(f"gathered_stored{h}") for h in range(2)]
        s_cp = sem("index_copied")
        s_pad = sem("pool_pad")
        s_pad_pe = sem("tensor_pad")
        s_tab = [sem(f"table_written{h}") for h in range(2)]
        s_look = [sem(f"table_read{h}") for h in range(U)]
        s_lc = sem("looked_up")
        s_wl = [sem(f"wide_loaded{h}") for h in range(2)]
        s_ws = [sem(f"wide_scattered{h}") for h in range(2)]
        s_e = {k: sem("edge_" + k) for k in ("loaded0", "loaded1", "x0", "turned", "copied", "base_copied", "hid", "relu", "y", "base",
                                             "diff", "acc")}
        s_rin = sem("records_loaded")
        s_key = sem("keys_moved")
        s_std = sem("y_std")
        RADIX_STEPS = 2 + 2 * RADIX // 8 + 3 + 1 + 6 + 5 * RADIX // 8 - 1 + 2
        DV = {}
        WTS = 16 * 34


        def halves(eng, body):
            body(0, 0, True, False)
            with eng.Fori(0, GM - 1) as i:
                body(i, 1, True, True)
                body(i + 1, 0, True, True)
            body(GM - 1, 1, True, True)
            body(GM, 0, False, True)

        GA = 2 * 16 * T

        block = ctx.enter_context(nc.Block())

        @block.vector
        def _(dve):
            steps = [0]

            def step(ins, name=None):
                steps[0] += 1
                ins.then_inc(s_dve, 1)
                dve.wait_ge(s_dve, steps[0])
                if name:
                    DV[name] = steps[0]

            tt, ts, stt, scan = dve.tensor_tensor, dve.tensor_scalar, dve.scalar_tensor_tensor, dve.tensor_tensor_scan
            dve.sem_inc(S["v_ready"], U)
            dve.sem_inc(S["v2_ready"], U)
            dve.sem_inc(S["v_final"], U)
            dve.sem_inc(S["y_counted"], U)
            dve.sem_inc(S["msg_ready"], 1)
            dve.memset(const[:, 0:1], EPS / 4)
            dve.memset(const[:, 1:2], EPS)
            dve.memset(pick3[:, :], 0.0)
            for k in range(L + 1):
                ins = dve.memset(bias3[k][:, :], 0.0)
            step(ins, "consts")
            for k in range(3):
                ins = dve.memset(pick3[32 * k:32 * k + 1, :], 1.0)
            step(ins)

            hotv = hot.rearrange("p (r t) -> p r t", t=TE)
            cumv = cum.rearrange("p (r t) -> p r t", t=TE)

            def mark(step, keyf, c, nb, n=P):
                step(tt(hotv[0:n, 0:nb], keyf[0:n, :].unsqueeze(1).to_broadcast([n, nb, TE]),
                        bins[0:n, c * nb:(c + 1) * nb].unsqueeze(2).to_broadcast([n, nb, TE]), ALU.is_equal))

            def count(step, keyf, total, nb, n=P):
                for c in range(total // nb):
                    mark(step, keyf, c, nb, n)
                    lo = c * nb * TE
                    step(scan(cum[0:n, lo:lo + nb * TE], ones[0:n, 0:1].to_broadcast([n, nb * TE]), hot[0:n, 0:nb * TE],
                              0.0 if c == 0 else cum[0:n, lo - 1:lo], ALU.mult, ALU.add))
                dve.memset(excl[0:n, 0:1], 0.0)
                step(dve.tensor_copy(endv[0:n, 0:total], cumv[0:n, 0:total, TE - 1]))
                step(dve.tensor_copy(excl[0:n, 1:total], endv[0:n, 0:total - 1]))
                step(tt(tot[0:n, 0:total], endv[0:n, 0:total], excl[0:n, 0:total], ALU.subtract))

            def place(step, keyf, total, nb, n=P):
                for c in range(total // nb):
                    mark(step, keyf, c, nb, n)
                    part = cumv[0:n, c * nb:(c + 1) * nb, :]
                    step(tt(part, part, off[0:n, c * nb:(c + 1) * nb].unsqueeze(2).to_broadcast([n, nb, TE]), ALU.add))
                    step(tt(part, part, hotv[0:n, 0:nb], ALU.mult))
                    step(dve.tensor_reduce((slotf if c == 0 else tmpf)[0:n, :], part.rearrange("p r t -> p t r"), AX.X, ALU.add))
                    if c:
                        step(tt(slotf[0:n, :], slotf[0:n, :], tmpf[0:n, :], ALU.add))

            dve.wait_ge(s_fill, 5)
            dve.wait_ge(s_idx, 16 * 7)
            step(tt(tmpf[:, :], dprev[:, :], dsti[:, :], ALU.is_gt))
            step(dve.tensor_reduce(out_of_order[:, :], tmpf[:, :], AX.X, ALU.max), "order_seen")
            dve.wait_ge(s_pe, 1)
            step(ts(unsorted[:, :], bank[0][0:1, 0:1], 1.0, None, ALU.min), "order_known")
            flag = dve.value_load(unsorted[0:1, 0:1], min_val=0, max_val=1)
            with dve.If(flag > 0):
                n = PE_FULL
                dve.tensor_copy(edge_s[0:n, :, 0], srci[0:n, :])
                dve.tensor_copy(edge_s[0:n, :, 1], dsti[0:n, :])
                dve.tensor_copy(edge_s[0:n, :, 2], reli[0:n, :])
                dve.tensor_copy(edge_s[0:n, :, 3], dsti[0:n, :]).then_inc(s_q["step"], 1)
                dve.wait_ge(s_q["step"], 1)
                with dve.Fori(0, PASSES) as k:
                    done = [0]

                    def link(ins):
                        done[0] += 1
                        ins.then_inc(s_q["step"], 1)
                        dve.wait_ge(s_q["step"], k * RADIX_STEPS + done[0] + 1)
                    link(ts(lo_i[0:n, :], edge_s[0:n, :, 3], RADIX - 1, None, ALU.bitwise_and))
                    link(dve.tensor_copy(relf[0:n, :], lo_i[0:n, :]))
                    count(link, relf, RADIX, 8, n)
                    link(dve.memset(slotf[0:1, 0:1], 0.0))
                    dve.sem_inc(s_q["counted"], 1)
                    dve.wait_ge(s_q["summed"], k + 1)
                    link(dve.tensor_copy(tiles[0:n, 0:RADIX], bank[0][0:n, RADIX:2 * RADIX]))
                    link(dve.tensor_copy(cross[0:n, 0:RADIX], bank[0][0:n, 0:RADIX]))
                    link(scan(tend[0:n, 0:RADIX], ones[0:n, 0:RADIX], tiles[0:n, 0:RADIX], 0.0, ALU.mult, ALU.add))
                    link(tt(off[0:n, 0:RADIX], tend[0:n, 0:RADIX], tiles[0:n, 0:RADIX], ALU.subtract))
                    link(tt(off[0:n, 0:RADIX], off[0:n, 0:RADIX], cross[0:n, 0:RADIX], ALU.add))
                    link(stt(off[0:n, 0:RADIX], off[0:n, 0:RADIX], -1.0, excl[0:n, 0:RADIX], ALU.add, ALU.subtract))
                    place(link, relf, RADIX, 8, n)
                    link(dve.tensor_copy(hi_i[0:n, :], slotf[0:n, :]))
                    link(ts(edge_s[0:n, :, 3], edge_s[0:n, :, 3], DIGIT, None, ALU.logical_shift_right))
                    dve.sem_inc(s_q["placed"], 1)
                    dve.wait_ge(s_q["loaded"], 16 * (k + 1))
                    assert done[0] == RADIX_STEPS
                dve.tensor_copy(srci[0:n, :], edge_s[0:n, :, 0])
                dve.tensor_copy(dsti[0:n, :], edge_s[0:n, :, 1])
                dve.tensor_copy(reli[0:n, :], edge_s[0:n, :, 2]).then_inc(s_q["step"], 1)
                dve.wait_ge(s_q["step"], PASSES * RADIX_STEPS + 2)
                dve.wait_ge(s_q["shifted"], 16 * 4)

            ts(dclamp[:, :], dsti[:, :], float(N - 1), None, ALU.min)
            tt(keep[:, :], dsti[:, :], dprev[:, :], ALU.is_equal)
            tt(last[:, :], dsti[:, :], dnext[:, :], ALU.not_equal)
            dve.tensor_copy(relf[:, :], reli[:, :])
            step(dve.memset(rec[:, :, :], 0.0), "dst_clamped")
            scan(openk[:, :], keep[:, :], keep[:, :], 1.0, ALU.min, ALU.min)
            step(stt(tmpf[:, :], last[:, :], -float(BIG), dsti[:, :], ALU.mult, ALU.add))
            step(ts(last_i[:, :], tmpf[:, :], float(BIG), None, ALU.add))
            step(ts(tmpf[:, :], dsti[:, :], 1.0, float(R), ALU.add, ALU.mult))
            tt(rec[:, :, 2], tmpf[:, :], relf[:, :], ALU.add)
            dve.tensor_copy(rec[:, :, 0], edge1[:, :])
            step(dve.tensor_copy(ak[:, :], openk[:, TE - 1:TE].to_broadcast([P, D])))

            count(step, relf, R, BINS)
            DV["counted"] = steps[0]
            dve.wait_ge(s_pe, 2)
            ts(cnt_i[:, :], bank[0][:, R:2 * R], float(P - 1), None, ALU.add)
            step(dve.tensor_copy(cross[:, :], bank[0][:, 0:R]))
            step(ts(cnt_i[:, :], cnt_i[:, :], 7, None, ALU.logical_shift_right))
            step(dve.tensor_copy(tiles[:, :], cnt_i[:, :]))
            step(scan(tend[:, :], ones[:, 0:R], tiles[:, :], 0.0, ALU.mult, ALU.add))
            step(tt(off[:, :], tend[:, :], tiles[:, :], ALU.subtract))
            step(stt(off[:, :], off[:, :], float(P), cross[:, :], ALU.mult, ALU.add))
            step(stt(off[:, :], off[:, :], -1.0, excl[:, :], ALU.add, ALU.subtract))
            for h in range(2):
                step(ts(relge[:, :], tend[0:HALF, :], tile_no[:, h:h + 1], None, ALU.is_le))
                step(dve.tensor_reduce(relt[:, h:h + 1], relge[:, :], AX.X, ALU.add))
            step(ts(relt[:, :], relt[:, :], float(R - 1), float(D), ALU.min, ALU.mult), "tile_rel")
            place(step, relf, R, BINS)
            step(ts(tmpf[:, :], relf[:, :], float(R), float(BIG), ALU.is_ge, ALU.mult))
            step(tt(hi_i[:, :], slotf[:, :], tmpf[:, :], ALU.add))
            step(ts(lo_i[:, :], hi_i[:, :], P - 1, None, ALU.bitwise_and))
            step(ts(hi_i[:, :], hi_i[:, :], 7, None, ALU.logical_shift_right))
            step(stt(addr_i[:, :], lo_i[:, :], float(TS), hi_i[:, :], ALU.mult, ALU.add))
            dve.wait_ge(s_pe, 4)
            dve.tensor_copy(akT[:, :], bank[2][0:D, 0:P])
            dve.memset(carT[:, 0:1], 0.0)
            ts(long_open[:, :], bank[2][0:1, P:P + 1], 1.0, None, ALU.min)
            step(dve.tensor_copy(rel_tab[:, :], bank[1][0:1, 0:TS]), "sorted")

            def norm_bias(k, row):
                step(dve.tensor_copy(split_b[:, 0, :], row))
                step(tt(split[:, 0, :], row, split_b[:, 0, :], ALU.subtract))
                step(dve.tensor_copy(split_b[:, 1, :], split[:, 0, :]))
                step(tt(split[:, 1, :], split[:, 0, :], split_b[:, 1, :], ALU.subtract))
                step(dve.tensor_copy(split_b[:, 2, :], split[:, 1, :]))
                for r in range(3):
                    q = slice(32 * r, 32 * r + 1)
                    ins = dve.tensor_copy(bias3[k][q, :].rearrange("p (t d) -> p t d", d=D),
                                          split_b[q, r, :].unsqueeze(1).to_broadcast([1, T, D]))
                step(ins)
            dve.wait_ge(s_wts, WTS)
            for k in range(L):
                norm_bias(1 + k, row_v[:, 3 + k, :])
            step(ts(eps1[:, :], eps1[:, :], 1.0, None, ALU.add), "eps")

            def stats(i, us):
                for u, p in us:
                    dve.wait_ge(S["x_turned"], at("x_turned", "stats", U + i * U + u + 1))
                    dve.tensor_copy(xT[u][:, 0:4 * p], bank[2 * u][:, 0:4 * p]).then_inc(S["x_copied"], 1)
                for u, p in us:
                    dve.wait_ge(S["y_ready"], at("y_ready", "stats", i * U + u + 1))
                    dve.bn_stats(ybn[:, bass.ds((i * U + u) * 6, 6)], bank[2 * u][:, 0:4 * p]).then_inc(S["y_counted"], 1)
            rounds(dve, GD, U, stats, last=REST)
            dve.wait_ge(S["y_counted"], at("y_counted", "stats", GD + U))

            def segment_sum(use):
                dve.wait_ge(S["agg_loaded"], at("agg_loaded", use, 16))
                with dve.Fori(0, D // 4) as i:
                    for k in range(4):
                        col = aggv[:, :, bass.ds(i * 4 + k, 1)].rearrange("p t o -> p (t o)")
                        scan(col, keep[:, :], col, 0.0, ALU.mult, ALU.add).then_inc(S["scanned"], 1)
                dve.wait_ge(S["end_turned"], at("end_turned", use, 1))
                dve.tensor_copy(endT[:, :], bank[4][0:D, 0:P]).then_inc(S["carry_step"], 1)
                dve.wait_ge(S["carry_step"], at("carry_step", use, 1))
                scan(carT[:, 1:P + 1], akT[:, :], endT[:, :], 0.0, ALU.mult, ALU.add).then_inc(S["carry_step"], 1)
                dve.wait_ge(S["carry_turned"], at("carry_turned", use, 1))
                dve.tensor_copy(carry[:, :], bank[5][:, 0:D]).then_inc(S["carry_step"], 1)
                dve.wait_ge(S["carry_step"], at("carry_step", use, 3))
                dve.wait_ge(S["scanned"], at("scanned", use, D))
                flag = dve.value_load(long_open[0:1, 0:1], min_val=0, max_val=1)
                with dve.If(flag > 0):
                    with dve.Fori(0, D // 4) as i:
                        for k in range(4):
                            col = aggv[:, :, bass.ds(i * 4 + k, 1)].rearrange("p t o -> p (t o)")
                            stt(col, openk[:, :], carry[:, bass.ds(i * 4 + k, 1)], col, ALU.mult, ALU.add).then_inc(S["carried"], 1)
                with dve.If(flag < 1):
                    part = orow[2][:, 0:SHORT * D].rearrange("p (t d) -> p t d", d=D)
                    tt(part, openk[:, 0:SHORT].unsqueeze(2).to_broadcast([P, SHORT, D]),
                       carry[:, :].unsqueeze(1).to_broadcast([P, SHORT, D]), ALU.mult).then_inc(S["carried"], 1)
                    dve.wait_ge(S["carried"], at("carried", use, 1))
                    tt(aggv[:, 0:SHORT, :], aggv[:, 0:SHORT, :], part, ALU.add).then_inc(S["carried"], 1)
                    dve.sem_inc(S["carried"], D - 2)
                dve.wait_ge(S["carried"], at("carried", use, D))
            segment_sum("neigh")

            def agg_group(g):
                return agg[:, bass.ds(g * W, W)]

            dve.memset(acc[0][:, :], 0.0)
            step(dve.memset(acc[1][:, :], 0.0))
            dve.sem_inc(s_e["acc"], 3)

            def edge_change(i, us):
                for b, _ in us:
                    g = i * 2 + b
                    dve.wait_ge(s_e[f"loaded{b}"], 16 * (i + 1))
                    dve.wait_ge(s_e["turned"], g + 1)
                    stt(xr[2 * b + 1][:, :], xr[2 * b][:, :], eps1[:, 0:1], agg_group(g), ALU.mult, ALU.add).then_inc(s_e["x0"], 1)
                for b, _ in us:
                    g = i * 2 + b
                    dve.wait_ge(s_e["turned"], g + 3)
                    dve.tensor_copy(xT[2 * b + 1][:, :], bank[4 * b + 2][:, :]).then_inc(s_e["copied"], 1)
                for b, _ in us:
                    g = i * 2 + b
                    base, y1 = orow[3 * b], bank[4 * b + 2]
                    dve.wait_ge(s_e["base"], g + 1)
                    dve.wait_ge(s_e["acc"], 2 * g + 3)
                    tt(orow[1][:, :], y1[:, :], base[:, :], ALU.subtract)
                    tt(orow[2][:, :], y1[:, :], base[:, :], ALU.add).then_inc(s_e["diff"], 1)
                    dve.wait_ge(s_e["diff"], 2 * g + 1)
                    tt(orow[1][:, :].rearrange("p (t d) -> p t d", d=D), orow[1][:, :].rearrange("p (t d) -> p t d", d=D),
                       last[:, bass.ds(g * T, T)].unsqueeze(2).to_broadcast([P, T, D]), ALU.mult).then_inc(s_e["diff"], 1)
                    dve.wait_ge(s_e["diff"], 2 * g + 2)
                    tt(acc[0][:, :], acc[0][:, :], orow[1][:, :], ALU.add)
                    tt(orow[2][:, :], orow[2][:, :], orow[1][:, :], ALU.mult).then_inc(s_e["acc"], 1)
                    dve.wait_ge(s_e["acc"], 2 * g + 4)
                    tt(acc[1][:, :], acc[1][:, :], orow[2][:, :], ALU.add).then_inc(s_e["acc"], 1)
            rounds(dve, GE, 2, edge_change)
            dve.wait_ge(s_e["acc"], 2 * GE + 3)

            for k in range(2):
                ins = dve.tensor_reduce(corr_rhs[k], acc[k][:, :].rearrange("p (t d) -> p d t", d=D), AX.X, ALU.add)
            step(dve.bn_aggr(sums[:, 0:2], ybn[:, :]))
            step(tt(sums[:, 2:3], sums[:, 0:1], sums[:, 0:1], ALU.mult))
            step(tt(sums[:, 3:4], sums[:, 1:2], sums[:, 2:3], ALU.add))
            for k in range(2):
                ins = ts(st_rhs[k], fold[:, :], sums[:, (0, 3)[k]:(0, 3)[k] + 1], float(N // 2), ALU.mult, ALU.mult)
            step(ins, "moments")
            dve.wait_ge(s_pe, 5)
            ts(mom[:, 0, :], bank[4][:, 0:D], 1.0 / N, None, ALU.mult)
            step(ts(mom[:, 1, :], bank[4][:, D:2 * D], 1.0 / N, None, ALU.mult))
            step(tt(split[:, 0, :], mom[:, 0, :], mom[:, 0, :], ALU.mult))
            step(tt(mom[:, 1, :], mom[:, 1, :], split[:, 0, :], ALU.subtract), "y_var")
            dve.wait_ge(s_std, 1)
            step(dve.reciprocal(mom[:, 1, :], mom[:, 1, :]))
            step(tt(mom[:, 1, :], mom[:, 1, :], row_v[:, 1, :], ALU.mult))
            step(tt(mom[:, 0, :], mom[:, 0, :], row_v[:, 0, :], ALU.add))
            step(tt(mom[:, 0, :], row_v[:, 0, :], mom[:, 0, :], ALU.subtract))
            step(tt(mom[:, 0, :], mom[:, 0, :], mom[:, 1, :], ALU.mult))
            step(tt(mom[:, 0, :], mom[:, 0, :], row_v[:, 2, :], ALU.add))
            step(ts(mom[:, 0, :], mom[:, 0, :], 0.5, None, ALU.mult))
            norm_bias(0, mom[:, 0, :])
            for h in range(2):
                q = slice(h * D, (h + 1) * D)
                ins = stt(w2n[:, q], w2[:, q], 0.5, mom[:, 1, :], ALU.mult, ALU.mult)
            step(ins, "w2n")

            def layer_norm(stage, i, us, buf, stats_, small, nb, names):
                seen, inner, var, std, final = names
                q, r = norm_cols(us), norm_round(stage, i, us)
                for u, p in us:
                    for j in range(T):
                        ins = dve.bn_stats(stats_[0:p, u * T + j, :], buf[u][0:p, j * D:(j + 1) * D])
                    ins.then_inc(S[seen], 1)
                c = lambda k: at(inner, stage, r * 4 + k)
                dve.wait_ge(S[seen], nth(seen, stage, i, us[-1][0]))
                me, m2e, mo, m2o = (stats_[:, q, k] for k in (1, 2, 4, 5))
                tt(small[:, 0, q], me, mo, ALU.add)
                tt(small[:, 1, q], me, mo, ALU.subtract)
                tt(small[:, 2, q], m2e, m2o, ALU.add).then_inc(S[inner], 1)
                dve.wait_ge(S[inner], c(1))
                stt(small[:, 1, q], small[:, 1, q], D / 4.0, small[:, 1, q], ALU.mult, ALU.mult).then_inc(S[inner], 1)
                dve.wait_ge(S[inner], c(2))
                tt(small[:, 3, q], small[:, 1, q], small[:, 2, q], ALU.add).then_inc(S[var], 1)
                dve.wait_ge(S[std], at(std, stage, r + 1))
                dve.reciprocal(small[:, 5, q], small[:, 4, q]).then_inc(S[inner], 1)
                dve.wait_ge(S[inner], c(3))
                stt(nb[:, q], small[:, 0, q], -0.5, small[:, 5, q], ALU.mult, ALU.mult).then_inc(S[inner], 1)
                dve.wait_ge(S[inner], c(4))
                for u, p in us:
                    for j in range(T):
                        k = u * T + j
                        ins = ts(buf[u][0:p, j * D:(j + 1) * D], buf[u][0:p, j * D:(j + 1) * D], small[0:p, 5, k:k + 1],
                                 nb[0:p, k:k + 1], ALU.mult, ALU.add)
                    ins.then_inc(S[final], 1)
            LN1 = ("v_stats", "ln_step", "var_ready", "std_ready", "x1_ready")
            LN2 = ("v2_stats", "ln2_step", "var2_ready", "std2_ready", "out_ready")

            def sum_x(stage, i, us):
                for u, p in us:
                    if stage in FIRST:
                        dve.wait_ge(S["v2_ready"], free("v2_ready", stage, i, u))
                    else:
                        dve.wait_ge(S[f"stored{u}"], at(f"stored{u}", stage, 16 * (i + 1)))
                    dve.wait_ge(S["y_ready"], nth("y_ready", stage, i, u))
                    stt(vr[u][0:p, :], bank[2 * u][0:p, :], 0.0, xr[u][0:p, :], ALU.max, ALU.add).then_inc(S["v_ready"], 1)
                dve.wait_ge(S["v_ready"], nth_after_free("v_ready", stage, i, us[-1][0]))

            def x1s(i, us):
                sum_x("x1s", i, us)
                layer_norm("x1s", i, us, vr, st, lns, lnb, LN1)
            rounds(dve, GE, U, x1s)

            def x1d(i, us):
                for u, p in us:
                    g = i * U + u
                    dve.wait_ge(S["x_turned"], at("x_turned", "x1d", g + 1))
                    dve.wait_ge(S[f"loaded{u}"], at(f"loaded{u}", "x1d", 16 * (i + 1)))
                    stt(orow[u][:, :], xr[u][:, :], eps1[:, 0:1], agg_group(g), ALU.mult, ALU.add).then_inc(S["x0_ready"], 1)
                sum_x("x1d", i, us)
                layer_norm("x1d", i, us, vr, st, lns, lnb, LN1)
            rounds(dve, GE, U, x1d)
            for u in range(U):
                dve.wait_ge(S[f"stored{u}"], at(f"stored{u}", "x1d", 16 + 16 * uses("x1d", u)))

            def dense_x1(stage, i, us):
                sum_x(stage, i, us)
                layer_norm(stage, i, us, vr, st, lns, lnb, LN1)

            def dense_out(stage, i, us):
                for u, p in us:
                    sm = f"stored{u}" if stage == "dense" else f"out_stored{u}"
                    dve.wait_ge(S["r2_ready"], nth("r2_ready", stage, i, u))
                    dve.wait_ge(S[sm], at(sm, stage, 16 * (i + 1)))
                    dve.wait_ge(S["x1_ready"], nth("x1_ready", stage, i, u))
                    tt(orow[u][0:p, :], bank[2 * u][0:p, :], vr[u][0:p, :], ALU.add).then_inc(S["v2_ready"], 1)
                dve.wait_ge(S["v2_ready"], nth_after_free("v2_ready", stage, i, us[-1][0]))
                layer_norm(stage, i, us, orow, st2, lns2, lnb2, LN2)

            def dense(i, us):
                dense_x1("dense", i, us)
                dense_out("dense", i, us)
            rounds(dve, DENSE_ONLY, U, dense, last=REST)

            riv = rec_in.rearrange("p (t w) -> p t w", w=WD)
            for h in range(2):
                dve.wait_ge(s_rin, 16 * (h + 1))
                step(dve.tensor_copy(slot_rec[:, h * HALF:(h + 1) * HALF, :], riv[:, :, D:D + 3]),
                     ("half_read", "rec_ready")[h])
            for out_i, k in ((qidx, 0), (lidx, 1)):
                step(ts(inv[:, :], slot_rec[:, :, k], 0.0, float(BIG), ALU.is_equal, ALU.mult))
                step(stt(out_i[:, :], slot_rec[:, :, k], -1.0, inv[:, :], ALU.add, ALU.add), "indices_ready")
            dve.wait_ge(s_pe, 6)
            step(dve.tensor_copy(keyT, bank[0][0:HALF, 0:2 * P]), "key_turned")
            dve.wait_ge(s_key, 32)
            step(tt(runF, keyT, keyP, ALU.not_equal))
            tt(runS, runF, slot_no[:, :], ALU.mult)
            step(ts(runX, slot_no[:, :], -float(BIG), None, ALU.add))
            step(tt(runX, runX, runF, ALU.mult))
            step(ts(runE, runX, float(BIG), None, ALU.add))
            for h in range(2):
                q = slice(h * P, (h + 1) * P)
                scan(runS[:, q], runS[:, q], runS[:, q], 0.0, ALU.max, ALU.max)
                e = runE[:, q][:, ::-1]
                ins = scan(e, e, e, float(BIG), ALU.min, ALU.min)
            step(ins, "run_ends")
            dve.wait_ge(s_pe, 7)
            dve.tensor_copy(line[:, 0, 0:TS], bank[1][0:1, 0:TS])
            dve.tensor_copy(line[:, 1, 0:TS], bank[2][0:1, 0:TS])
            dve.memset(line[:, 2, 0:1], 0.0)
            step(dve.memset(line[:, 3, TS:TS + 1], float(BIG)))
            scan(line[:, 2, 1:TS + 1], line[:, 0, 0:TS], line[:, 0, 0:TS], 0.0, ALU.max, ALU.max)
            step(scan(line[:, 3, 0:TS][:, ::-1], line[:, 1, 0:TS][:, ::-1], line[:, 1, 0:TS][:, ::-1], float(BIG),
                      ALU.min, ALU.min), "run_carry")
            dve.wait_ge(s_pe, 8)
            step(dve.tensor_copy(runc[:, :], bank[3][0:HALF, 0:4]))
            for h in range(2):
                q = slice(h * P, (h + 1) * P)
                ts(runS[:, q], runS[:, q], runc[:, h:h + 1], None, ALU.max)
                ts(runX[:, h * P:(h + 1) * P - 1], runE[:, h * P + 1:(h + 1) * P], runc[:, 2 + h:3 + h], None, ALU.min)
                ins = dve.tensor_copy(runX[:, (h + 1) * P - 1:(h + 1) * P], runc[:, 2 + h:3 + h])
            step(ins)
            step(tt(runX, runX, runS, ALU.subtract))
            step(dve.reciprocal(runX, runX), "run_inv")
            dve.wait_ge(s_pe, 9)
            step(dve.tensor_copy(inv[:, :], bank[4][:, 0:TS]), "slots_ready")

            for l in range(L):
                stage = SL[l]

                def mean(i, h, stage=stage):
                    g = i * 2 + h
                    dve.wait_ge(S["msg_sums"], at("msg_sums", stage, g + 1))
                    dve.wait_ge(S[f"msg_out{h}"], at(f"msg_out{h}", stage, 16 + 16 * T * i))
                    tt(ring_d[h][:, :].rearrange("p (t d) -> p t d", d=D),
                       bank[6][:, :].rearrange("p (t d) -> p t d", d=D),
                       inv[:, bass.ds(g * T, T)].unsqueeze(2).to_broadcast([P, T, D]), ALU.mult).then_inc(S["msg_ready"], 1)
                for u in range(2):
                    prev = f"d{l - 1}" if l else "dense"
                    dve.wait_ge(S[f"stored{u}"], at(f"stored{u}", prev, 16 + 16 * uses(prev, u)))

                def half(i, h, dense, earlier, mix=f"mix{l}"):
                    mean(i, h)
                    if dense:
                        dense_x1(mix, i, [(h, P)])
                    if earlier:
                        dense_out(mix, before_half(i, h)[0], [(1 - h, P)])
                halves(dve, half)
                segment_sum(f"m{l}")
                stage = f"d{l}"

                def dst_stage(i, us, l=l, stage=stage):
                    free = "scattered" if l == L - 1 else "stored"
                    for u, p in us:
                        dve.wait_ge(S[f"{free}{u}"], at(f"{free}{u}", stage, 16 + (16 * T if l == L - 1 else 16) * i))
                        dve.wait_ge(S["y_ready"], at("y_ready", stage, i * U + u + 1))
                        tt(vr[u][:, :], bank[2 * u + 1][:, :], agg_group(i * U + u), ALU.add).then_inc(S["v_ready"], 1)
                    if l == L - 1:
                        for u, p in us:
                            dve.wait_ge(S["v_ready"], at("v_ready", stage, U + i * U + u + 1))
                            dve.wait_ge(S[f"x1_loaded{u}"], at(f"x1_loaded{u}", stage, 16 * (i + 1)))
                            tt(vr[u][:, :], vr[u][:, :], aT[u][:, :], ALU.add).then_inc(S["v_final"], 1)
                        dve.wait_ge(S["v_final"], at("v_final", stage, U + i * U + len(us)))
                        layer_norm(stage, i, us, vr, st, lns, lnb, LN1)
                rounds(dve, GE, U, dst_stage)

        @block.sync
        def _(sp):
            for k, sm in enumerate(s_rst + [S[f"out_stored{h}"] for h in range(2)]):
                sp.dma_start(primer[:, 24 + k:25 + k], eps.rearrange("(p o) -> p o", p=1)).then_inc(sm, 16)
            sp.wait_ge(s_fill, 1)
            v2 = lambda a, n: a[0:n * TE].rearrange("(p t) -> p t", t=TE)
            sp.dma_start(srci[0:PE_FULL, :], v2(src, PE_FULL)).then_inc(s_idx, 16)
            sp.dma_start(dsti[0:PE_FULL, :], v2(dst, PE_FULL)).then_inc(s_idx, 16)
            sp.dma_start(reli[0:PE_FULL, :], v2(etype, PE_FULL)).then_inc(s_idx, 16)
            sp.dma_start(dprev[1:PE_FULL, :], dst[TE - 1:E - 1].rearrange("(p t) -> p t", t=TE)).then_inc(s_idx, 16)
            sp.dma_start(dprev[0:1, 1:TE], dst[0:TE - 1].rearrange("(p t) -> p t", p=1)).then_inc(s_idx, 16)
            sp.dma_start(dnext[0:PE_FULL - 1, :], dst[1:E - TE + 1].rearrange("(p t) -> p t", t=TE)).then_inc(s_idx, 16)
            sp.dma_start(dnext[PE_FULL - 1:PE_FULL, 0:TE - 1],
                         dst[E - TE + 1:E].rearrange("(p t) -> p t", p=1)).then_inc(s_idx, 16)
            sp.wait_ge(s_dve, DV["order_known"])
            flag = sp.value_load(unsorted[0:1, 0:1], min_val=0, max_val=1)
            with sp.If(flag > 0):
                with sp.Fori(0, PASSES) as k:
                    sp.wait_ge(s_q["scattered"], 16 * TE * (k + 1))
                    sp.dma_start(edge_s[0:PE_FULL, :, :], edge_rec.rearrange("(p t) w -> p t w", t=TE)).then_inc(s_q["loaded"], 16)
                sp.wait_ge(s_q["loaded"], 16 * PASSES)
                ds_ = edge_rec[:, 1:2]
                with nc.allow_non_contiguous_dma(reason="one word of every edge record"):
                    sp.dma_start(dprev[1:PE_FULL, :], ds_[TE - 1:E - 1, :].rearrange("(p t) o -> p (t o)", t=TE)).then_inc(s_q["shifted"], 16)
                    sp.dma_start(dprev[0:1, 1:TE], ds_[0:TE - 1, :].rearrange("(p t) o -> p (t o)", p=1)).then_inc(s_q["shifted"], 16)
                    sp.dma_start(dnext[0:PE_FULL - 1, :], ds_[1:E - TE + 1, :].rearrange("(p t) o -> p (t o)", t=TE)).then_inc(s_q["shifted"], 16)
                    sp.dma_start(dnext[PE_FULL - 1:PE_FULL, 0:TE - 1],
                                 ds_[E - TE + 1:E, :].rearrange("(p t) o -> p (t o)", p=1)).then_inc(s_q["shifted"], 16)
            for h in range(2):
                q = slice(h * D, (h + 1) * D)
                for tile, w in ((w1, W1), (w2, W2), (root[0], w0_root), (root[1], w1_root), (root[2], w2_root)):
                    sp.dma_start(tile[q, q], w[:, :]).then_inc(s_wts, 16)
                for tile, b in ((b1c, b1), (rootb[0], b0), (rootb[1], c1), (rootb[2], c2)):
                    sp.dma_start(tile[q, :], b.rearrange("(d o) -> d o", o=1)).then_inc(s_wts, 16)
            for k, b in enumerate((b2, gamma, beta, b0, c1, c2)):
                sp.dma_start(row_v[:, k, :], b.partition_broadcast(P)).then_inc(s_wts, 16)
            sp.dma_start(eps1[:, :], eps.partition_broadcast(P)).then_inc(s_wts, 16)
            wv = rel_w[:, :].rearrange("d (l r o) -> d l r o", l=L, r=R)
            nb = w0_rel.shape[1]
            db = D // nb
            for l, w in ((0, w0_rel), (1, w1_rel)):
                for b in range(nb):
                    q = slice(b * db, (b + 1) * db)
                    sp.dma_start(wv[q, l, :, q], w[:, b].rearrange("r d o -> d r o")).then_inc(s_wts, 16)
            sp.dma_start(wv[:, 2], w2_rel.rearrange("r d o -> d r o")).then_inc(s_wts, 16)

            sp.wait_ge(s_fill, 2)
            sp.dma_start(node_table.rearrange("(p t) o -> p (t o)", p=PE_FULL), zeros[0:PE_FULL, :]).then_inc(s_zero, 16)
            sp.dma_start(msg_rows[E:EP, :].rearrange("(p t) d -> p (t d)", p=120),
                         zeros[0:120, 0:(EP - E) * D // 120]).then_inc(s_zero, 16)
            sp.dma_start(key_line[0:1].rearrange("(p o) -> p o", p=1), zeros[0:1, 0:1]).then_inc(s_zero, 16)
            with sp.Fori(0, GS) as g:
                sp.dma_start(slot_view(0, g), zeros[:, 0:T * WD].rearrange("p (t w) -> p t w", t=T)).then_inc(s_zero, 16)

            def load_nodes(stage, i, us):
                for u, p in us:
                    name = "x_turned" if stage == "stats" else "v_ready"
                    sp.wait_ge(S[name], free(name, stage, i, u))
                    sp.dma_start(xr[u][0:p, :], node_rows(x, FIRST[stage] + i * width(stage) + u, p)).then_inc(S[f"loaded{u}"], 16)

            def store_gathered(i, h):
                sp.wait_ge(s_rows[h], GA * (i + 1))
                g = i * 2 + h
                sp.dma_start(edge_rows(src_x, g), ring_s[h][:, :]).then_inc(s_rst[h], 16)
                sp.dma_start(edge_rows(dst_x, g), ring_d[h][:, :]).then_inc(s_rst[h], 16)

            def load_round(i):
                load_nodes("stats", i, [(u, P) for u in range(U)])
            with sp.Fori(0, SORTING) as i:
                for h in range(2):
                    store_gathered(i, h)
            with sp.Fori(0, FASTER) as i:
                load_round(i * 3)
                store_gathered(SORTING + i, 0)
                load_round(i * 3 + 1)
                store_gathered(SORTING + i, 1)
                load_round(i * 3 + 2)
            with sp.Fori(0, GE // 2 - SORTING - FASTER) as i:
                for h in range(2):
                    load_round(3 * FASTER + i * 2 + h)
                    store_gathered(SORTING + FASTER + i, h)
            load_nodes("stats", GD // U, [(0, P), (1, REST)])
            store_gathered(GE // 2, 0)

            sp.wait_ge(s_rst[0], 16 + 32 * per_buffer(GE, 2, 0))
            sp.wait_ge(s_rst[1], 16 + 32 * per_buffer(GE, 2, 1))
            sp.wait_ge(s_dve, DV["sorted"])
            sp.dma_start(agg[:, :], src_x.rearrange("(p t) d -> p (t d)", p=P)).then_inc(S["agg_loaded"], 16)
            def edge_load(i, us):
                for b, _ in us:
                    sp.wait_ge(s_e["turned"], i * 2 + b + 1)
                    sp.dma_start(xr[2 * b][:, :], edge_rows(dst_x, i * 2 + b)).then_inc(s_e[f"loaded{b}"], 16)
            rounds(sp, GE, 2, edge_load)

            def load_edges(stage, rows, dest=None, extra=None):
                def loads(i, us):
                    for u, p in us:
                        name = "x_turned" if stage.startswith("d") else "v_ready"
                        sp.wait_ge(S[name], at(name, stage, i * U + u + 1))
                        sp.dma_start(xr[u][:, :], edge_rows(rows, i * U + u)).then_inc(S[f"loaded{u}"], 16)
                        if extra is not None:
                            sp.wait_ge(S["v_final"], at("v_final", stage, i * U + u + 1))
                            sp.dma_start(aT[u][:, :], edge_rows(extra, i * U + u)).then_inc(S[f"x1_loaded{u}"], 16)

                def stores(i, us):
                    for u, _ in us:
                        sp.wait_ge(S["x1_ready"], at("x1_ready", stage, i * U + u + 1))
                        sp.dma_start(edge_rows(dest, i * U + u), vr[u][:, :]).then_inc(S[f"stored{u}"], 16)
                if dest is None:
                    rounds(sp, GE, U, loads)
                    return
                full, rest = divmod(GE, U)
                wide_round, last_round = [(u, P) for u in range(U)], [(u, P) for u in range(rest)]
                loads(0, wide_round)
                with sp.Fori(0, full - 1) as i:
                    loads(i + 1, wide_round)
                    stores(i, wide_round)
                loads(full, last_round)
                stores(full - 1, wide_round)
                stores(full, last_round)

            sp.wait_ge(s_e["acc"], 2 * GE + 3)
            load_edges("x1s", src_x, src_x1)
            sp.wait_ge(S["v_ready"], at("v_ready", "x1s", GE + U))
            load_edges("x1d", dst_x, dst_rows[0])
            sp.wait_ge(S["v_ready"], at("v_ready", "x1d", GE + U))
            rounds(sp, DENSE_ONLY, U, lambda i, us: load_nodes("dense", i, us), last=REST)

            for h in range(2):
                sp.wait_ge(s_ws[h], 16 + 16 * T * per_buffer(GE, 2, h))
            sv = slot_rows[0].rearrange("(p t) w -> p t w", p=P)
            sp.wait_ge(S["x0_ready"], at("x0_ready", "x1d", GE))
            for h in range(2):
                if h:
                    sp.wait_ge(s_dve, DV["half_read"])
                sp.dma_start(rec_in.rearrange("p (t w) -> p t w", w=WD), sv[:, h * HALF:(h + 1) * HALF, :]).then_inc(s_rin, 16)
            def shift_keys():
                sp.wait_ge(s_dve, DV["key_turned"])
                kl = key_line[1:NS + 1].rearrange("(h t c) -> t h c", h=2, c=P)
                sp.dma_start(kl, keyT.rearrange("t (h c) -> t h c", h=2)).then_inc(s_key, 16)
                sp.wait_ge(s_key, 16)
                sp.dma_start(keyP.rearrange("t (h c) -> t h c", h=2),
                             key_line[0:NS].rearrange("(h t c) -> t h c", h=2, c=P)).then_inc(s_key, 16)

            for l in range(L):
                stage = SL[l]

                def load_slots(i, h, l=l, stage=stage):
                    sp.wait_ge(S["s_turned"], at("s_turned", stage, i * 2 + h + 1))
                    dest = srow[h] if l == 0 else srow[h][:, :, 0:D]
                    sp.dma_start(dest, slot_view(l, i * 2 + h)).then_inc(S[f"slot_loaded{h}"], 16)

                mix = f"mix{l}"
                if l:
                    for h in range(2):
                        sp.wait_ge(S[f"slot_stored{h}"], at(f"slot_stored{h}", SL[l - 1], 16 + 16 * per_buffer(GS, 2, h)))
                load_slots(0, 0)
                load_slots(0, 1)
                if l == 0:
                    shift_keys()
                sp.wait_ge(S["v_ready"], at("v_ready", mix, U))
                load_nodes(mix, 0, [(0, P), (1, P)])

                def half(i, h, more_slots=True, more_nodes=True, earlier=True, mix=mix):
                    if more_slots:
                        load_slots(i + 1, h)
                    if more_nodes:
                        load_nodes(mix, i + 1, [(h, P)])
                    if earlier:
                        j, u = before_half(i, h)
                        sp.wait_ge(S["out_ready"], nth("out_ready", mix, j, u))
                        sp.dma_start(node_rows(out, FIRST[mix] + j * 2 + u, P), orow[u][:, :]).then_inc(S[f"out_stored{u}"], 16)
                half(0, 0, earlier=False)
                with sp.Fori(0, GM - 2) as i:
                    half(i, 1)
                    half(i + 1, 0)
                half(GM - 2, 1)
                half(GM - 1, 0, more_nodes=False)
                half(GM - 1, 1, more_slots=False, more_nodes=False)
                half(GM, 0, more_slots=False, more_nodes=False)
                for h in range(2):
                    sp.wait_ge(S[f"msg_out{h}"], at(f"msg_out{h}", stage, 16 + 16 * T * per_buffer(GS, 2, h)))
                sp.wait_ge(S["v_ready"], at("v_ready", mix, 2 * GM + U))
                sp.wait_ge(S["v2_ready"], at("v2_ready", mix, 2 * GM + U))
                if l == 0:
                    sp.wait_ge(s_dve, DV["slots_ready"])
                sp.dma_start(agg[:, :], msg_rows.rearrange("(p t) d -> p (t d)", p=P)).then_inc(S["agg_loaded"], 16)
                load_edges(f"d{l}", dst_rows[l], dst_rows[l + 1] if l < L - 1 else None, dst_rows[0] if l == L - 1 else None)

        @block.gpsimd
        def _(pool):
            def pad():
                pool.sem_inc(s_pad, 1)

            for w_ in (w1, w2, root[0], root[1], root[2], rel_w):
                pool.memset(w_[:, :], 0.0)
            for t_, v_ in ((srci, 0), (dsti, N), (reli, R), (dprev, -1)):
                pool.memset(t_[:, :], v_)
            pool.memset(dnext[:, :], N).then_inc(s_fill, 1)
            pool.memset(zeros[:, :], 0.0).then_inc(s_fill, 1)
            for k, sm in enumerate(s_tab + s_ws + [S[f"msg_out{h}"] for h in range(2)] + [S[f"scattered{u}"] for u in range(U)]):
                pool.dma_start(primer[:, k:k + 1], eps.rearrange("(p o) -> p o", p=1)).then_inc(sm, 16)
            pool.iota(bins[:, :], [[1, R]], base=0, channel_multiplier=0, allow_small_or_imprecise_dtypes=True)
            pool.iota(tile_no[:, :], [[HALF, 2]], base=0, channel_multiplier=1, allow_small_or_imprecise_dtypes=True)
            pool.iota(slot_no[:, :], [[HALF * P, 2], [1, P]], base=0, channel_multiplier=P,
                      allow_small_or_imprecise_dtypes=True)
            pool.iota(edge1[:, :], [[1, TE]], base=1, channel_multiplier=TE, allow_small_or_imprecise_dtypes=True)
            pool.memset(ident[:, :], 0.0)
            pool.memset(fold[:, :], 0.0)
            pool.memset(before[:, :], 1.0)
            pool.memset(ones[:, :], 1.0).then_inc(s_fill, 1)
            pool.wait_ge(s_fill, 3)
            pool.affine_select(out=ident[:, :], in_=ident[:, :], compare_op=ALU.not_equal, fill=1.0, base=0,
                               pattern=[[-1, P]], channel_multiplier=1)
            pool.affine_select(out=before[:, :], in_=before[:, :], compare_op=ALU.is_gt, fill=0.0, base=0,
                               pattern=[[1, P]], channel_multiplier=-1)
            pool.affine_select(out=fold[:, :], in_=fold[:, :], compare_op=ALU.not_equal, fill=1.0, base=0,
                               pattern=[[-1, D]], channel_multiplier=1).then_inc(s_fill, 1)
            pool.wait_ge(s_fill, 4)
            pool.affine_select(out=fold[:, :], in_=fold[:, :], compare_op=ALU.not_equal, fill=1.0, base=-D,
                               pattern=[[-1, D]], channel_multiplier=1).then_inc(s_fill, 1)

            pool.wait_ge(s_dve, DV["order_known"])
            flag = pool.value_load(unsorted[0:1, 0:1], min_val=0, max_val=1)
            with pool.If(flag > 0):
                with pool.Fori(0, PASSES) as k:
                    pool.wait_ge(s_q["placed"], k + 1)
                    pad()
                    with pool.Fori(0, GE) as g:
                        pool.tensor_copy(idx_a[0][0:PE_FULL, :], hi_i[0:PE_FULL, bass.ds(g * T, T)])
                        pool.tensor_copy(ring_q[0:PE_FULL, :, :], edge_s[0:PE_FULL, bass.ds(g * T, T), :]).then_inc(s_q["copied"], 1)
                        pool.wait_ge(s_q["copied"], k * GE + g + 1)
                        pad()
                        for j in range(T):
                            pool.indirect_dma_start(
                                out=edge_rec[:, :],
                                out_offset=bass.IndirectOffsetOnAxis(ap=idx_a[0][0:PE_FULL, j:j + 1], axis=0),
                                in_=ring_q[0:PE_FULL, j, :], in_offset=None).then_inc(s_q["scattered"], 16)
                        pool.wait_ge(s_q["scattered"], (k * GE + g + 1) * T * 16)
                        pad()

            pool.wait_ge(s_idx, 16 * 7)
            pool.wait_ge(s_dve, DV["dst_clamped"])

            def gather_x(i, us):
                for h, _ in us:
                    g = i * 2 + h
                    pool.wait_ge(s_rst[h], 16 + 32 * i)
                    pad()
                    pool.tensor_copy(idx_a[h][:, :], srci[:, bass.ds(g * T, T)])
                    pool.tensor_copy(idx_b[h][:, :], dclamp[:, bass.ds(g * T, T)]).then_inc(s_cp, 1)
                    pool.wait_ge(s_cp, g + 1)
                    pad()
                    for k in range(T):
                        for ring, idx in ((ring_s, idx_a), (ring_d, idx_b)):
                            pool.indirect_dma_start(
                                out=ring[h][:, k * D:(k + 1) * D], out_offset=None, in_=x[:, :],
                                in_offset=bass.IndirectOffsetOnAxis(ap=idx[h][:, k:k + 1], axis=0)
                            ).then_inc(s_rows[h], 16)
            rounds(pool, GE, 2, gather_x)

            pool.wait_ge(s_zero, 16 * (3 + GS))
            pool.wait_ge(s_dve, DV["sorted"])
            for h in range(2):
                pool.wait_ge(s_rows[h], GA * per_buffer(GE, 2, h))

            def write_table(i, us):
                for h, _ in us:
                    g = i * 2 + h
                    pool.wait_ge(s_tab[h], 16 + 16 * T * i)
                    pad()
                    pool.tensor_copy(idx_a[h][:, :], last_i[:, bass.ds(g * T, T)])
                    pool.tensor_copy(val[h][:, :], edge1[:, bass.ds(g * T, T)]).then_inc(s_cp, 1)
                    pool.wait_ge(s_cp, GE + g + 1)
                    pad()
                    for k in range(T):
                        pool.indirect_dma_start(
                            out=node_table[:, :], out_offset=bass.IndirectOffsetOnAxis(ap=idx_a[h][:, k:k + 1], axis=0),
                            in_=val[h][:, k:k + 1], in_offset=None, bounds_check=N - 1, oob_is_err=False
                        ).then_inc(s_tab[h], 16)
            rounds(pool, GE, 2, write_table)
            for h in range(2):
                pool.wait_ge(s_tab[h], 16 + 16 * T * per_buffer(GE, 2, h))

            def read_table(i, us):
                def fetch(u):
                    g = i * U + u
                    pool.wait_ge(s_lc, g + 1)
                    pad()
                    pool.tensor_copy(idx_a[u][:, :], srci[:, bass.ds(g * T, T)]).then_inc(s_cp, 1)
                    pool.wait_ge(s_cp, 2 * GE + g + 1)
                    pad()
                    for k in range(T):
                        pool.indirect_dma_start(
                            out=val[u][:, k:k + 1], out_offset=None, in_=node_table[:, :],
                            in_offset=bass.IndirectOffsetOnAxis(ap=idx_a[u][:, k:k + 1], axis=0)
                        ).then_inc(s_look[u], 16)

                def keep_value(u):
                    pool.wait_ge(s_look[u], 16 * T * (i + 1))
                    pad()
                    pool.tensor_copy(rec[:, bass.ds((i * U + u) * T, T), 1], val[u][:, :]).then_inc(s_lc, 1)
                ks = [u for u, _ in us]
                for u in ks:
                    fetch(u)
                    if u:
                        keep_value(u - 1)
                keep_value(ks[-1])
            pool.sem_inc(s_lc, U)
            rounds(pool, GE, U, read_table)
            pool.wait_ge(s_lc, GE + U)

            for u in range(U):
                pool.wait_ge(S[f"stored{u}"], at(f"stored{u}", "x1s", 16 + 16 * per_buffer(GE, U, u)))

            def to_slots(i, us):
                for h, _ in us:
                    g = i * 2 + h
                    pool.wait_ge(s_ws[h], 16 + 16 * T * i)
                    pad()
                    pool.dma_start(wide[h][:, :, 0:D], edge_rows(src_x1, g).rearrange("p (t d) -> p t d", d=D)).then_inc(s_wl[h], 16)
                    pool.tensor_copy(wide[h][:, :, D:WD], rec[:, bass.ds(g * T, T), :])
                    pool.tensor_copy(idx_a[h][:, :], addr_i[:, bass.ds(g * T, T)]).then_inc(s_cp, 1)
                for h, _ in us:
                    g = i * 2 + h
                    pool.wait_ge(s_cp, 3 * GE + g + 1)
                    pool.wait_ge(s_wl[h], 16 * (i + 1))
                    pad()
                    for k in range(T):
                        pool.indirect_dma_start(
                            out=slot_rows[0][:, :], out_offset=bass.IndirectOffsetOnAxis(ap=idx_a[h][:, k:k + 1], axis=0),
                            in_=wide[h][:, k, :], in_offset=None, bounds_check=NS - 1, oob_is_err=False
                        ).then_inc(s_ws[h], 16)
            rounds(pool, GE, 2, to_slots)

            for h in range(2):
                pool.wait_ge(s_ws[h], 16 + 16 * T * per_buffer(GE, 2, h))
            pool.wait_ge(s_dve, DV["indices_ready"])
            for l in range(L):
                stage = SL[l]
                if l == 0:
                    for u in range(U):
                        pool.wait_ge(S[f"stored{u}"], at(f"stored{u}", "x1d", 16 + 16 * per_buffer(GE, U, u)))
                else:
                    for u in range(U):
                        pool.wait_ge(S[f"stored{u}"], at(f"stored{u}", f"d{l - 1}", 16 + 16 * per_buffer(GE, U, u)))
                    pool.wait_ge(S["agg_loaded"], at("agg_loaded", f"m{l - 1}", 16))

                def fetch_indices(i, h, stage=stage):
                    pool.wait_ge(S[f"fetched{h}"], at(f"fetched{h}", stage, 16 * T * i))
                    pad()
                    pool.tensor_copy(idx_a[h][:, :], lidx[:, bass.ds((i * 2 + h) * T, T)]).then_inc(S["slot_idx"], 1)

                def fetch(i, h, l=l, stage=stage):
                    pool.wait_ge(S["slot_idx"], at("slot_idx", stage, i * 2 + h + 1))
                    pool.wait_ge(S[f"slot_loaded{h}"], at(f"slot_loaded{h}", stage, 16 * (i + 1)))
                    pad()
                    for k in range(T):
                        pool.indirect_dma_start(
                            out=wide[h][:, k, 0:D], out_offset=None, in_=dst_rows[l][:, :],
                            in_offset=bass.IndirectOffsetOnAxis(ap=idx_a[h][:, k:k + 1], axis=0),
                            bounds_check=EP - 1, oob_is_err=False).then_inc(S[f"fetched{h}"], 16)

                def send_indices(i, h, stage=stage):
                    pool.wait_ge(S[f"msg_out{h}"], at(f"msg_out{h}", stage, 16 + 16 * T * i))
                    pad()
                    pool.tensor_copy(idx_b[h][:, :], qidx[:, bass.ds((i * 2 + h) * T, T)]).then_inc(S["msg_idx"], 1)

                def send(i, h, stage=stage):
                    pool.wait_ge(S["msg_idx"], at("msg_idx", stage, i * 2 + h + 1))
                    pool.wait_ge(S["msg_ready"], at("msg_ready", stage, 1 + i * 2 + h + 1))
                    pad()
                    for k in range(T):
                        pool.indirect_dma_start(
                            out=msg_rows[:, :],
                            out_offset=bass.IndirectOffsetOnAxis(ap=idx_b[h][:, k:k + 1], axis=0),
                            in_=ring_d[h][:, k * D:(k + 1) * D], in_offset=None, bounds_check=EP - 1,
                            oob_is_err=False).then_inc(S[f"msg_out{h}"], 16)

                if l:
                    for h in range(2):
                        pool.wait_ge(S[f"fetched{h}"], at(f"fetched{h}", stage, 0))
                        pool.wait_ge(S[f"msg_out{h}"], at(f"msg_out{h}", stage, 16))
                for h in range(2):
                    pool.tensor_copy(idx_a[h][:, :], lidx[:, h * T:(h + 1) * T]).then_inc(S["slot_idx"], 1)
                send_indices(0, 0)
                fetch(0, 0)
                fetch(0, 1)

                def half(i, h):
                    fetch_indices(i + 1, h)
                    send(i, h)
                    send_indices(after_half(i, h)[0], 1 - h)
                    fetch(i + 1, h)
                with pool.Fori(0, GM - 1) as i:
                    half(i, 0)
                    half(i, 1)
                half(GM - 1, 0)
                send(GM - 1, 1)
                send_indices(GM, 0)
                send(GM, 0)

            for u in range(U):
                pool.wait_ge(S[f"stored{u}"], at(f"stored{u}", "dense", 16 + 16 * uses("dense", u)))
            for u in range(2):
                pool.wait_ge(S[f"out_stored{u}"], at(f"out_stored{u}", "mix2", 16 + 16 * GM))
            for h in range(2):
                pool.wait_ge(S[f"msg_out{h}"], at(f"msg_out{h}", SL[-1], 16 + 16 * T * per_buffer(GS, 2, h)))

            def write_out(i, us):
                for u, _ in us:
                    g = i * U + u
                    pool.wait_ge(S[f"scattered{u}"], at(f"scattered{u}", "d2", 16 + 16 * T * i))
                    pad()
                    pool.tensor_copy(idx_a[u][:, :], last_i[:, bass.ds(g * T, T)]).then_inc(s_cp, 1)
                    pool.wait_ge(s_cp, 4 * GE + g + 1)
                    pool.wait_ge(S["x1_ready"], at("x1_ready", "d2", g + 1))
                    pad()
                    for k in range(T):
                        pool.indirect_dma_start(
                            out=out[:, :], out_offset=bass.IndirectOffsetOnAxis(ap=idx_a[u][:, k:k + 1], axis=0),
                            in_=vr[u][:, k * D:(k + 1) * D], in_offset=None, bounds_check=N - 1,
                            oob_is_err=False).then_inc(S[f"scattered{u}"], 16)
            rounds(pool, GE, U, write_out)
            for u in range(U):
                pool.wait_ge(S[f"scattered{u}"], at(f"scattered{u}", "d2", 16 + 16 * T * per_buffer(GE, U, u)))

        @block.scalar
        def _(act):
            for u in range(U):
                act.dma_start(primer[:, 16 + u:17 + u], eps.rearrange("(p o) -> p o", p=1)).then_inc(S[f"stored{u}"], 16)
            for h in range(2):
                act.dma_start(primer[:, 28 + h:29 + h], eps.rearrange("(p o) -> p o", p=1)).then_inc(S[f"slot_stored{h}"], 16)
            act.sem_inc(S["base_relu"], 1)
            act.wait_ge(s_wts, WTS)
            act.wait_ge(s_dve, DV["eps"])

            def relu_hidden(stage, i, us, scale):
                for u, p in us:
                    act.wait_ge(S["hid_ready"], nth("hid_ready", stage, i, u))
                    act.activation(aT[u][:, 0:4 * p], bank[2 * u + 1][:, 0:4 * p], ACT.Relu, bias=b1c[:, 0:1],
                                   scale=scale).then_inc(S["hid_relu"], 1)

            def root_std(stage, var, std, i, us, k):
                act.wait_ge(S[var], at(var, stage, norm_round(stage, i, us) + 1))
                q = norm_cols(us)
                small = lns2 if var == "var2_ready" else lns
                act.activation(small[:, 4, q], small[:, 3, q], ACT.Sqrt, bias=const[:, k:k + 1],
                               scale=1.0 / D).then_inc(S[std], 1)

            def copy_x(stage, i, us):
                for u, p in us:
                    act.wait_ge(S["x_turned"], nth_after_free("x_turned", stage, i, u))
                    act.activation(xT[u][:, 0:4 * p], bank[2 * u][:, 0:4 * p], ACT.Copy).then_inc(S["x_copied"], 1)

            rounds(act, GD, U, lambda i, us: relu_hidden("stats", i, us, eps1[:, 0:1]), last=REST)

            def edge_change(i, us):
                for b, _ in us:
                    act.wait_ge(s_e["turned"], i * 2 + b + 3)
                    act.activation(xT[2 * b][:, :], bank[4 * b][:, :], ACT.Copy).then_inc(s_e["base_copied"], 1)
                for b, _ in us:
                    act.wait_ge(s_e["hid"], i * 2 + b + 1)
                    act.activation(aT[2 * b][:, :], bank[4 * b + 1][:, :], ACT.Relu, bias=b1c[:, 0:1], scale=eps1[:, 0:1])
                    act.activation(aT[2 * b + 1][:, :], bank[4 * b + 3][:, :], ACT.Relu, bias=b1c[:, 0:1]).then_inc(s_e["relu"], 1)
                for b, _ in us:
                    g = i * 2 + b
                    act.wait_ge(s_e["y"], g + 1)
                    act.wait_ge(s_e["acc"], 2 * g + 1)
                    act.activation(orow[3 * b][:, :], bank[4 * b][:, :], ACT.Copy).then_inc(s_e["base"], 1)
            rounds(act, GE, 2, edge_change)

            act.wait_ge(s_dve, DV["y_var"])
            act.activation(mom[:, 1, :], mom[:, 1, :], ACT.Sqrt, bias=const[:, 1:2]).then_inc(s_std, 1)

            def x1_stage(stage, scale):
                def body(i, us):
                    copy_x(stage, i, us)
                    relu_hidden(stage, i, us, scale)
                    root_std(stage, "var_ready", "std_ready", i, us, 0)
                rounds(act, GE, U, body)
            x1_stage("x1s", eps1[:, 0:1])
            x1_stage("x1d", 1.0)

            def copy_x1(stage, i, us):
                for u, p in us:
                    act.wait_ge(S["x1_turned"], nth("x1_turned", stage, i, u))
                    act.activation(xT[u][:, 0:4 * p], bank[2 * u + 1][:, 0:4 * p], ACT.Copy).then_inc(S["x1_copied"], 1)

            def root_relus(stage, i, us):
                for u, p in us:
                    act.wait_ge(S["r0_ready"], nth("r0_ready", stage, i, u))
                    act.activation(aT[u][:, 0:4 * p], bank[2 * u][:, 0:4 * p], ACT.Relu, bias=rootb[0][:, 0:1]).then_inc(S["r0_relu"], 1)
                for u, p in us:
                    act.wait_ge(S["r1_ready"], nth("r1_ready", stage, i, u))
                    act.activation(xT[u][:, 0:4 * p], bank[2 * u + 1][:, 0:4 * p], ACT.Relu, bias=rootb[1][:, 0:1]).then_inc(S["r1_relu"], 1)

            def dense(i, us):
                copy_x("dense", i, us)
                relu_hidden("dense", i, us, eps1[:, 0:1])
                root_std("dense", "var_ready", "std_ready", i, us, 0)
                copy_x1("dense", i, us)
                root_relus("dense", i, us)
                root_std("dense", "var2_ready", "std2_ready", i, us, 1)
                for u, p in us:
                    act.wait_ge(S["out_ready"], nth("out_ready", "dense", i, u))
                    act.dma_start(node_rows(out, FIRST["dense"] + i * U + u, p), orow[u][0:p, :]).then_inc(S[f"stored{u}"], 16)
            rounds(act, DENSE_ONLY, U, dense, last=REST)

            for l in range(L):
                stage = SL[l]

                def copy_slots(i, h, stage=stage):
                    act.wait_ge(S["s_turned"], at("s_turned", stage, 2 + i * 2 + h + 1))
                    act.activation(sT[h][0][0:D, :], bank[4][0:D, :], ACT.Copy)
                    act.activation(sT[h][1][0:D, :], bank[5][0:D, :], ACT.Copy).then_inc(S["s_copied"], 1)

                def next_rows(i, h, l=l, stage=stage):
                    if l == L - 1:
                        return
                    act.wait_ge(S["base_ready"], at("base_ready", stage, i * 2 + h + 1))
                    act.wait_ge(S[f"slot_stored{h}"], at(f"slot_stored{h}", stage, 16 * (i + 1)))
                    act.activation(ring_s[h][:, :], bank[7][:, :], ACT.Relu).then_inc(S["base_relu"], 1)
                    act.wait_ge(S["base_relu"], at("base_relu", stage, 1 + i * 2 + h + 1))
                    act.dma_start(slot_view(l + 1, i * 2 + h),
                                  ring_s[h][:, :].rearrange("p (t d) -> p t d", d=D)).then_inc(S[f"slot_stored{h}"], 16)

                def half(i, h, dense, earlier, more=True, mix=f"mix{l}"):
                    now, then = [(h, P)], [(1 - h, P)]
                    j, k = before_half(i, h)[0], after_half(i, h)[0]
                    if dense:
                        relu_hidden(mix, i, now, eps1[:, 0:1])
                    if earlier:
                        root_relus(mix, j, then)
                    if dense:
                        root_std(mix, "var_ready", "std_ready", i, now, 0)
                    next_rows(i, h)
                    if dense and more:
                        copy_x(mix, k, then)
                    if dense:
                        copy_x1(mix, i, now)
                    if earlier:
                        root_std(mix, "var2_ready", "std2_ready", j, then, 1)
                    if dense:
                        copy_slots(k, 1 - h)
                copy_x(f"mix{l}", 0, [(0, P)])
                copy_slots(0, 0)
                half(0, 0, True, False)
                with act.Fori(0, GM - 1) as i:
                    half(i, 1, True, True)
                    half(i + 1, 0, True, True)
                half(GM - 1, 1, True, True, more=False)
                half(GM, 0, False, True)
                stage = f"d{l}"

                def dst_stage(i, us, l=l, stage=stage):
                    copy_x(stage, i, us)
                    if l == L - 1:
                        root_std(stage, "var_ready", "std_ready", i, us, 1)
                        return
                    for u, _ in us:
                        act.wait_ge(S["v_ready"], at("v_ready", stage, U + i * U + u + 1))
                        act.activation(vr[u][:, :], vr[u][:, :], ACT.Relu).then_inc(S["x1_ready"], 1)
                rounds(act, GE, U, dst_stage)

        @block.tensor
        def _(pe):
            mm = pe.matmul
            pe.sem_inc(S["x_turned"], U)
            pe.sem_inc(S["s_turned"], 2)
            step = [0]

            def done(ins):
                step[0] += 1
                ins.then_inc(s_pe, 1)

            pe.wait_ge(s_fill, 5)
            pe.wait_ge(s_dve, DV["order_seen"])
            done(mm(bank[0][:, 0:1], ones[:, :], out_of_order[:, :], start=True, stop=True))
            pe.wait_ge(s_dve, DV["order_known"])
            flag = pe.value_load(unsorted[0:1, 0:1], min_val=0, max_val=1)
            with pe.If(flag > 0):
                n = PE_FULL
                with pe.Fori(0, PASSES) as k:
                    pe.wait_ge(s_q["counted"], k + 1)
                    pe.sem_inc(s_pad_pe, 1)
                    mm(bank[0][0:n, 0:RADIX], before[0:n, 0:n], tot[0:n, 0:RADIX], start=True, stop=True)
                    mm(bank[0][0:n, RADIX:2 * RADIX], ones[0:n, 0:n], tot[0:n, 0:RADIX], start=True, stop=True).then_inc(s_q["summed"], 1)
            pe.wait_ge(s_dve, DV["counted"])
            mm(bank[0][:, 0:R], before[:, :], tot[:, :], start=True, stop=True)
            done(mm(bank[0][:, R:2 * R], ones[:, :], tot[:, :], start=True, stop=True))
            pe.wait_ge(s_dve, DV["tile_rel"])
            mm(bank[1][0:1, 0:HALF], relt[:, 0:1], ident[0:HALF, 0:HALF], start=True, stop=True)
            done(mm(bank[1][0:1, HALF:TS], relt[:, 1:2], ident[0:HALF, 0:HALF], start=True, stop=True))
            mm(bank[2][0:1, P:P + 1], ones[:, 0:1], openk[:, SHORT:SHORT + 1], start=True, stop=True)
            done(mm(bank[2][0:D, 0:P], ak[:, :], ident[:, :], start=True, stop=True))
            pe.wait_ge(s_dve, DV["sorted"])
            pe.wait_ge(s_wts, WTS)

            def turn(dest, rows, p):
                for j in range(4):
                    ins = pe.transpose(dest[:, j * p:(j + 1) * p], rows[0:p, j * P:(j + 1) * P], ident[0:p, 0:p])
                return ins

            def turn_x(stage, i, us, rows=None):
                for u, p in us:
                    if rows is None:
                        pe.wait_ge(S[f"loaded{u}"], at(f"loaded{u}", stage, 16 * (i + 1)))
                        if stage == "stats":
                            pe.wait_ge(S["y_counted"], at("y_counted", stage, i * U + u + 1))
                        elif stage in FIRST:
                            pe.wait_ge(S["v2_ready"], free("v2_ready", stage, i, u))
                        elif stage == "x1s":
                            pe.wait_ge(S["v_ready"], at("v_ready", stage, i * U + u + 1))
                        turn(bank[2 * u], xr[u], p).then_inc(S["x_turned"], 1)
                    else:
                        pe.wait_ge(S["x0_ready"], at("x0_ready", stage, i * U + u + 1))
                        turn(bank[2 * u], rows[u], p).then_inc(S["x_turned"], 1)

            def hidden(stage, i, us):
                for u, p in us:
                    pe.wait_ge(S["x_copied"], nth("x_copied", stage, i, u))
                    mm(bank[2 * u + 1][:, 0:4 * p], w1[:, :], xT[u][:, 0:4 * p], start=True, stop=True).then_inc(S["hid_ready"], 1)

            def rows_out(dest, lhs, w, bias, p):
                if bias is not None:
                    mm(dest[0:p, :], pick3[:, 0:p], bias[:, :], start=True, stop=False, skip_group_check=True)
                for j in range(4):
                    ins = mm(dest[0:p, j * P:(j + 1) * P], lhs[:, j * p:(j + 1) * p], w[:, :], start=bias is None,
                             stop=True, skip_group_check=True)
                return ins

            def stats(i, us):
                turn_x("stats", i, us)
                hidden("stats", i, us)
                for u, p in us:
                    pe.wait_ge(S["hid_relu"], at("hid_relu", "stats", i * U + u + 1))
                    mm(bank[2 * u][:, 0:4 * p], w2[:, :], aT[u][:, 0:4 * p], start=True, stop=True).then_inc(S["y_ready"], 1)
            rounds(pe, GD, U, stats, last=REST)
            pe.wait_ge(S["y_counted"], at("y_counted", "stats", GD + U))

            def carry_turns(use):
                pe.wait_ge(S["scanned"], at("scanned", use, D))
                pe.transpose(bank[4][0:D, 0:P], agg[:, (TE - 1) * D:TE * D], ident[:, :]).then_inc(S["end_turned"], 1)
                pe.wait_ge(S["carry_step"], at("carry_step", use, 2))
                pe.transpose(bank[5][:, 0:D], carT[:, 0:P], ident[0:D, 0:D]).then_inc(S["carry_turned"], 1)
                pe.wait_ge(S["carry_step"], at("carry_step", use, 3))
            carry_turns("neigh")

            pe.sem_inc(s_e["turned"], 2)

            def edge_change(i, us):
                for b, _ in us:
                    g = i * 2 + b
                    pe.wait_ge(s_e["x0"], g + 1)
                    pe.wait_ge(s_e["acc"], 2 * g + 1)
                    turn(bank[4 * b], xr[2 * b], P)
                    turn(bank[4 * b + 2], xr[2 * b + 1], P).then_inc(s_e["turned"], 1)
                for b, _ in us:
                    g = i * 2 + b
                    pe.wait_ge(s_e["base_copied"], g + 1)
                    mm(bank[4 * b + 1][:, :], w1[:, :], xT[2 * b][:, :], start=True, stop=True)
                    pe.wait_ge(s_e["copied"], g + 1)
                    mm(bank[4 * b + 3][:, :], w1[:, :], xT[2 * b + 1][:, :], start=True, stop=True).then_inc(s_e["hid"], 1)
                for b, _ in us:
                    pe.wait_ge(s_e["relu"], i * 2 + b + 1)
                    rows_out(bank[4 * b], aT[2 * b], w2, None, P)
                    rows_out(bank[4 * b + 2], aT[2 * b + 1], w2, None, P).then_inc(s_e["y"], 1)
            rounds(pe, GE, 2, edge_change)

            pe.wait_ge(s_dve, DV["moments"])
            for k in range(2):
                mm(bank[4][:, k * D:(k + 1) * D], ones[:, :], st_rhs[k], start=True, stop=False, skip_group_check=True)
                ins = mm(bank[4][:, k * D:(k + 1) * D], ones[:, :], corr_rhs[k], start=False, stop=True, skip_group_check=True)
            done(ins)
            pe.wait_ge(s_dve, DV["w2n"])

            def x1_stage(stage, rows):
                def body(i, us):
                    turn_x(stage, i, us, rows)
                    hidden(stage, i, us)
                    for u, p in us:
                        pe.wait_ge(S["hid_relu"], at("hid_relu", stage, i * U + u + 1))
                        rows_out(bank[2 * u], aT[u], w2n, bias3[0], p).then_inc(S["y_ready"], 1)
                rounds(pe, GE, U, body)
            x1_stage("x1s", None)
            x1_stage("x1d", orow)

            def dense_y(stage, i, us):
                for u, p in us:
                    pe.wait_ge(S["hid_relu"], nth("hid_relu", stage, i, u))
                    rows_out(bank[2 * u], aT[u], w2n, bias3[0], p).then_inc(S["y_ready"], 1)

            def turn_x1(stage, i, us):
                for u, p in us:
                    pe.wait_ge(S["x1_ready"], nth("x1_ready", stage, i, u))
                    turn(bank[2 * u + 1], vr[u], p).then_inc(S["x1_turned"], 1)

            def root_0(stage, i, us):
                for u, p in us:
                    pe.wait_ge(S["x1_copied"], nth("x1_copied", stage, i, u))
                    mm(bank[2 * u][:, 0:4 * p], root[0][:, :], xT[u][:, 0:4 * p], start=True, stop=True).then_inc(S["r0_ready"], 1)

            def root_1(stage, i, us):
                for u, p in us:
                    pe.wait_ge(S["r0_relu"], nth("r0_relu", stage, i, u))
                    mm(bank[2 * u + 1][:, 0:4 * p], root[1][:, :], aT[u][:, 0:4 * p], start=True, stop=True).then_inc(S["r1_ready"], 1)

            def root_2(stage, i, us):
                for u, p in us:
                    pe.wait_ge(S["r1_relu"], nth("r1_relu", stage, i, u))
                    rows_out(bank[2 * u], xT[u], root[2], bias3[3], p).then_inc(S["r2_ready"], 1)

            def dense(i, us):
                turn_x("dense", i, us)
                hidden("dense", i, us)
                dense_y("dense", i, us)
                turn_x1("dense", i, us)
                root_0("dense", i, us)
                root_1("dense", i, us)
                root_2("dense", i, us)
            rounds(pe, DENSE_ONLY, U, dense, last=REST)

            pe.wait_ge(s_dve, DV["rec_ready"])
            for h in range(2):
                ins = pe.transpose(bank[0][0:HALF, h * P:(h + 1) * P],
                                   slot_rec[:, h * HALF:(h + 1) * HALF, 2], ident[:, :])
            done(ins)
            pe.wait_ge(s_dve, DV["run_ends"])
            for h in range(2):
                mm(bank[1][0:1, h * HALF:(h + 1) * HALF], runS[:, (h + 1) * P - 1:(h + 1) * P], ident[0:HALF, 0:HALF],
                   start=True, stop=True)
                ins = mm(bank[2][0:1, h * HALF:(h + 1) * HALF], runE[:, h * P:h * P + 1], ident[0:HALF, 0:HALF],
                         start=True, stop=True)
            done(ins)
            pe.wait_ge(s_dve, DV["run_carry"])
            for h in range(2):
                mm(bank[3][0:HALF, h:h + 1], line[0:1, 2, h * HALF:(h + 1) * HALF], ones[0:1, 0:1], start=True, stop=True)
                ins = mm(bank[3][0:HALF, 2 + h:3 + h], line[0:1, 3, 1 + h * HALF:1 + (h + 1) * HALF], ones[0:1, 0:1],
                         start=True, stop=True)
            done(ins)
            pe.wait_ge(s_dve, DV["run_inv"])
            for h in range(2):
                ins = pe.transpose(bank[4][:, h * HALF:(h + 1) * HALF], runX[:, h * P:(h + 1) * P], ident[0:HALF, 0:HALF])
            done(ins)
            pe.wait_ge(s_dve, DV["slots_ready"])

            for l in range(L):
                stage = SL[l]

                def turn_slots(i, h, stage=stage):
                    pe.wait_ge(S[f"fetched{h}"], at(f"fetched{h}", stage, 16 * T * (i + 1)))
                    pe.sem_inc(s_pad_pe, 1)
                    for k in range(T):
                        ins = pe.transpose(bank[4 + k // 4][0:D, (k % 4) * P:(k % 4 + 1) * P], wide[h][:, k, 0:D], ident[:, :])
                    ins.then_inc(S["s_turned"], 1)

                def weight_columns(i, h):
                    return [pe.value_load(rel_tab[0:1, bass.ds((i * 2 + h) * T + k, 1)])
                            for k in range(T)]

                def messages(i, h, w_at, l=l, stage=stage):
                    g = i * 2 + h
                    pe.wait_ge(S["s_copied"], at("s_copied", stage, g + 1))
                    pe.wait_ge(S["msg_ready"], at("msg_ready", stage, g + 1))
                    for k in range(T):
                        lhs = sT[h][k // 4][0:D, (k % 4) * P:(k % 4 + 1) * P]
                        ins = mm(bank[6][:, k * D:(k + 1) * D], lhs,
                                 rel_w[:, bass.ds(w_at[k] + l * R * D, D)], start=True, stop=True)
                    ins.then_inc(S["msg_sums"], 1)

                def next_rows(i, h, l=l, stage=stage):
                    if l == L - 1:
                        return
                    pe.wait_ge(S["base_relu"], at("base_relu", stage, i * 2 + h + 1))
                    mm(bank[7][:, :], pick3[:, :], bias3[1 + l][:, :], start=True, stop=False, skip_group_check=True)
                    for k in range(T):
                        lhs = sT[h][k // 4][0:D, (k % 4) * P:(k % 4 + 1) * P]
                        ins = mm(bank[7][:, k * D:(k + 1) * D], lhs, root[l][0:D, 0:D], start=False, stop=True,
                                 skip_group_check=True)
                    ins.then_inc(S["base_ready"], 1)

                def half(i, h, dense, earlier, mix=f"mix{l}"):
                    now, then = [(h, P)], [(1 - h, P)]
                    j = before_half(i, h)[0]
                    w_at = weight_columns(i, h)
                    if dense:
                        turn_x(mix, i, now)
                    if earlier:
                        turn_x1(mix, j, then)
                    turn_slots(i, h)
                    if dense:
                        hidden(mix, i, now)
                    if earlier:
                        root_0(mix, j, then)
                    messages(i, h, w_at)
                    if dense:
                        dense_y(mix, i, now)
                    if earlier:
                        root_1(mix, j, then)
                    next_rows(i, h)
                    if earlier:
                        root_2(mix, j, then)
                halves(pe, half)
                carry_turns(f"m{l}")
                stage = f"d{l}"

                def dst_stage(i, us, l=l, stage=stage):
                    turn_x(stage, i, us)
                    for u, p in us:
                        pe.wait_ge(S["x_copied"], at("x_copied", stage, i * U + u + 1))
                        pe.wait_ge(S["v_ready"], at("v_ready", stage, i * U + u + 1))
                        rows_out(bank[2 * u + 1], xT[u], root[l], bias3[1 + l], p).then_inc(S["y_ready"], 1)
                rounds(pe, GE, U, dst_stage)



_INS = ['x', 'src', 'dst', 'edge_type_50', 'L0_gnn_W1', 'L0_gnn_b1', 'L0_gnn_W2', 'L0_gnn_b2', 'L0_gnn_gamma',
        'L0_gnn_beta', 'L0_gnn_eps', 'L1_gnn_w0_rel', 'L1_gnn_w0_root', 'L1_gnn_b0', 'L1_gnn_w1_rel',
        'L1_gnn_w1_root', 'L1_gnn_b1', 'L1_gnn_w2_rel', 'L1_gnn_w2_root', 'L1_gnn_b2']


def kernel(**inputs):
    import concourse.bacc as _bacc
    from concourse.bass_utils import run_bass_kernel_spmd as _run

    nc = _bacc.Bacc("TRN2", target_bir_lowering=False, num_devices=1)
    arrays, args = {}, []
    for name in _INS:
        a = np.ascontiguousarray(inputs[name])
        arrays[f"in_{name}_dram"] = a
        args.append(nc.dram_tensor(f"in_{name}_dram", a.shape, mybir.dt.from_np(a.dtype), kind="ExternalInput").ap())
    out = nc.dram_tensor("out_0_dram", (N, D), F32, kind="ExternalOutput").ap()
    build(nc, *args, out)
    r = _run(nc, [arrays], core_ids=[0])
    return r.results[0]["out_0_dram"]
```
